# Optimizing a Trainium2 kernel written in Bass

```python
import numpy as np
import jax
import jax.numpy as jnp

def _softmax(x, axis=-1):
    return jax.nn.softmax(x, axis=axis)

def _gelu(x):
    return jax.nn.gelu(x, approximate=True)

def _silu(x):
    return jax.nn.silu(x)

def _sigmoid(x):
    return jax.nn.sigmoid(x)

def _layernorm(x, axis=-1, eps=1e-05):
    m = jnp.mean(x, axis=axis, keepdims=True)
    v = jnp.var(x, axis=axis, keepdims=True)
    return (x - m) / jnp.sqrt(v + eps)

def _scatter_add(tgt, idx, src, axis=0):
    return tgt.at[idx].add(src)

def _segment_sum(src, seg, n):
    return jax.ops.segment_sum(src, seg, n)
kernel_name = 'mk_recurrent_d2_jaxref_r8_a46f0c'

def setup_inputs(seed: int=0):
    np.random.seed(seed)
    _w = jnp.asarray

    def _L0_attn_setup():
        import jax, jax.numpy as jnp
        import numpy as np
        H = 8
        R = 2
        D = 128
        DEG = 2
        GATE_OFFSET = 6.906768

        def _power_attention(q, k, v, log_g):
            B, T, hq, d = q.shape
            scale = 1.0 / d ** 0.5
            k = jnp.repeat(k, R, axis=2)
            v = jnp.repeat(v, R, axis=2)
            logG = jnp.cumsum(log_g, axis=1)
            logG = jnp.repeat(logG, R, axis=2)
            logG = jnp.transpose(logG, (0, 2, 1))
            qk = jnp.einsum('bthd,bshd->bhts', q, k) * scale
            a = qk ** DEG
            gate = logG[:, :, :, None] - logG[:, :, None, :]
            causal = jnp.tril(jnp.ones((T, T), dtype=bool))
            a = jnp.where(causal, a * jnp.exp(gate), 0.0)
            norm = jnp.sum(a, axis=-1) + 1e-06
            y = jnp.einsum('bhts,bshd->bthd', a, v)
            y = y / jnp.transpose(norm, (0, 2, 1))[..., None]
            return y
        key = jax.random.key(seed)
        ks = jax.random.split(key, 7)
        B, T, C = (1, 256, 256)
        q_dim = H * R * D
        kv_dim = H * D
        s = 0.02
        return {'hidden_states': jax.random.normal(ks[0], (B, T, C), dtype=jnp.float32), 'Wq': jax.random.normal(ks[1], (C, q_dim), dtype=jnp.float32) * s, 'Wk': jax.random.normal(ks[2], (C, kv_dim), dtype=jnp.float32) * s, 'Wv': jax.random.normal(ks[3], (C, kv_dim), dtype=jnp.float32) * s, 'Wg': jax.random.normal(ks[4], (C, H), dtype=jnp.float32) * s, 'Wc': jax.random.normal(ks[5], (q_dim, C), dtype=jnp.float32) * s, 'bc': jnp.zeros((C,), dtype=jnp.float32)}
    _L0_attn_in = _L0_attn_setup()

    def _L0_ffn_setup():
        import jax, jax.numpy as jnp
        import numpy as np
        D = 256
        M = 128
        E = 32
        K = 6
        G = 8
        KG = 4
        SH = 256
        SCALE = 2.5

        def _route(xf, Wr, br):
            T = xf.shape[0]
            s = jax.nn.sigmoid(xf @ Wr.T + br)
            sg = s.reshape(T, G, E // G)
            group_w = jax.lax.top_k(sg, 2)[0].sum(-1)
            top_g = jax.lax.top_k(group_w, KG)[1]
            gmask = jnp.zeros((T, G), bool).at[jnp.arange(T)[:, None], top_g].set(True)
            masked = jnp.where(gmask[:, :, None], sg, 0.0).reshape(T, E)
            idx = jax.lax.top_k(masked, K)[1]
            w = jnp.take_along_axis(s, idx, axis=1)
            w = w / (w.sum(-1, keepdims=True) + 1e-20)
            return (idx, w * SCALE)
        key = jax.random.key(seed)
        ks = jax.random.split(key, 7)
        w = 0.02
        return {'hidden_tensor': jax.random.normal(ks[0], (2, 256, D), dtype=jnp.float32), 'Wr': jax.random.normal(ks[1], (E, D), dtype=jnp.float32) * w, 'br': jax.random.normal(ks[2], (E,), dtype=jnp.float32) * w, 'W1': jax.random.normal(ks[3], (E, M, D), dtype=jnp.float32) * w, 'W2': jax.random.normal(ks[4], (E, D, M), dtype=jnp.float32) * w, 'Ws1': jax.random.normal(ks[5], (SH, D), dtype=jnp.float32) * w, 'Ws2': jax.random.normal(ks[6], (D, SH), dtype=jnp.float32) * w}
    _L0_ffn_in = _L0_ffn_setup()

    def _L1_attn_setup():
        import jax, jax.numpy as jnp
        import numpy as np
        from jax import lax
        B, L, D = (4, 256, 256)
        R = 256
        DH = D // 4
        key = jax.random.key(seed)
        ks = jax.random.split(key, 12)
        s = 0.02
        x = jax.random.normal(ks[0], (B, L, D), dtype=jnp.float32)
        Wu = jax.random.normal(ks[1], (R, D), dtype=jnp.float32) * s
        bu = jnp.zeros((R,), dtype=jnp.float32)
        Wv = jax.random.normal(ks[2], (R, D), dtype=jnp.float32) * s
        bv = jnp.zeros((R,), dtype=jnp.float32)
        Wg1 = jax.random.normal(ks[3], (DH, D), dtype=jnp.float32) * s
        bg1 = jnp.zeros((DH,), dtype=jnp.float32)
        Wg2 = jax.random.normal(ks[4], (R, DH), dtype=jnp.float32) * s
        bg2 = jnp.zeros((R,), dtype=jnp.float32)
        conv_w = jax.random.normal(ks[5], (D, 1, 3), dtype=jnp.float32) * s
        conv_b = jnp.zeros((D,), dtype=jnp.float32)
        return {'x': x, 'Wu': Wu, 'bu': bu, 'Wv': Wv, 'bv': bv, 'Wg1': Wg1, 'bg1': bg1, 'Wg2': Wg2, 'bg2': bg2, 'conv_w': conv_w, 'conv_b': conv_b}
    _L1_attn_in = _L1_attn_setup()

    def _L1_ffn_setup():
        import jax, jax.numpy as jnp
        import numpy as np
        TOP_K = 4
        key = jax.random.key(seed)
        ks = jax.random.split(key, 8)
        B, S, D, E, H, HS = (2, 256, 256, 16, 128, 512)
        scaled = lambda k, shape, fan: jax.random.normal(k, shape, jnp.float32) * fan ** (-0.5)
        return {'x': jax.random.normal(ks[0], (B, S, D), jnp.float32), 'w_router': scaled(ks[1], (D, E), D), 'we1': scaled(ks[2], (E, D, H), D), 'we3': scaled(ks[3], (E, D, H), D), 'we2': scaled(ks[4], (E, H, D), H), 'ws1': scaled(ks[5], (D, HS), D), 'ws3': scaled(ks[6], (D, HS), D), 'ws2': scaled(ks[7], (HS, D), HS)}
    _L1_ffn_in = _L1_ffn_setup()
    _d = {'L0_attn_hidden_states': _L0_attn_in['hidden_states'], 'L0_attn_Wq': _L0_attn_in['Wq'], 'L0_attn_Wk': _L0_attn_in['Wk'], 'L0_attn_Wv': _L0_attn_in['Wv'], 'L0_attn_Wg': _L0_attn_in['Wg'], 'L0_attn_Wc': _L0_attn_in['Wc'], 'L0_attn_bc': _L0_attn_in['bc'], 'L0_ffn_Wr': _L0_ffn_in['Wr'], 'L0_ffn_br': _L0_ffn_in['br'], 'L0_ffn_W1': _L0_ffn_in['W1'], 'L0_ffn_W2': _L0_ffn_in['W2'], 'L0_ffn_Ws1': _L0_ffn_in['Ws1'], 'L0_ffn_Ws2': _L0_ffn_in['Ws2'], 'L1_attn_Wu': _L1_attn_in['Wu'], 'L1_attn_bu': _L1_attn_in['bu'], 'L1_attn_Wv': _L1_attn_in['Wv'], 'L1_attn_bv': _L1_attn_in['bv'], 'L1_attn_Wg1': _L1_attn_in['Wg1'], 'L1_attn_bg1': _L1_attn_in['bg1'], 'L1_attn_Wg2': _L1_attn_in['Wg2'], 'L1_attn_bg2': _L1_attn_in['bg2'], 'L1_attn_conv_w': _L1_attn_in['conv_w'], 'L1_attn_conv_b': _L1_attn_in['conv_b'], 'L1_ffn_w_router': _L1_ffn_in['w_router'], 'L1_ffn_we1': _L1_ffn_in['we1'], 'L1_ffn_we3': _L1_ffn_in['we3'], 'L1_ffn_we2': _L1_ffn_in['we2'], 'L1_ffn_ws1': _L1_ffn_in['ws1'], 'L1_ffn_ws3': _L1_ffn_in['ws3'], 'L1_ffn_ws2': _L1_ffn_in['ws2']}
    _x0 = _d['L0_attn_hidden_states']
    _d['L0_attn_hidden_states'] = jax.random.normal(jax.random.fold_in(jax.random.key(seed), 1), (8, 512, 256), dtype=_x0.dtype)
    del _x0
    return _d

def reference(L0_attn_hidden_states, L0_attn_Wq, L0_attn_Wk, L0_attn_Wv, L0_attn_Wg, L0_attn_Wc, L0_attn_bc, L0_ffn_Wr, L0_ffn_br, L0_ffn_W1, L0_ffn_W2, L0_ffn_Ws1, L0_ffn_Ws2, L1_attn_Wu, L1_attn_bu, L1_attn_Wv, L1_attn_bv, L1_attn_Wg1, L1_attn_bg1, L1_attn_Wg2, L1_attn_bg2, L1_attn_conv_w, L1_attn_conv_b, L1_ffn_w_router, L1_ffn_we1, L1_ffn_we3, L1_ffn_we2, L1_ffn_ws1, L1_ffn_ws3, L1_ffn_ws2):

    def _L0_attn_ref(hidden_states, Wq, Wk, Wv, Wg, Wc, bc):
        import jax, jax.numpy as jnp
        import numpy as np
        H = 8
        R = 2
        D = 128
        DEG = 2
        GATE_OFFSET = 6.906768

        def _power_attention(q, k, v, log_g):
            B, T, hq, d = q.shape
            scale = 1.0 / d ** 0.5
            k = jnp.repeat(k, R, axis=2)
            v = jnp.repeat(v, R, axis=2)
            logG = jnp.cumsum(log_g, axis=1)
            logG = jnp.repeat(logG, R, axis=2)
            logG = jnp.transpose(logG, (0, 2, 1))
            qk = jnp.einsum('bthd,bshd->bhts', q, k) * scale
            a = qk ** DEG
            gate = logG[:, :, :, None] - logG[:, :, None, :]
            causal = jnp.tril(jnp.ones((T, T), dtype=bool))
            a = jnp.where(causal, a * jnp.exp(gate), 0.0)
            norm = jnp.sum(a, axis=-1) + 1e-06
            y = jnp.einsum('bhts,bshd->bthd', a, v)
            y = y / jnp.transpose(norm, (0, 2, 1))[..., None]
            return y
        B, T, C = hidden_states.shape
        q = (hidden_states @ Wq).reshape(B, T, H * R, D)
        k = (hidden_states @ Wk).reshape(B, T, H, D)
        v = (hidden_states @ Wv).reshape(B, T, H, D)
        g = hidden_states @ Wg
        log_g = jax.nn.log_sigmoid(GATE_OFFSET + g.astype(jnp.float32))
        y = _power_attention(q, k, v, log_g)
        y = y.reshape(B, T, H * R * D)
        return y @ Wc + bc

    def _L0_ffn_ref(hidden_tensor, Wr, br, W1, W2, Ws1, Ws2):
        import jax, jax.numpy as jnp
        import numpy as np
        D = 256
        M = 128
        E = 32
        K = 6
        G = 8
        KG = 4
        SH = 256
        SCALE = 2.5

        def _route(xf, Wr, br):
            T = xf.shape[0]
            s = jax.nn.sigmoid(xf @ Wr.T + br)
            sg = s.reshape(T, G, E // G)
            group_w = jax.lax.top_k(sg, 2)[0].sum(-1)
            top_g = jax.lax.top_k(group_w, KG)[1]
            gmask = jnp.zeros((T, G), bool).at[jnp.arange(T)[:, None], top_g].set(True)
            masked = jnp.where(gmask[:, :, None], sg, 0.0).reshape(T, E)
            idx = jax.lax.top_k(masked, K)[1]
            w = jnp.take_along_axis(s, idx, axis=1)
            w = w / (w.sum(-1, keepdims=True) + 1e-20)
            return (idx, w * SCALE)
        B, Tlen, C = hidden_tensor.shape
        xf = hidden_tensor.reshape(-1, C).astype(jnp.float32)
        T = xf.shape[0]
        idx, w = _route(xf, Wr, br)
        gate = jnp.zeros((T, E), w.dtype).at[jnp.arange(T)[:, None], idx].add(w)

        def step(acc, ew):
            w1, w2, g = ew
            h = jnp.square(jax.nn.relu(xf @ w1.T)) @ w2.T
            return (acc + g[:, None] * h, None)
        acc, _ = jax.lax.scan(step, jnp.zeros_like(xf), (W1, W2, gate.T))
        moe_out = acc.reshape(B, Tlen, C).astype(hidden_tensor.dtype)
        shared = jnp.square(jax.nn.relu(hidden_tensor @ Ws1.T)) @ Ws2.T
        return shared + moe_out

    def _L1_attn_ref(x, Wu, bu, Wv, bv, Wg1, bg1, Wg2, bg2, conv_w, conv_b):
        import jax, jax.numpy as jnp
        import numpy as np
        from jax import lax
        B, L, D = (4, 256, 256)
        R = 256
        DH = D // 4
        xc = jnp.transpose(x, (0, 2, 1))
        t = lax.conv_general_dilated(xc, conv_w, window_strides=(1,), padding=[(1, 1)], dimension_numbers=('NCH', 'OIH', 'NCH'), feature_group_count=D)
        t_out = jnp.transpose(t + conv_b[None, :, None], (0, 2, 1))
        u = jnp.einsum('bld,rd->blr', x, Wu) + bu
        v = jnp.einsum('bld,rd->blr', x, Wv) + bv
        h = jax.nn.relu(jnp.einsum('bld,hd->blh', x, Wg1) + bg1)
        gates = jax.nn.sigmoid(jnp.einsum('blh,rh->blr', h, Wg2) + bg2)
        u_gated = u * gates
        v_gated = v * gates
        k_cumsum = jnp.cumsum(u_gated, axis=1)
        global_out = k_cumsum * v_gated
        uv_term = jnp.einsum('blr,rd->bld', global_out, Wu.T[:R, :])
        return t_out + uv_term

    def _L1_ffn_ref(x, w_router, we1, we3, we2, ws1, ws3, ws2):
        import jax, jax.numpy as jnp
        import numpy as np
        TOP_K = 4
        B, S, D = x.shape
        T = B * S
        E = w_router.shape[1]
        xt = x.reshape(T, D)
        probs = jax.nn.softmax(xt @ w_router, axis=-1)
        top_w, top_i = jax.lax.top_k(probs, TOP_K)
        top_w = top_w / jnp.sum(top_w, axis=-1, keepdims=True)
        cw = jnp.zeros((T, E), xt.dtype).at[jnp.arange(T)[:, None], top_i].add(top_w)
        g = jax.nn.silu(jnp.einsum('td,edh->teh', xt, we1)) * jnp.einsum('td,edh->teh', xt, we3)
        g = g * cw[:, :, None]
        moe_out = jnp.einsum('teh,ehd->td', g, we2)
        shared = jax.nn.silu(xt @ ws1) * (xt @ ws3) @ ws2
        k = TOP_K
        out = shared / (k + 1) + moe_out * (k / (k + 1))
        return out.reshape(B, S, D)
    x = L0_attn_hidden_states
    xn = _layernorm(x, axis=-1)
    s = _L0_attn_ref(xn, L0_attn_Wq, L0_attn_Wk, L0_attn_Wv, L0_attn_Wg, L0_attn_Wc, L0_attn_bc)
    g = _silu(_L0_ffn_ref(xn, L0_ffn_Wr, L0_ffn_br, L0_ffn_W1, L0_ffn_W2, L0_ffn_Ws1, L0_ffn_Ws2))
    x = x + s * g
    xn = _layernorm(x, axis=-1)
    s = _L1_attn_ref(xn, L1_attn_Wu, L1_attn_bu, L1_attn_Wv, L1_attn_bv, L1_attn_Wg1, L1_attn_bg1, L1_attn_Wg2, L1_attn_bg2, L1_attn_conv_w, L1_attn_conv_b)
    g = _silu(_L1_ffn_ref(xn, L1_ffn_w_router, L1_ffn_we1, L1_ffn_we3, L1_ffn_we2, L1_ffn_ws1, L1_ffn_ws3, L1_ffn_ws2))
    x = x + s * g
    return x

_drawn_inputs = setup_inputs


def setup_inputs(seed=0):
    import zlib

    import numpy as np

    out = dict(_drawn_inputs(seed))
    spreads = {'L0_attn_bc': (0.0, 0.8),
     'L1_attn_bu': (0.0, 0.1),
     'L1_attn_bv': (0.0, 0.1),
     'L1_attn_bg1': (0.0, 0.8),
     'L1_attn_bg2': (0.0, 0.593),
     'L1_attn_conv_b': (0.0, 0.563)}
    factors = {'L0_attn_Wq': 8.0,
     'L0_attn_Wk': 8.0,
     'L0_attn_Wv': 8.0,
     'L0_attn_Wg': 8.0,
     'L0_attn_Wc': 8.0,
     'L0_ffn_Wr': 8.0,
     'L0_ffn_br': 8.0,
     'L0_ffn_W1': 8.0,
     'L0_ffn_W2': 8.0,
     'L0_ffn_Ws1': 8.0,
     'L0_ffn_Ws2': 8.0,
     'L1_attn_Wg1': 8.0,
     'L1_attn_Wg2': 8.0,
     'L1_attn_conv_w': 8.0}
    for name, (base, spread) in spreads.items():
        noise = np.random.default_rng([zlib.crc32(name.encode()), seed]).standard_normal(out[name].shape)
        drawn = base * np.exp(spread * noise) if base else spread * noise
        out[name] = jnp.asarray(drawn.astype(out[name].dtype))
    for name, factor in factors.items():
        out[name] = (out[name] * factor).astype(out[name].dtype)
    return out
```

```python
from contextlib import ExitStack, contextmanager

import concourse.bass as bass
from concourse import mybir

F32 = mybir.dt.float32
F32R = mybir.dt.float32r
ALU = mybir.AluOpType
ACT = mybir.ActivationFunctionType
AX_X = mybir.AxisListType.X

P = 128
NB, T, D = 8, 512, 256
KC = D // P
TT = T // P
NT = NB * TT
HKV, REP, DH = 8, 2, 128
E0, TOP0, G0, TOPG0 = 32, 6, 8, 4
SHARED0 = 2
SCALE0 = 2.5
E1, TOP1 = 16, 4
SHARED1 = 4
LOG0 = E0 + HKV
EPS_LN = 1e-5
EPS_NORM = 1e-6
GATE_OFFSET = 6.906768
QKV = (REP + 2) * DH
W_ATT = KC * QKV + REP * D
W_E0 = KC * P + D
W_E1 = 2 * KC * P + D
DG = D // 4
MIX_AT = {"u": 0, "v": KC * D, "g1": 2 * KC * D, "g2": 2 * KC * D + KC * P}
W_MIX = 2 * KC * D + KC * P + D
COL_AT = {"bu": 0, "bv": 2, "bg1": 4, "bg2": 5, "conv0": 7, "conv1": 9, "conv2": 11, "conv_b": 13}
COLS = 15
GROUP = 4
CHUNKS = [(0, 0, 512), (1, 512, 384), (3, 896, 128), (2, 1024, 256)]
BANKS = [(0, 512), (512, 1024), (1024, 1280)]
CAUSAL = 1280


class Steps:

    def __init__(self, sem, per):
        self.sem, self.per = sem, per

    def prime(self, engine):
        engine.sem_inc(self.sem, 2 * self.per)

    def __call__(self, i, k=None):
        return self.sem, i * self.per + (2 * self.per + (self.per if k is None else k))


class Space:

    def __init__(self, nc, ctx, tag):
        self.nc, self.ctx, self.tag, self.sems = nc, ctx, tag, []

    def sb(self, name, shape, dt=F32):
        return self.ctx.enter_context(self.nc.sbuf_tensor(f"{self.tag}_{name}", shape, dt))

    def ps(self, name, shape):
        return self.ctx.enter_context(self.nc.psum_tensor(f"{self.tag}_{name}", shape, F32))

    def sem(self, name):
        self.sems.append(self.ctx.enter_context(self.nc.semaphore(f"{self.tag}_{name}")))
        return self.sems[-1]

    @contextmanager
    def block(self):
        with self.nc.Block() as block:
            yield block
        for sem in self.sems:
            self.nc.gpsimd.sem_clear(sem)

    def steps(self, name, per):
        return Steps(self.sem(name), per)


def product3(pe, out, w_hi, w_lo, x_hi, x_lo, first, last):
    pe.matmul(out, w_hi, x_hi, start=first, stop=False)
    pe.matmul(out, w_lo, x_hi, start=False, stop=False)
    return pe.matmul(out, w_hi, x_lo, start=False, stop=last)


def constants(nc, c):
    with ExitStack() as ctx:
        s = Space(nc, ctx, "cst")
        filled, shaped = s.sem("filled"), s.sem("shaped")
        block = ctx.enter_context(s.block())

        @block.gpsimd
        def _(pool):
            pool.memset(c.mean[:, :], 1.0 / D)
            pool.memset(c.ones[:, :], 1.0)
            pool.memset(c.ones_r[:, :].bitcast(F32), 1.0)
            pool.memset(c.eps_ln[:, :], EPS_LN)
            pool.memset(c.eps_norm[:, :], EPS_NORM)
            pool.memset(c.ident[:, :], 0.0).then_inc(filled, 1)
            pool.memset(c.upto[:, :], 1.0).then_inc(filled, 1)
            pool.wait_ge(filled, 2)
            pool.affine_select(out=c.ident[:, :], in_=c.ident[:, :], compare_op=ALU.not_equal, fill=1.0,
                               base=0, pattern=[[-1, P]], channel_multiplier=1).then_inc(shaped, 1)
            pool.affine_select(out=c.upto[:, :], in_=c.upto[:, :], compare_op=ALU.is_ge, fill=0.0,
                               base=0, pattern=[[1, P]], channel_multiplier=-1).then_inc(shaped, 1)
            pool.wait_ge(shaped, 2)


def layernorm(nc, c, tag, rw_dram, n_log, logits, x_dram, combine=None):
    with ExitStack() as ctx:
        s = Space(nc, ctx, tag)
        x = s.sb("x", [P, 2, KC, T])
        xc = s.sb("xc", [P, 2, KC, T])
        sq = s.sb("sq", [P, KC, T])
        xn = s.sb("xn", [P, 2, KC, T])
        rstd = s.sb("rstd", [P, 2, T])
        newt = s.sb("newt", [P, T])
        lgt = s.sb("lgt", [P, T])
        rw = s.sb("rw", [P, KC, P])
        rw_hi = s.sb("rw_hi", [P, KC, P], F32R)
        rw_lo = s.sb("rw_lo", [P, KC, P], F32R)
        mean_ps = s.ps("mean", [P, 2, T])
        var_ps = s.ps("var", [P, 2, T])
        log_ps = s.ps("log", [P, 2, T])
        tok_ps = s.ps("tok", [P, 2, T])
        rw_cleared, rw_loaded, rw_split = s.sem("rw_cleared"), s.sem("rw_loaded"), s.sem("rw_split")
        x_loaded = [s.steps(f"x_loaded{q}", 16) for q in range(2)]
        mean_ready = s.steps("mean_ready", 1)
        centred = s.steps("centred", KC)
        squared = s.steps("squared", KC)
        var_ready = s.steps("var_ready", 1)
        ln_var = s.steps("ln_var", 1)
        rstd_raw = s.steps("rstd_raw", 1)
        newton = s.steps("newton", 4)
        normed = s.steps("normed", KC)
        hi_ready = s.steps("hi_ready", KC)
        lo_ready = s.steps("lo_ready", KC)
        log_ready = s.steps("log_ready", 1)
        log_out = s.steps("log_out", 1)
        tok_ready = s.steps("tok_ready", 1)
        tok_out = s.steps("tok_out", 1)
        if combine:
            ffn_act = s.sb("ffn_act", [P, 2, KC, T])
            mixer = s.sb("mixer", [P, 2, KC, T])
            bias = s.sb("bias", [P, KC])
            bias_loaded = s.sem("bias_loaded")
            mixer_loaded = [s.steps(f"mixer_loaded{q}", 16) for q in range(2)]
            ffn_ready = s.steps("ffn_ready", KC)
            gated = s.steps("gated", KC)
            x_ready = s.steps("x_ready", KC)
            x_stored = [s.steps(f"x_stored{q}", 16) for q in range(2)]
        block = ctx.enter_context(s.block())

        def rows(engine):
            with engine.Fori(0, NB // 2) as pair:
                for par in range(2):
                    yield pair, par, pair * 2 + par

        @block.sync
        def _(sp):
            [q.prime(sp) for q in x_loaded]
            sp.wait_ge(rw_cleared, 1)
            sp.dma_start(rw[:, :, 0:n_log], rw_dram).then_inc(rw_loaded, 16)
            if combine:
                [q.prime(sp) for q in mixer_loaded]
                [q.prime(sp) for q in x_stored]
                sp.dma_start(bias[:, :], combine.bias).then_inc(bias_loaded, 16)
            for pair, par, i in rows(sp):
                sp.wait_ge(*centred(i - 2))
                if combine:
                    sp.wait_ge(*x_stored[par](pair - 1))
                sp.dma_start(x[:, par], x_dram[i]).then_inc(x_loaded[par].sem, 16)
                if combine:
                    sp.dma_start(mixer[:, par], combine.mixer[i]).then_inc(mixer_loaded[par].sem, 16)
            if combine:
                for q in x_stored:
                    sp.wait_ge(*q(NB // 2 - 1))

        @block.tensor
        def _(pe):
            for counter in (mean_ready, var_ready, log_ready, tok_ready):
                counter.prime(pe)
            pe.wait_ge(rw_split, 2)
            for pair, par, i in rows(pe):
                pe.wait_ge(*(x_ready(i) if combine else x_loaded[par](pair)))
                pe.wait_ge(*centred(i - 2))
                for k in range(KC):
                    mm = pe.matmul(mean_ps[:, par], c.mean[:, :], x[:, par, k], start=(k == 0), stop=(k == KC - 1))
                mm.then_inc(mean_ready.sem, 1)
                pe.wait_ge(*squared(i))
                pe.wait_ge(*newton(i - 2))
                for k in range(KC):
                    mm = pe.matmul(var_ps[:, par], c.mean[:, :], sq[:, k], start=(k == 0), stop=(k == KC - 1))
                mm.then_inc(var_ready.sem, 1)
                pe.wait_ge(*hi_ready(i))
                pe.wait_ge(*lo_ready(i))
                pe.wait_ge(*log_out(i - 2))
                for k in range(KC):
                    mm = product3(pe, log_ps[:, par], rw_hi[:, k], rw_lo[:, k], c.xn_hi[:, i, k], c.xn_lo[:, i, k],
                                  k == 0, k == KC - 1)
                mm.then_inc(log_ready.sem, 1)
                pe.wait_ge(*log_out(i))
                pe.wait_ge(*tok_out(i - 2))
                for j in range(TT):
                    mm = pe.transpose(tok_ps[:, par, j * P:(j + 1) * P], lgt[:, j * P:(j + 1) * P], c.ident[:, :])
                mm.then_inc(tok_ready.sem, 1)

        @block.vector
        def _(dve):
            for counter in (centred, newton, normed, tok_out):
                counter.prime(dve)
            dve.wait_ge(rw_split, 1)
            dve.tensor_tensor(rw_lo[:, :, :], rw[:, :, :], rw_hi[:, :, :].bitcast(F32), ALU.subtract).then_inc(rw_split, 1)
            if combine:
                gated.prime(dve)
                x_ready.prime(dve)
                dve.wait_ge(bias_loaded, 16)
            for pair, par, i in rows(dve):
                dve.wait_ge(*x_loaded[par](pair))
                if combine:
                    dve.wait_ge(*mixer_loaded[par](pair))
                    for k in range(KC):
                        dve.wait_ge(*ffn_ready(i, k + 1))
                        dve.scalar_tensor_tensor(out=mixer[:, par, k], in0=mixer[:, par, k], scalar=bias[:, k:k + 1],
                                                 in1=ffn_act[:, par, k], op0=ALU.add, op1=ALU.mult).then_inc(gated.sem, 1)
                        dve.wait_ge(*gated(i, k + 1))
                        dve.tensor_tensor(x[:, par, k], x[:, par, k], mixer[:, par, k], ALU.add).then_inc(x_ready.sem, 1)
                    dve.wait_ge(*x_ready(i))
                dve.wait_ge(*mean_ready(i))
                dve.wait_ge(*squared(i - 2))
                dve.wait_ge(*normed(i - 2))
                for k in range(KC):
                    dve.tensor_tensor(xc[:, par, k], x[:, par, k], mean_ps[:, par], ALU.subtract).then_inc(centred.sem, 1)
                dve.wait_ge(*rstd_raw(i))
                dve.wait_ge(*newton(i - 1))
                dve.tensor_tensor(newt[:, :], rstd[:, par], rstd[:, par], ALU.mult).then_inc(newton.sem, 1)
                dve.wait_ge(*newton(i, 1))
                dve.scalar_tensor_tensor(out=newt[:, :], in0=var_ps[:, par], scalar=EPS_LN, in1=newt[:, :],
                                         op0=ALU.add, op1=ALU.mult).then_inc(newton.sem, 1)
                dve.wait_ge(*newton(i, 2))
                dve.tensor_scalar(newt[:, :], newt[:, :], -0.5, 1.5, ALU.mult, ALU.add).then_inc(newton.sem, 1)
                dve.wait_ge(*newton(i, 3))
                dve.tensor_tensor(rstd[:, par], rstd[:, par], newt[:, :], ALU.mult).then_inc(newton.sem, 1)
                dve.wait_ge(*newton(i))
                dve.wait_ge(*lo_ready(i - 2))
                for k in range(KC):
                    dve.tensor_tensor(xn[:, par, k], xc[:, par, k], rstd[:, par], ALU.mult).then_inc(normed.sem, 1)
                dve.wait_ge(*tok_ready(i))
                dve.tensor_copy(logits[:, bass.ds(i * TT, TT), :],
                                tok_ps[:, par].rearrange("p (j n) -> p j n", j=TT)[:, :, 0:n_log])\
                   .then_inc(tok_out.sem, 1)

        @block.scalar
        def _(act):
            for counter in (squared, ln_var, rstd_raw, hi_ready, log_out):
                counter.prime(act)
            if combine:
                ffn_ready.prime(act)
            if not combine:
                act.preload_act_table_set("natural_log_exp_and_others")
            act.wait_ge(rw_loaded, 16)
            act.activation(rw_hi[:, :, :], rw[:, :, :], ACT.Copy).then_inc(rw_split, 1)
            for pair, par, i in rows(act):
                if combine:
                    act.wait_ge(*gated(i - 2))
                    for k in range(KC):
                        act.activation(ffn_act[:, par, k], c.acc[:, i, k], ACT.Silu).then_inc(ffn_ready.sem, 1)
                    act.wait_ge(*x_ready(i))
                    act.dma_start(combine.x_out[i], x[:, par]).then_inc(x_stored[par].sem, 16)
                act.wait_ge(*var_ready(i - 1))
                for k in range(KC):
                    act.wait_ge(*centred(i, k + 1))
                    act.activation(sq[:, k], xc[:, par, k], ACT.Square).then_inc(squared.sem, 1)
                act.wait_ge(*var_ready(i))
                act.wait_ge(*normed(i - 2))
                act.activation(rstd[:, par], var_ps[:, par], ACT.Ln, bias=c.eps_ln[:, :]).then_inc(ln_var.sem, 1)
                act.wait_ge(*ln_var(i))
                act.activation(rstd[:, par], rstd[:, par], ACT.Exp, scale=-0.5).then_inc(rstd_raw.sem, 1)
                for k in range(KC):
                    act.wait_ge(*normed(i, k + 1))
                    act.activation(c.xn_hi[:, i, k], xn[:, par, k], ACT.Copy).then_inc(hi_ready.sem, 1)
                act.wait_ge(*log_ready(i))
                act.wait_ge(*tok_ready(i - 1))
                act.activation(lgt[:, :], log_ps[:, par], ACT.Copy).then_inc(log_out.sem, 1)

        @block.gpsimd
        def _(pool):
            lo_ready.prime(pool)
            pool.memset(rw[:, :, :], 0.0).then_inc(rw_cleared, 1)
            for pair, par, i in rows(pool):
                for k in range(KC):
                    pool.wait_ge(*hi_ready(i, k + 1))
                    pool.tensor_tensor(c.xn_lo[:, i, k], xn[:, par, k], c.xn_hi[:, i, k].bitcast(F32), ALU.subtract)\
                        .then_inc(lo_ready.sem, 1)


class Chain:

    def __init__(self, engine, sem):
        self.engine, self.sem, self.n = engine, sem, 0

    def __call__(self, instruction):
        self.n += 1
        instruction.then_inc(self.sem, 1)
        self.engine.wait_ge(self.sem, self.n)
        return self.n


def decay_logs(nc, c, logits, g_rows):
    with ExitStack() as ctx:
        s = Space(nc, ctx, "dec")
        N = NT * HKV
        z, absz, u, den, ratio, q, poly, logg = (s.sb(n, [P, N]) for n in ("z", "absz", "u", "den", "ratio", "q", "poly", "logg"))
        total = s.sb("total", [P, NB, TT, HKV])
        before = s.sb("before", [P, NB, TT, HKV])
        g = s.sb("g", [P, NB, HKV, TT])
        g_t = s.sb("g_t", [P, 2, P])
        cum_ps = s.ps("cum", [P, NB, TT, HKV])
        tot_ps = s.ps("tot", [P, NB, TT, HKV])
        turn_ps = s.ps("turn", [P, 2, P])
        absz_ready, u_ready, log_ready, sums_ready, g_ready, turned, stored = (
            s.sem(n) for n in ("absz_ready", "u_ready", "log_ready", "sums_ready", "g_ready", "turned", "stored"))
        steps = s.sem("dve_steps")
        block = ctx.enter_context(s.block())

        @block.vector
        def _(dve):
            link = Chain(dve, steps)
            link(dve.tensor_scalar(z[:, :].rearrange("p (n h) -> p n h", h=HKV), logits[:, :, E0:LOG0],
                                   GATE_OFFSET, None, ALU.add))
            dve.scalar_tensor_tensor(out=absz[:, :], in0=z[:, :], scalar=-1.0, in1=z[:, :],
                                     op0=ALU.mult, op1=ALU.max).then_inc(absz_ready, 1)
            dve.wait_ge(u_ready, 1)
            link(dve.tensor_scalar(den[:, :], u[:, :], 2.0, None, ALU.add))
            link(dve.reciprocal(den[:, :], den[:, :]))
            link(dve.tensor_tensor(ratio[:, :], u[:, :], den[:, :], ALU.mult))
            link(dve.tensor_tensor(q[:, :], ratio[:, :], ratio[:, :], ALU.mult))
            link(dve.tensor_scalar(poly[:, :], q[:, :], 1.0 / 17.0, None, ALU.mult))
            for odd in (15, 13, 11, 9, 7, 5, 3):
                link(dve.scalar_tensor_tensor(out=poly[:, :], in0=poly[:, :], scalar=1.0 / odd, in1=q[:, :],
                                              op0=ALU.add, op1=ALU.mult))
            link(dve.scalar_tensor_tensor(out=poly[:, :], in0=poly[:, :], scalar=1.0, in1=ratio[:, :],
                                          op0=ALU.add, op1=ALU.mult))
            link(dve.tensor_scalar(z[:, :], z[:, :], 0.0, None, ALU.min))
            dve.scalar_tensor_tensor(out=logg[:, :], in0=poly[:, :], scalar=-2.0, in1=z[:, :],
                                     op0=ALU.mult, op1=ALU.add).then_inc(log_ready, 1)
            dve.wait_ge(sums_ready, 2)
            link(dve.memset(before[:, :, :, :], 0.0))
            link(dve.tensor_copy(total[:, :, :, :], tot_ps[:, :, :, :]))
            for j in range(1, TT):
                link(dve.tensor_tensor(before[:, :, j], before[:, :, j - 1], total[:, :, j - 1], ALU.add))
            link(dve.tensor_tensor(g[:, :, :, :].rearrange("p b h j -> p b j h"), cum_ps[:, :, :, :], before[:, :, :, :],
                                   ALU.add))
            dve.tensor_scalar(c.neg_g[:, :], g[:, :, :, :].rearrange("p b h j -> p (b h j)"), -1.0, None,
                              ALU.mult).then_inc(g_ready, 1)
            dve.wait_ge(turned, 1)
            dve.tensor_copy(g_t[:, :, :], turn_ps[:, :, :]).then_inc(g_ready, 1)

        @block.scalar
        def _(act):
            act.preload_act_table_set("natural_log_exp_and_others")
            act.wait_ge(absz_ready, 1)
            act.activation(u[:, :], absz[:, :], ACT.Exp, scale=-1.0).then_inc(u_ready, 1)

        @block.tensor
        def _(pe):
            pe.wait_ge(log_ready, 1)
            pe.matmul(cum_ps[:, :, :, :].rearrange("p b j h -> p (b j h)"), c.upto[:, :], logg[:, :],
                      start=True, stop=True).then_inc(sums_ready, 1)
            pe.matmul(tot_ps[:, :, :, :].rearrange("p b j h -> p (b j h)"), c.ones[:, :], logg[:, :],
                      start=True, stop=True).then_inc(sums_ready, 1)
            pe.wait_ge(g_ready, 1)
            for half in range(2):
                mm = pe.transpose(turn_ps[:, half], g[:, :, :, :].rearrange("p b h j -> p (b h j)")[:, half * P:(half + 1) * P],
                                  c.ident[:, :])
            mm.then_inc(turned, 1)

        @block.sync
        def _(sp):
            sp.wait_ge(g_ready, 2)
            sp.dma_start(g_rows.rearrange("r (j t) -> (r j) t", t=P).rearrange("(a p) t -> p a t", p=P), g_t[:, :, :])\
              .then_inc(stored, 16)
            sp.wait_ge(stored, 16)


def pick_top(dve, link, values, pad_at, top8, picked, k, is_picked):
    for n in range(NT):
        dve.max(top8[:, n], values[:, n, 0:pad_at]).then_inc(link.sem, 1)
    link.n += NT
    dve.wait_ge(link.sem, link.n)
    link(dve.memset(top8[:, :, k:8], -1.0))
    for n in range(NT):
        dve.match_replace(picked[:, n], top8[:, n], values[:, n], -2.0).then_inc(link.sem, 1)
    link.n += NT
    dve.wait_ge(link.sem, link.n)
    link(dve.tensor_scalar(is_picked, picked[:, :, 0:pad_at], -2.0, None, ALU.is_equal))


def store_gates(sp, gates, g_t, n_e, tiles, stored):
    to = gates[0:n_e, :].rearrange("e (g l t) -> l e g t", l=tiles, t=P)
    for tile in range(tiles):
        sp.dma_start(to[tile], g_t[tile * n_e:(tile + 1) * n_e]).then_inc(stored, 16)


def route0(nc, c, logits, bias_row, gates):
    with ExitStack() as ctx:
        s = Space(nc, ctx, "rt0")
        GS = E0 // G0
        bias = s.sb("bias", [P, E0])
        score = s.sb("score", [P, NT, E0])
        pair = s.sb("pair", [P, NT * G0, 6])
        group = s.sb("group", [P, NT, G0 + 8])
        top8 = s.sb("top8", [P, NT, 8])
        gpick = s.sb("gpick", [P, NT, G0 + 8])
        gmask = s.sb("gmask", [P, NT, G0])
        masked = s.sb("masked", [P, NT, E0 + 8])
        epick = s.sb("epick", [P, NT, E0 + 8])
        weight = s.sb("weight", [P, NT, E0])
        norm = s.sb("norm", [P, NT])
        g_t = s.sb("g_t", [P, NB, P])
        turn_ps = s.ps("turn", [P, NB, P])
        loaded, logit_ready, score_ready, gates_ready, turned, g_t_ready, stored = (
            s.sem(n) for n in ("loaded", "logit_ready", "score_ready", "gates_ready", "turned", "g_t_ready", "stored"))
        steps = s.sem("dve_steps")
        block = ctx.enter_context(s.block())

        @block.scalar
        def _(act):
            act.wait_ge(logit_ready, 1)
            act.activation(score[:, :, :], weight[:, :, :], ACT.Sigmoid).then_inc(score_ready, 1)

        @block.vector
        def _(dve):
            link = Chain(dve, steps)
            link(dve.memset(group[:, :, :], -1.0))
            link(dve.memset(masked[:, :, :], -1.0))
            dve.wait_ge(loaded, 16)
            dve.tensor_tensor(weight[:, :, :], logits[:, :, 0:E0], bias[:, :].unsqueeze(1).to_broadcast([P, NT, E0]),
                              ALU.add).then_inc(logit_ready, 1)
            dve.wait_ge(score_ready, 1)
            four = score[:, :, :].rearrange("p n (g e) -> p (n g) e", e=GS)
            link(dve.tensor_tensor(pair[:, :, 0:2], four[:, :, 0:2], four[:, :, 2:4], ALU.add))
            link(dve.tensor_tensor(pair[:, :, 2:4], four[:, :, 0:4:2], four[:, :, 1:4:2], ALU.add))
            link(dve.tensor_tensor(pair[:, :, 4:5], four[:, :, 0:1], four[:, :, 3:4], ALU.add))
            link(dve.tensor_tensor(pair[:, :, 5:6], four[:, :, 1:2], four[:, :, 2:3], ALU.add))
            link(dve.tensor_reduce(group[:, :, 0:G0], pair[:, :, :].rearrange("p (n g) e -> p n g e", g=G0), AX_X, ALU.max))
            pick_top(dve, link, group, G0, top8, gpick, TOPG0, gmask[:, :, :])
            link(dve.tensor_tensor(masked[:, :, 0:E0].rearrange("p n (g e) -> p n g e", e=GS),
                                   score[:, :, :].rearrange("p n (g e) -> p n g e", e=GS),
                                   gmask[:, :, :].unsqueeze(3).to_broadcast([P, NT, G0, GS]), ALU.mult))
            pick_top(dve, link, masked, E0, top8, epick, TOP0, weight[:, :, :])
            link(dve.tensor_tensor(weight[:, :, :], weight[:, :, :], score[:, :, :], ALU.mult))
            link(dve.tensor_reduce(norm[:, :], weight[:, :, :], AX_X, ALU.add))
            link(dve.tensor_scalar(norm[:, :], norm[:, :], 1e-20, None, ALU.add))
            link(dve.reciprocal(norm[:, :], norm[:, :]))
            link(dve.tensor_tensor(weight[:, :, :], weight[:, :, :], norm[:, :].unsqueeze(2).to_broadcast([P, NT, E0]), ALU.mult))
            dve.tensor_scalar(weight[:, :, :], weight[:, :, :], SCALE0, None, ALU.mult).then_inc(gates_ready, 1)
            dve.wait_ge(turned, 1)
            dve.tensor_copy(g_t[:, :, :], turn_ps[:, :, :]).then_inc(g_t_ready, 1)

        @block.tensor
        def _(pe):
            pe.wait_ge(gates_ready, 1)
            for b in range(NB):
                mm = pe.transpose(turn_ps[:, b], weight[:, b * TT:(b + 1) * TT].rearrange("p n e -> p (n e)"), c.ident[:, :])
            mm.then_inc(turned, 1)

        @block.sync
        def _(sp):
            sp.dma_start(bias[:, :], bias_row.to_broadcast([P, E0])).then_inc(loaded, 16)
            sp.dma_start(gates[E0:E0 + SHARED0, :].rearrange("e (n t) -> (e n) t", t=P), c.ones[0:SHARED0 * NT, :])\
              .then_inc(stored, 16)
            sp.wait_ge(g_t_ready, 1)
            store_gates(sp, gates, g_t, E0, TT, stored)
            sp.wait_ge(stored, 16 * (1 + TT))


def attention(nc, c, weights, g_rows):
    TILES = len(BANKS)
    with ExitStack() as ctx:
        s = Space(nc, ctx, "att")
        w_raw = s.sb("w_raw", [P, W_ATT])
        w_hi = s.sb("w_hi", [P, 2, W_ATT], F32R)
        w_lo = s.sb("w_lo", [P, 2, W_ATT], F32R)
        qk_hi = s.sb("qk_hi", [P, REP + 1, T], F32R)
        qk_lo = s.sb("qk_lo", [P, REP + 1, T], F32R)
        v_feat = s.sb("v_feat", [P, T])
        v_hi = s.sb("v_hi", [P, T], F32R)
        v_lo = s.sb("v_lo", [P, T], F32R)
        g_all = s.sb("g_all", [P, T])
        decay = s.sb("decay", [P, CAUSAL])
        a = s.sb("a", [P, TILES, T])
        a_hi = s.sb("a_hi", [P, REP, CAUSAL], F32R)
        a_lo = s.sb("a_lo", [P, REP, CAUSAL], F32R)
        inv = s.sb("inv", [P, T])
        fix = s.sb("fix", [P, T])
        y = s.sb("y", [P, T])
        y_hi = s.sb("y_hi", [P, REP, T], F32R)
        y_lo = s.sb("y_lo", [P, REP, T], F32R)
        work_ps = s.ps("work", [P, 3, T])
        score_ps = s.ps("score", [P, 2, T])
        y_ps = s.ps("y_ps", [P, REP, T])
        norm_ps = s.ps("norm", [P, T])

        cleared, mask_begun = s.sem("acc_cleared"), s.sem("mask_begun")
        w_loaded = s.steps("w_loaded", 16)
        w_hi_ready = s.steps("w_hi_ready", 1)
        w_ready = s.steps("w_ready", 1)
        g_loaded = s.steps("g_loaded", 16)
        decay_raw = s.steps("decay_raw", 1)
        decay_ready = s.steps("decay_ready", 1)
        qk_proj = s.steps("qk_proj", REP + 1)
        qk_hi_ready = s.steps("qk_hi_ready", REP + 1)
        qk_ready = s.steps("qk_ready", REP + 1)
        v_proj = s.steps("v_proj", 1)
        v_copied = s.steps("v_copied", 1)
        v_turned = s.steps("v_turned", 1)
        v_hi_ready = s.steps("v_hi_ready", 1)
        v_ready = s.steps("v_ready", 1)
        scored = s.steps("scored", REP * TILES)
        squared = s.steps("squared", REP * TILES)
        decayed = s.steps("decayed", REP * TILES)
        a_hi_ready = s.steps("a_hi_ready", REP * TILES)
        a_ready = s.steps("a_ready", REP * TILES)
        summed = s.steps("summed", REP)
        logged = s.steps("logged", REP)
        inv_raw = s.steps("inv_raw", REP)
        fixed = s.steps("fixed", 3 * REP)
        y_hi_ready = s.steps("y_hi_ready", REP)
        y_ready = s.steps("y_ready", REP)
        mixed = s.steps("mixed", KC)
        added = s.steps("added", KC)
        block = ctx.enter_context(s.block())

        def col(w, par, part, k=0):
            at = {"q0": 0, "q1": DH, "k": REP * DH, "v": (REP + 1) * DH}
            if part in at:
                return w[:, par, k * QKV + at[part]:k * QKV + at[part] + DH]
            q, chunk = part
            at = KC * QKV + q * D + chunk * P
            return w[:, par, at:at + P]

        def walk(engine, start, unit, end):
            with engine.Fori(0, HKV // 2) as pair:
                base = pair * (2 * NB)
                start(base, pair)
                for par in range(2):
                    i0 = base + par * NB
                    unit(i0, 0, par, pair, (i0 + 1, 1, par), None if par == 0 else (i0 - 1, NB - 1, 0))
                    with engine.Fori(1, NB - 1) as b:
                        unit(i0 + b, b, par, pair, (i0 + b + 1, b + 1, par), (i0 + b - 1, b - 1, par))
                    unit(i0 + (NB - 1), NB - 1, par, pair, (i0 + NB, 0, 1) if par == 0 else None,
                         (i0 + (NB - 2), NB - 2, par))
                end(base + (2 * NB - 1), NB - 1, 1)

        def first_row(b):
            return isinstance(b, int) and b == 0

        @block.sync
        def _(sp):
            w_loaded.prime(sp)
            g_loaded.prime(sp)

            def load_w(h):
                sp.wait_ge(*w_ready(h - 1))
                sp.dma_start(w_raw[:, :], weights[h]).then_inc(w_loaded.sem, 16)

            def load_g(i, b, h):
                sp.wait_ge(*decay_raw(i - 1))
                sp.dma_start(g_all[:, :], g_rows[bass.ds(b * HKV + h, 1), :].to_broadcast([P, T])).then_inc(g_loaded.sem, 16)

            load_w(0)

            def start(i, pair):
                load_g(i, 0, pair * 2)

            def unit(i, b, par, pair, nxt, prev):
                if first_row(b):
                    load_w(pair * 2 + (par + 1))
                if nxt:
                    load_g(nxt[0], nxt[1], pair * 2 + nxt[2])

            walk(sp, start, unit, lambda *_: None)

        @block.tensor
        def _(pe):
            for counter in (qk_proj, v_proj, v_turned, scored, summed, mixed):
                counter.prime(pe)

            def project(i, b, par, part, n):
                bank = {"q0": 2, "q1": 0, "k": 1, "v": 2}[part]
                for k in range(KC):
                    mm = product3(pe, work_ps[:, bank], col(w_hi, par, part, k), col(w_lo, par, part, k),
                                  c.xn_hi[:, b, k], c.xn_lo[:, b, k], k == 0, k == KC - 1)
                mm.then_inc(n.sem, 1)

            def project_q0(i, b, par):
                pe.wait_ge(*v_copied(i - 1))
                project(i, b, par, "q0", qk_proj)

            def project_q1_k(i, b, par, last_out):
                pe.wait_ge(*v_ready(i - 1))
                pe.wait_ge(*added(last_out, 1))
                project(i, b, par, "q1", qk_proj)
                pe.wait_ge(*added(last_out))
                project(i, b, par, "k", qk_proj)

            def project_v(i, b, par):
                pe.wait_ge(*qk_ready(i, 1))
                project(i, b, par, "v", v_proj)
                pe.wait_ge(*qk_ready(i, 2))
                pe.wait_ge(*v_copied(i))
                for j in range(TT):
                    mm = pe.transpose(work_ps[:, 0, j * P:(j + 1) * P], v_feat[:, j * P:(j + 1) * P], c.ident[:, :])
                mm.then_inc(v_turned.sem, 1)

            def output(i, par, last_proj):
                pe.wait_ge(*y_ready(i))
                pe.wait_ge(*v_ready(last_proj))
                pe.wait_ge(*qk_ready(last_proj))
                for chunk in range(KC):
                    for q in range(REP):
                        mm = product3(pe, work_ps[:, chunk], col(w_hi, par, (q, chunk)), col(w_lo, par, (q, chunk)),
                                      y_hi[:, q], y_lo[:, q], q == 0, q == REP - 1)
                    mm.then_inc(mixed.sem, 1)

            def scores(i, q):
                pe.wait_ge(*qk_ready(i))
                for tile, (lo, hi) in enumerate(BANKS):
                    n = q * TILES + tile
                    pe.wait_ge(*(squared(i, n - 1) if n >= 2 else squared(i - 1, REP * TILES + n - 1)))
                    for j, at, width in CHUNKS:
                        if lo <= at < hi:
                            keys, t0 = slice(j * P, (j + 1) * P), T - width
                            mm = product3(pe, score_ps[:, n % 2, at - lo:at - lo + width],
                                          qk_hi[:, REP, keys], qk_lo[:, REP, keys],
                                          qk_hi[:, q, t0:T], qk_lo[:, q, t0:T], True, True)
                    mm.then_inc(scored.sem, 1)

            def weigh(i, q):
                pe.wait_ge(*v_ready(i))
                pe.wait_ge(*fixed(i - 1, 3 * q + 3))
                pe.wait_ge(*(fixed(i, 1) if q else fixed(i - 1, 4)))
                for tile, (lo, hi) in enumerate(BANKS):
                    pe.wait_ge(*a_ready(i, q * TILES + tile + 1))
                    for j, at, width in CHUNKS:
                        if lo <= at < hi:
                            keys, t0 = slice(j * P, (j + 1) * P), T - width
                            first, last = j == 0, j == 2
                            product3(pe, y_ps[:, q, t0:T], v_hi[:, keys], v_lo[:, keys],
                                     a_hi[:, q, at:at + width], a_lo[:, q, at:at + width], first, last)
                            pe.matmul(norm_ps[:, t0:T], c.ones_r[:, :], a_hi[:, q, at:at + width], start=first, stop=False)
                            mm = pe.matmul(norm_ps[:, t0:T], c.ones_r[:, :], a_lo[:, q, at:at + width], start=False, stop=last)
                mm.then_inc(summed.sem, 1)

            def start(i, pair):
                pe.wait_ge(*w_ready(pair * 2))
                project_q0(i, 0, 0)
                project_q1_k(i, 0, 0, i - 1)
                project_v(i, 0, 0)

            def unit(i, b, par, pair, nxt, prev):
                scores(i, 0)
                scores(i, 1)
                if prev:
                    output(prev[0], prev[2], i)
                last_out = i - 1
                if nxt:
                    if first_row(nxt[1]):
                        pe.wait_ge(*w_ready(pair * 2 + 1))
                    project_q0(*nxt)
                weigh(i, 0)
                if nxt:
                    project_q1_k(*nxt, last_out)
                weigh(i, 1)
                if nxt:
                    project_v(*nxt)

            walk(pe, start, unit, lambda i, b, par: output(i, par, i))

        @block.scalar
        def _(act):
            for counter in (w_hi_ready, decay_raw, qk_hi_ready, v_copied, v_hi_ready, squared, logged, inv_raw, y_hi_ready):
                counter.prime(act)
            act.preload_act_table_set("natural_log_exp_and_others")

            def split_w(h, par, last_out):
                act.wait_ge(*w_loaded(h))
                act.wait_ge(*mixed(last_out))
                act.activation(w_hi[:, par], w_raw[:, :], ACT.Copy).then_inc(w_hi_ready.sem, 1)

            def decays(i, b, h):
                act.wait_ge(*g_loaded(i))
                act.wait_ge(*decayed(i - 1))
                for j, at, width in CHUNKS:
                    ins = act.activation(decay[:, at:at + width], g_all[:, T - width:T], ACT.Exp,
                                         bias=c.neg_g[:, bass.ds(b * (HKV * TT) + h * TT + j, 1)])
                ins.then_inc(decay_raw.sem, 1)

            def qk_high(i, n):
                act.wait_ge(*qk_proj(i, n + 1))
                act.wait_ge(*scored(i - 1))
                act.activation(qk_hi[:, n], work_ps[:, {0: 2, 1: 0, 2: 1}[n]], ACT.Copy).then_inc(qk_hi_ready.sem, 1)

            def v_copy(i):
                act.wait_ge(*v_proj(i))
                act.wait_ge(*v_turned(i - 1))
                act.activation(v_feat[:, :], work_ps[:, 2], ACT.Copy).then_inc(v_copied.sem, 1)

            def v_high(i):
                act.wait_ge(*v_turned(i))
                act.wait_ge(*summed(i - 1))
                act.activation(v_hi[:, :], work_ps[:, 0], ACT.Copy).then_inc(v_hi_ready.sem, 1)

            def square(i, q):
                for tile, (lo, hi) in enumerate(BANKS):
                    n = q * TILES + tile
                    act.wait_ge(*scored(i, n + 1))
                    act.wait_ge(*(a_ready(i, tile + 1) if q else a_ready(i - 1, TILES + tile + 1)))
                    act.activation(a[:, tile, 0:hi - lo], score_ps[:, n % 2, 0:hi - lo], ACT.Square,
                                   scale=DH ** -0.5).then_inc(squared.sem, 1)

            def invert(i, q):
                act.wait_ge(*summed(i, q + 1))
                act.wait_ge(*(fixed(i, 2) if q else fixed(i - 1, 5)))
                act.activation(inv[:, :], norm_ps[:, :], ACT.Ln, bias=c.eps_norm[:, :]).then_inc(logged.sem, 1)
                act.wait_ge(*logged(i, q + 1))
                act.activation(inv[:, :], inv[:, :], ACT.Exp, scale=-1.0).then_inc(inv_raw.sem, 1)

            def y_high(i, q):
                act.wait_ge(*fixed(i, 3 * q + 3))
                act.wait_ge(*mixed(i - 1))
                act.activation(y_hi[:, q], y[:, :], ACT.Copy).then_inc(y_hi_ready.sem, 1)

            split_w(0, 0, -1)

            def start(i, pair):
                decays(i, 0, pair * 2)
                for n in range(REP + 1):
                    qk_high(i, n)
                v_copy(i)
                v_high(i)

            def unit(i, b, par, pair, nxt, prev):
                square(i, 0)
                if prev:
                    y_high(prev[0], 1)
                square(i, 1)
                if nxt:
                    qk_high(nxt[0], 0)
                invert(i, 0)
                if nxt:
                    qk_high(nxt[0], 1)
                y_high(i, 0)
                if nxt:
                    qk_high(nxt[0], 2)
                    decays(nxt[0], nxt[1], pair * 2 + nxt[2])
                    v_copy(nxt[0])
                invert(i, 1)
                if nxt:
                    v_high(nxt[0])
                if first_row(b):
                    split_w(pair * 2 + (par + 1), 1 - par, i - 1)

            walk(act, start, unit, lambda i, b, par: y_high(i, 1))

        @block.vector
        def _(dve):
            for counter in (qk_ready, v_ready, a_hi_ready, a_ready, fixed, y_ready, added):
                counter.prime(dve)
            dve.wait_ge(cleared, 1)

            def qk_low(i, n):
                dve.wait_ge(*qk_hi_ready(i, n + 1))
                dve.tensor_tensor(qk_lo[:, n], work_ps[:, {0: 2, 1: 0, 2: 1}[n]], qk_hi[:, n].bitcast(F32),
                                  ALU.subtract).then_inc(qk_ready.sem, 1)

            def v_low(i):
                dve.wait_ge(*v_hi_ready(i))
                dve.tensor_tensor(v_lo[:, :], work_ps[:, 0], v_hi[:, :].bitcast(F32), ALU.subtract).then_inc(v_ready.sem, 1)

            def split_a(i, q, tile):
                lo, hi = BANKS[tile]
                n = q * TILES + tile
                dve.wait_ge(*decayed(i, n + 1))
                dve.wait_ge(*summed(i - 1, q + 1))
                dve.tensor_copy(a_hi[:, q, lo:hi], a[:, tile, 0:hi - lo]).then_inc(a_hi_ready.sem, 1)
                dve.wait_ge(*a_hi_ready(i, n + 1))
                dve.tensor_tensor(a_lo[:, q, lo:hi], a[:, tile, 0:hi - lo], a_hi[:, q, lo:hi].bitcast(F32),
                                  ALU.subtract).then_inc(a_ready.sem, 1)

            def divide(i, q):
                dve.wait_ge(*inv_raw(i, q + 1))
                dve.wait_ge(*(fixed(i, 3) if q else fixed(i - 1)))
                dve.scalar_tensor_tensor(out=fix[:, :], in0=norm_ps[:, :], scalar=EPS_NORM, in1=inv[:, :],
                                         op0=ALU.add, op1=ALU.mult).then_inc(fixed.sem, 1)
                dve.wait_ge(*fixed(i, 3 * q + 1))
                dve.scalar_tensor_tensor(out=fix[:, :], in0=fix[:, :], scalar=-2.0, in1=inv[:, :],
                                         op0=ALU.add, op1=ALU.mult).then_inc(fixed.sem, 1)
                dve.wait_ge(*fixed(i, 3 * q + 2))
                dve.wait_ge(*(y_ready(i, 1) if q else y_ready(i - 1)))
                dve.scalar_tensor_tensor(out=y[:, :], in0=y_ps[:, q], scalar=-1.0, in1=fix[:, :],
                                         op0=ALU.mult, op1=ALU.mult).then_inc(fixed.sem, 1)

            def y_low(i, q):
                dve.wait_ge(*y_hi_ready(i, q + 1))
                dve.tensor_tensor(y_lo[:, q], y[:, :], y_hi[:, q].bitcast(F32), ALU.subtract).then_inc(y_ready.sem, 1)

            def add(i, b):
                for chunk in range(KC):
                    dve.wait_ge(*mixed(i, chunk + 1))
                    dve.tensor_tensor(c.acc[:, b, chunk], c.acc[:, b, chunk], work_ps[:, chunk], ALU.add).then_inc(added.sem, 1)

            def start(i, pair):
                for n in range(REP + 1):
                    qk_low(i, n)
                v_low(i)

            def unit(i, b, par, pair, nxt, prev):
                if prev:
                    divide(prev[0], 1)
                split_a(i, 0, 0)
                if prev:
                    y_low(prev[0], 1)
                split_a(i, 0, 1)
                split_a(i, 0, 2)
                split_a(i, 1, 0)
                split_a(i, 1, 1)
                if prev:
                    add(prev[0], prev[1])
                split_a(i, 1, 2)
                if nxt:
                    qk_low(nxt[0], 0)
                divide(i, 0)
                if nxt:
                    qk_low(nxt[0], 1)
                y_low(i, 0)
                if nxt:
                    qk_low(nxt[0], 2)
                    v_low(nxt[0])

            def end(i, b, par):
                divide(i, 1)
                y_low(i, 1)
                add(i, b)

            walk(dve, start, unit, end)

        @block.gpsimd
        def _(pool):
            for counter in (w_ready, decay_ready, decayed):
                counter.prime(pool)
            pool.memset(c.acc[:, :, :, :], 0.0).then_inc(cleared, 1)

            def split_w(h, par):
                pool.wait_ge(*w_hi_ready(h))
                pool.tensor_tensor(w_lo[:, par], w_raw[:, :], w_hi[:, par].bitcast(F32), ALU.subtract).then_inc(w_ready.sem, 1)

            def mask(i):
                pool.wait_ge(*decay_raw(i))
                pool.sem_inc(mask_begun, 1)
                for j, at, width in CHUNKS:
                    ins = pool.affine_select(out=decay[:, at:at + P], in_=decay[:, at:at + P], compare_op=ALU.is_ge,
                                             fill=0.0, base=0, pattern=[[1, P]], channel_multiplier=-1)
                ins.then_inc(decay_ready.sem, 1)

            def apply_decay(i, q):
                if q == 0:
                    pool.wait_ge(*decay_ready(i))
                for tile, (lo, hi) in enumerate(BANKS):
                    n = q * TILES + tile
                    pool.wait_ge(*squared(i, n + 1))
                    pool.tensor_tensor(a[:, tile, 0:hi - lo], a[:, tile, 0:hi - lo], decay[:, lo:hi], ALU.mult)\
                        .then_inc(decayed.sem, 1)

            split_w(0, 0)

            def start(i, pair):
                mask(i)

            def unit(i, b, par, pair, nxt, prev):
                apply_decay(i, 0)
                apply_decay(i, 1)
                if nxt:
                    mask(nxt[0])
                if first_row(b):
                    split_w(pair * 2 + (par + 1), 1 - par)

            walk(pool, start, unit, lambda *_: None)


def experts(nc, c, tag, weights, gates, n_full, last_size, swiglu, mixer_out):
    NZ = 2 if swiglu else 1
    W_E = W_E1 if swiglu else W_E0
    ZB = 4
    with ExitStack() as ctx:
        s = Space(nc, ctx, tag)
        w_raw = s.sb("w_raw", [P, GROUP * W_E])
        w_hi = s.sb("w_hi", [P, 2, GROUP * W_E], F32R)
        w_lo = s.sb("w_lo", [P, 2, GROUP * W_E], F32R)
        gate = s.sb("gate", [P, 2, GROUP, T])
        act_gate = s.sb("act_gate", [P, 2, T])
        h = s.sb("h", [P, 2, T])
        h_hi = s.sb("h_hi", [P, GROUP, T], F32R)
        h_lo = s.sb("h_lo", [P, GROUP, T], F32R)
        z_ps = s.ps("z", [P, ZB, T])
        out_ps = s.ps("out", [P, 2, KC, T])
        mixer_stored, cleared = s.sem("mixer_stored"), s.sem("acc_cleared")
        w_loaded = s.steps("w_loaded", 16)
        w_hi_ready = s.steps("w_hi_ready", 1)
        w_ready = s.steps("w_ready", 1)
        g_loaded = [s.steps(f"g_loaded{q}", 16) for q in range(2)]
        projected = s.steps("projected", GROUP)
        silu_ready = s.steps("silu_ready", GROUP)
        act_ready = s.steps("act_ready", GROUP)
        h_ready = s.steps("h_ready", GROUP)
        h_hi_ready = s.steps("h_hi_ready", GROUP)
        h_split = s.steps("h_split", GROUP)
        used = s.steps("used", GROUP)
        added = s.steps("added", KC)
        block = ctx.enter_context(s.block())

        def walk(engine, unit, prefetch=None):
            def group(g, par, size):
                for sub in range(2):
                    unit(g * NB + sub, g, 0, sub, par, size)
                if prefetch and size == GROUP and not isinstance(g, int):
                    prefetch(g + 1, 1 - par, g * NB - 1)
                with engine.Fori(1, NB // 2) as pair:
                    for sub in range(2):
                        unit(g * NB + (pair * 2 + sub), g, pair, sub, par, size)

            with engine.Fori(0, n_full // 2) as two:
                for par in range(2):
                    group(two * 2 + par, par, GROUP)
            group(n_full, 0, last_size)

        @block.sync
        def _(sp):
            w_loaded.prime(sp)
            for q in g_loaded:
                q.prime(sp)

            def load_w(g, par, last):
                sp.wait_ge(*w_ready(g - 1))
                sp.dma_start(w_raw[:, :], weights[g]).then_inc(w_loaded.sem, 16)

            def unit(i, g, pr, sub, par, size):
                b = pr * 2 + sub
                sp.wait_ge(*act_ready(i - 2))
                src = gates[bass.ds(g * GROUP, size), bass.ds(b * T, T)]
                sp.dma_start(gate[:, sub, 0:size], src.unsqueeze(0).to_broadcast([P, size, T])).then_inc(g_loaded[sub].sem, 16)

            load_w(0, 0, -1)
            sp.dma_start(mixer_out.rearrange("b p k t -> p b k t"), c.acc[:, :, :, :]).then_inc(mixer_stored, 16)
            walk(sp, unit, load_w)
            sp.wait_ge(mixer_stored, 16)

        @block.tensor
        def _(pe):
            projected.prime(pe)
            used.prime(pe)

            def unit(i, g, pr, sub, par, size):
                b = pr * 2 + sub
                inc = GROUP // size
                if isinstance(b, int) and b == 0:
                    pe.wait_ge(*w_ready(g))
                for e in range(size):
                    pe.wait_ge(*(h_ready(i, (e - ZB // NZ + 1) * inc) if e >= ZB // NZ else h_ready(i - 1)))
                    for n in range(NZ):
                        for k in range(KC):
                            at = e * W_E + (n * KC + k) * P
                            mm = product3(pe, z_ps[:, (e * NZ + n) % ZB], w_hi[:, par, at:at + P], w_lo[:, par, at:at + P],
                                          c.xn_hi[:, b, k], c.xn_lo[:, b, k], k == 0, k == KC - 1)
                    mm.then_inc(projected.sem, inc)
                pe.wait_ge(*added(i - 2))
                for e in range(size):
                    pe.wait_ge(*h_split(i, (e + 1) * inc))
                    for chunk in range(KC):
                        at = e * W_E + NZ * KC * P + chunk * P
                        mm = product3(pe, out_ps[:, sub, chunk], w_hi[:, par, at:at + P], w_lo[:, par, at:at + P],
                                      h_hi[:, e], h_lo[:, e], e == 0, e == size - 1)
                    mm.then_inc(used.sem, inc)

            walk(pe, unit)

        @block.scalar
        def _(act):
            for counter in (w_hi_ready, silu_ready, h_hi_ready):
                counter.prime(act)
            if swiglu:
                act.preload_act_table_set("silu_and_others")

            def split_w(g, par, last):
                act.wait_ge(*w_loaded(g))
                act.wait_ge(*used(last))
                act.activation(w_hi[:, par], w_raw[:, :], ACT.Copy).then_inc(w_hi_ready.sem, 1)

            def silu(i, e, inc):
                act.wait_ge(*projected(i, (e + 1) * inc))
                act.wait_ge(*(h_ready(i, (e - 1) * inc) if e >= 2 else h_ready(i - 1)))
                act.activation(act_gate[:, e % 2], z_ps[:, e * NZ % ZB], ACT.Silu).then_inc(silu_ready.sem, inc)

            def unit(i, g, pr, sub, par, size):
                inc = GROUP // size
                for e in range(size + 1):
                    if swiglu and e < size:
                        silu(i, e, inc)
                    if e >= 1:
                        act.wait_ge(*h_ready(i, e * inc))
                        act.wait_ge(*used(i - 1))
                        act.activation(h_hi[:, e - 1], h[:, (e - 1) % 2], ACT.Copy).then_inc(h_hi_ready.sem, inc)

            split_w(0, 0, -1)
            walk(act, unit, split_w)

        @block.vector
        def _(dve):
            for counter in (h_ready, h_split, added) + (() if swiglu else (act_ready,)):
                counter.prime(dve)

            def low(i, e, inc):
                dve.wait_ge(*h_hi_ready(i, (e + 1) * inc))
                dve.tensor_tensor(h_lo[:, e], h[:, e % 2], h_hi[:, e].bitcast(F32), ALU.subtract).then_inc(h_split.sem, inc)

            def unit(i, g, pr, sub, par, size):
                b = pr * 2 + sub
                inc = GROUP // size
                if not swiglu:
                    dve.wait_ge(*g_loaded[sub](g * (NB // 2) + pr))
                for e in range(size):
                    n = (e + 1) * inc
                    z = z_ps[:, (e * NZ + NZ - 1) % ZB]
                    if swiglu:
                        dve.wait_ge(*act_ready(i, n))
                    else:
                        dve.wait_ge(*projected(i, n))
                        dve.wait_ge(*(h_ready(i, n - 2 * inc) if e >= 2 else h_ready(i - 1)))
                        dve.scalar_tensor_tensor(out=act_gate[:, e % 2], in0=z, scalar=0.0, in1=gate[:, sub, e],
                                                 op0=ALU.max, op1=ALU.mult).then_inc(act_ready.sem, inc)
                        dve.wait_ge(*act_ready(i, n))
                    dve.wait_ge(*(h_split(i, n - 2 * inc) if e >= 2 else h_split(i - 1)))
                    dve.tensor_tensor(h[:, e % 2], act_gate[:, e % 2], z, ALU.mult).then_inc(h_ready.sem, inc)
                    if e >= 1:
                        low(i, e - 1, inc)
                low(i, size - 1, inc)
                if isinstance(b, int) and b == 0:
                    dve.wait_ge(cleared, 1)
                for chunk in range(KC):
                    dve.wait_ge(*used(i))
                    dve.tensor_tensor(c.acc[:, b, chunk], c.acc[:, b, chunk], out_ps[:, sub, chunk], ALU.add).then_inc(added.sem, 1)

            walk(dve, unit)

        @block.gpsimd
        def _(pool):
            w_ready.prime(pool)
            if swiglu:
                act_ready.prime(pool)

            def split_w(g, par, last):
                pool.wait_ge(*w_hi_ready(g))
                pool.tensor_tensor(w_lo[:, par], w_raw[:, :], w_hi[:, par].bitcast(F32), ALU.subtract).then_inc(w_ready.sem, 1)

            def unit(i, g, pr, sub, par, size):
                if not swiglu:
                    return
                inc = GROUP // size
                pool.wait_ge(*g_loaded[sub](g * (NB // 2) + pr))
                for e in range(size):
                    pool.wait_ge(*silu_ready(i, (e + 1) * inc))
                    pool.tensor_tensor(act_gate[:, e % 2], act_gate[:, e % 2], gate[:, sub, e], ALU.mult)\
                        .then_inc(act_ready.sem, inc)

            split_w(0, 0, -1)
            pool.wait_ge(mixer_stored, 16)
            pool.memset(c.acc[:, :, :, :], 0.0).then_inc(cleared, 1)
            walk(pool, unit, split_w)


def route1(nc, c, logits, gates):
    TILES = P // E1
    with ExitStack() as ctx:
        s = Space(nc, ctx, "rt1")
        shifted = s.sb("shifted", [P, NT, E1])
        prob = s.sb("prob", [P, NT, E1 + 8])
        top8 = s.sb("top8", [P, NT, 8])
        pick = s.sb("pick", [P, NT, E1 + 8])
        weight = s.sb("weight", [P, NT, E1])
        stat = s.sb("stat", [P, NT])
        shared = s.sb("shared", [P, P])
        g_t = s.sb("g_t", [P, NT // TILES, P])
        turn_ps = s.ps("turn", [P, NT // TILES, P])
        shifted_ready, exp_ready, shared_ready, gates_ready, turned, g_t_ready, stored = (
            s.sem(n) for n in ("shifted_ready", "exp_ready", "shared_ready", "gates_ready", "turned", "g_t_ready", "stored"))
        steps = s.sem("dve_steps")
        block = ctx.enter_context(s.block())

        @block.scalar
        def _(act):
            act.preload_act_table_set("natural_log_exp_and_others")
            act.wait_ge(shifted_ready, 1)
            act.activation(weight[:, :, :], shifted[:, :, :], ACT.Exp).then_inc(exp_ready, 1)

        @block.gpsimd
        def _(pool):
            pool.memset(shared[:, :], 1.0 / (TOP1 + 1)).then_inc(shared_ready, 1)

        @block.vector
        def _(dve):
            link = Chain(dve, steps)

            def by_tile():
                return stat[:, :].unsqueeze(2).to_broadcast([P, NT, E1])

            link(dve.memset(prob[:, :, :], -1.0))
            link(dve.tensor_reduce(stat[:, :], logits[:, :, :], AX_X, ALU.max))
            dve.tensor_tensor(shifted[:, :, :], logits[:, :, :], by_tile(), ALU.subtract).then_inc(shifted_ready, 1)
            dve.wait_ge(exp_ready, 1)
            link(dve.tensor_reduce(stat[:, :], weight[:, :, :], AX_X, ALU.add))
            link(dve.reciprocal(stat[:, :], stat[:, :]))
            link(dve.tensor_tensor(prob[:, :, 0:E1], weight[:, :, :], by_tile(), ALU.mult))
            pick_top(dve, link, prob, E1, top8, pick, TOP1, weight[:, :, :])
            link(dve.tensor_tensor(weight[:, :, :], weight[:, :, :], prob[:, :, 0:E1], ALU.mult))
            link(dve.tensor_reduce(stat[:, :], weight[:, :, :], AX_X, ALU.add))
            link(dve.reciprocal(stat[:, :], stat[:, :]))
            link(dve.tensor_tensor(weight[:, :, :], weight[:, :, :], by_tile(), ALU.mult))
            dve.tensor_scalar(weight[:, :, :], weight[:, :, :], TOP1 / (TOP1 + 1), None, ALU.mult).then_inc(gates_ready, 1)
            dve.wait_ge(turned, 1)
            dve.tensor_copy(g_t[:, :, :], turn_ps[:, :, :]).then_inc(g_t_ready, 1)

        @block.tensor
        def _(pe):
            pe.wait_ge(gates_ready, 1)
            for n in range(NT // TILES):
                mm = pe.transpose(turn_ps[:, n], weight[:, n * TILES:(n + 1) * TILES].rearrange("p n e -> p (n e)"), c.ident[:, :])
            mm.then_inc(turned, 1)

        @block.sync
        def _(sp):
            sp.wait_ge(shared_ready, 1)
            sp.dma_start(gates[E1:E1 + SHARED1, :].rearrange("e (n t) -> (e n) t", t=P), shared[0:SHARED1 * NT, :])\
              .then_inc(stored, 16)
            sp.wait_ge(g_t_ready, 1)
            store_gates(sp, gates, g_t, E1, TILES, stored)
            sp.wait_ge(stored, 16 * (1 + TILES))


def mix(nc, c, w_mix, cols):
    U, V, G1, G2 = 0, 1, 2, 3
    with ExitStack() as ctx:
        s = Space(nc, ctx, "mix")
        w_raw = s.sb("w_raw", [P, W_MIX])
        w_hi = s.sb("w_hi", [P, W_MIX], F32R)
        w_lo = s.sb("w_lo", [P, W_MIX], F32R)
        col = s.sb("col", [P, COLS])
        ones = s.sb("ones", [P, T])
        hid = s.sb("hid", [P, T])
        hid_hi = s.sb("hid_hi", [P, T], F32R)
        hid_lo = s.sb("hid_lo", [P, T], F32R)
        gate = s.sb("gate", [P, KC, T])
        u = s.sb("u", [P, KC, T])
        v = s.sb("v", [P, KC, T])
        total = s.sb("total", [P, KC, T])
        prod = s.sb("prod", [P, KC, T])
        prod_hi = s.sb("prod_hi", [P, KC, T], F32R)
        prod_lo = s.sb("prod_lo", [P, KC, T], F32R)
        xn = s.sb("xn", [P, KC, T])
        conv = s.sb("conv", [P, 2, KC, T])
        u_ps = s.ps("u_ps", [P, KC, T])
        v_ps = s.ps("v_ps", [P, KC, T])
        g_ps = s.ps("g_ps", [P, 2, T])
        out_ps = s.ps("out", [P, KC, T])
        w_loaded, w_hi_ready, w_ready, col_loaded, ones_ready = (
            s.sem(n) for n in ("w_loaded", "w_hi_ready", "w_ready", "col_loaded", "ones_ready"))
        hid_proj = s.steps("hid_proj", 1)
        uv_proj = s.steps("uv_proj", 2)
        relu_ready = s.steps("relu_ready", 1)
        hid_hi_ready = s.steps("hid_hi_ready", 1)
        hid_split = s.steps("hid_split", 1)
        gate_proj = s.steps("gate_proj", KC)
        gate_ready = s.steps("gate_ready", KC)
        u_ready = s.steps("u_ready", KC)
        v_ready = s.steps("v_ready", KC)
        summed = s.steps("summed", KC)
        prod_ready = s.steps("prod_ready", KC)
        prod_hi_ready = s.steps("prod_hi_ready", KC)
        prod_split = s.steps("prod_split", KC)
        out_ready = s.steps("out_ready", KC)
        xn_ready = s.steps("xn_ready", KC)
        centre_ready = s.steps("centre_ready", KC)
        conv_ready = s.steps("conv_ready", 2 * KC)
        stored = s.steps("stored", KC)
        block = ctx.enter_context(s.block())

        def walk(engine, unit, end):
            unit(0, 0, None)
            with engine.Fori(0, NB // 2 - 1) as pair:
                for par in (1, 0):
                    i = pair * 2 + (2 - par)
                    unit(i, par, i - 1)
            unit(NB - 1, 1, NB - 2)
            end(NB - 1, 1)

        def w(which, k, chunk):
            return MIX_AT[which] + (k * KC + chunk) * P

        def cc(name, k):
            at = COL_AT[name] + k
            return col[:, at:at + 1]

        @block.sync
        def _(sp):
            sp.dma_start(w_raw[:, :], w_mix).then_inc(w_loaded, 16)
            sp.dma_start(col[:, :], cols).then_inc(col_loaded, 16)

        @block.tensor
        def _(pe):
            for counter in (hid_proj, uv_proj, gate_proj, out_ready):
                counter.prime(pe)
            pe.wait_ge(w_ready, 1)

            def project(out, i, at, step):
                for k in range(KC):
                    mm = product3(pe, out, w_hi[:, at + k * step:at + k * step + P], w_lo[:, at + k * step:at + k * step + P],
                                  c.xn_hi[:, i, k], c.xn_lo[:, i, k], k == 0, k == KC - 1)
                return mm

            def output(i):
                pe.wait_ge(*prod_split(i))
                pe.wait_ge(*stored(i - 1))
                for chunk in range(KC):
                    for k in range(KC):
                        at = w("u", k, chunk)
                        mm = product3(pe, out_ps[:, chunk], w_hi[:, at:at + P], w_lo[:, at:at + P],
                                      prod_hi[:, k], prod_lo[:, k], k == 0, k == KC - 1)
                    mm.then_inc(out_ready.sem, 1)

            def unit(i, par, prev):
                pe.wait_ge(*gate_ready(i - 1))
                project(g_ps[:, 0], i, MIX_AT["g1"], P).then_inc(hid_proj.sem, 1)
                pe.wait_ge(*u_ready(i - 1))
                pe.wait_ge(*v_ready(i - 1))
                for n, (name, out) in enumerate((("u", u_ps), ("v", v_ps))):
                    for chunk in range(KC):
                        mm = project(out[:, chunk], i, w(name, 0, chunk), KC * P)
                    mm.then_inc(uv_proj.sem, 1)
                    if n == 0:
                        pe.wait_ge(*hid_split(i))
                        for chunk in (1, 0):
                            at = MIX_AT["g2"] + chunk * P
                            product3(pe, g_ps[:, chunk], w_hi[:, at:at + P], w_lo[:, at:at + P], hid_hi[:, :], hid_lo[:, :],
                                     True, True).then_inc(gate_proj.sem, 1)
                if prev is not None:
                    output(prev)

            walk(pe, unit, lambda i, par: output(i))

        @block.scalar
        def _(act):
            for counter in (relu_ready, hid_hi_ready, gate_ready, prod_hi_ready, centre_ready):
                counter.prime(act)
            act.preload_act_table_set("sigmoid_and_others")
            act.wait_ge(w_loaded, 16)
            act.activation(w_hi[:, :], w_raw[:, :], ACT.Copy).then_inc(w_hi_ready, 1)
            act.wait_ge(col_loaded, 16)

            def prod_high(i):
                for k in range(KC):
                    act.wait_ge(*prod_ready(i, k + 1))
                    act.wait_ge(*out_ready(i - 1))
                    act.activation(prod_hi[:, k], prod[:, k], ACT.Copy).then_inc(prod_hi_ready.sem, 1)

            def unit(i, par, prev):
                act.wait_ge(*hid_proj(i))
                act.wait_ge(*hid_split(i - 1))
                act.activation(hid[:, :], g_ps[:, 0], ACT.Relu, bias=cc("bg1", 0)).then_inc(relu_ready.sem, 1)
                act.wait_ge(*relu_ready(i))
                act.wait_ge(*gate_proj(i - 1))
                act.activation(hid_hi[:, :], hid[:, :], ACT.Copy).then_inc(hid_hi_ready.sem, 1)
                if prev is not None:
                    prod_high(prev)
                for k in range(KC):
                    act.wait_ge(*xn_ready(i, k + 1))
                    act.wait_ge(*stored(i - 2))
                    act.activation(conv[:, par, k], xn[:, k], ACT.Identity, bias=cc("conv_b", k), scale=cc("conv1", k))\
                       .then_inc(centre_ready.sem, 1)
                for n, chunk in enumerate((1, 0)):
                    act.wait_ge(*gate_proj(i, n + 1))
                    act.wait_ge(*u_ready(i - 1))
                    act.wait_ge(*v_ready(i - 1))
                    act.activation(gate[:, chunk], g_ps[:, chunk], ACT.Sigmoid, bias=cc("bg2", chunk)).then_inc(gate_ready.sem, 1)

            walk(act, unit, lambda i, par: prod_high(i))

        @block.vector
        def _(dve):
            for counter in (u_ready, v_ready, summed, conv_ready, stored):
                counter.prime(dve)
            dve.memset(ones[:, :], 1.0).then_inc(ones_ready, 1)
            dve.wait_ge(ones_ready, 1)
            dve.wait_ge(col_loaded, 16)

            def store(i, par):
                for k in range(KC):
                    dve.wait_ge(*out_ready(i, k + 1))
                    dve.tensor_tensor(c.acc[:, i, k], conv[:, par, k], out_ps[:, k], ALU.add).then_inc(stored.sem, 1)

            def unit(i, par, prev):
                for k in range(KC):
                    dve.wait_ge(*centre_ready(i, k + 1))
                    dve.scalar_tensor_tensor(out=conv[:, par, k, 1:T], in0=xn[:, k, 0:T - 1], scalar=cc("conv0", k),
                                             in1=conv[:, par, k, 1:T], op0=ALU.mult, op1=ALU.add).then_inc(conv_ready.sem, 1)
                for k in range(KC):
                    dve.wait_ge(*conv_ready(i, k + 1))
                    dve.scalar_tensor_tensor(out=conv[:, par, k, 0:T - 1], in0=xn[:, k, 1:T], scalar=cc("conv2", k),
                                             in1=conv[:, par, k, 0:T - 1], op0=ALU.mult, op1=ALU.add).then_inc(conv_ready.sem, 1)
                dve.wait_ge(*conv_ready(i))
                dve.wait_ge(*gate_ready(i))
                dve.wait_ge(*uv_proj(i, 1))
                for k in range(KC):
                    dve.scalar_tensor_tensor(out=u[:, k], in0=u_ps[:, k], scalar=cc("bu", k), in1=gate[:, k],
                                             op0=ALU.add, op1=ALU.mult).then_inc(u_ready.sem, 1)
                dve.wait_ge(*uv_proj(i))
                dve.wait_ge(*prod_ready(i - 1))
                for k in range(KC):
                    dve.scalar_tensor_tensor(out=v[:, k], in0=v_ps[:, k], scalar=cc("bv", k), in1=gate[:, k],
                                             op0=ALU.add, op1=ALU.mult).then_inc(v_ready.sem, 1)
                for k in range(KC):
                    dve.wait_ge(*u_ready(i, k + 1))
                    dve.tensor_tensor_scan(total[:, k], ones[:, :], u[:, k], 0.0, ALU.mult, ALU.add).then_inc(summed.sem, 1)
                if prev is not None:
                    store(prev, 1 - par)

            walk(dve, unit, store)

        @block.gpsimd
        def _(pool):
            for counter in (hid_split, xn_ready, prod_ready, prod_split):
                counter.prime(pool)
            pool.wait_ge(w_hi_ready, 1)
            pool.tensor_tensor(w_lo[:, :], w_raw[:, :], w_hi[:, :].bitcast(F32), ALU.subtract).then_inc(w_ready, 1)

            def prod_low(i):
                for k in range(KC):
                    pool.wait_ge(*prod_hi_ready(i, k + 1))
                    pool.tensor_tensor(prod_lo[:, k], prod[:, k], prod_hi[:, k].bitcast(F32), ALU.subtract)\
                        .then_inc(prod_split.sem, 1)

            def unit(i, par, prev):
                pool.wait_ge(*hid_hi_ready(i))
                pool.tensor_tensor(hid_lo[:, :], hid[:, :], hid_hi[:, :].bitcast(F32), ALU.subtract).then_inc(hid_split.sem, 1)
                if prev is not None:
                    prod_low(prev)
                for k in range(KC):
                    pool.wait_ge(*conv_ready(i - 1))
                    pool.tensor_tensor(xn[:, k], c.xn_hi[:, i, k].bitcast(F32), c.xn_lo[:, i, k].bitcast(F32), ALU.add)\
                        .then_inc(xn_ready.sem, 1)
                for k in range(KC):
                    pool.wait_ge(*summed(i, k + 1))
                    pool.wait_ge(*v_ready(i, k + 1))
                    pool.wait_ge(*prod_split(i - 1))
                    pool.tensor_tensor(prod[:, k], total[:, k], v[:, k], ALU.mult).then_inc(prod_ready.sem, 1)

            walk(pool, unit, lambda i, par: prod_low(i))


def finish(nc, c, x1, mixer, out):
    with ExitStack() as ctx:
        s = Space(nc, ctx, "fin")
        x = s.sb("x", [P, 2, KC, T])
        m = s.sb("m", [P, 2, KC, T])
        act_ffn = s.sb("act_ffn", [P, 2, KC, T])
        x_loaded = [s.steps(f"x_loaded{q}", 16) for q in range(2)]
        m_loaded = [s.steps(f"m_loaded{q}", 16) for q in range(2)]
        stored = [s.steps(f"stored{q}", 16) for q in range(2)]
        silu_ready = s.steps("silu_ready", 1)
        gated = s.steps("gated", 1)
        summed = s.steps("summed", 1)
        block = ctx.enter_context(s.block())

        def rows(engine):
            with engine.Fori(0, NB // 2) as pair:
                for par in range(2):
                    yield pair, par, pair * 2 + par

        @block.sync
        def _(sp):
            for q in x_loaded + m_loaded:
                q.prime(sp)
            for pair, par, i in rows(sp):
                sp.wait_ge(*stored[par](pair - 1))
                sp.dma_start(x[:, par], x1[i]).then_inc(x_loaded[par].sem, 16)
                sp.dma_start(m[:, par], mixer[i]).then_inc(m_loaded[par].sem, 16)

        @block.scalar
        def _(act):
            silu_ready.prime(act)
            for q in stored:
                q.prime(act)
            act.preload_act_table_set("silu_and_others")
            for pair, par, i in rows(act):
                act.wait_ge(*gated(i - 2))
                act.activation(act_ffn[:, par], c.acc[:, i], ACT.Silu).then_inc(silu_ready.sem, 1)
                act.wait_ge(*summed(i))
                act.dma_start(out[i], x[:, par]).then_inc(stored[par].sem, 16)
            for q in stored:
                act.wait_ge(*q(NB // 2 - 1))

        @block.vector
        def _(dve):
            gated.prime(dve)
            summed.prime(dve)
            for pair, par, i in rows(dve):
                dve.wait_ge(*silu_ready(i))
                dve.wait_ge(*m_loaded[par](pair))
                dve.tensor_tensor(act_ffn[:, par], act_ffn[:, par], m[:, par], ALU.mult).then_inc(gated.sem, 1)
                dve.wait_ge(*gated(i))
                dve.wait_ge(*x_loaded[par](pair))
                dve.tensor_tensor(x[:, par], x[:, par], act_ffn[:, par], ALU.add).then_inc(summed.sem, 1)


def program(nc, a, out):
    with ExitStack() as ctx:
        s = Space(nc, ctx, "all")

        class c:
            mean = s.sb("mean", [P, P])
            ones = s.sb("ones", [P, P])
            ones_r = s.sb("ones_r", [P, P], F32R)
            ident = s.sb("ident", [P, P])
            upto = s.sb("upto", [P, P])
            eps_ln = s.sb("eps_ln", [P, 1])
            eps_norm = s.sb("eps_norm", [P, 1])
            neg_g = s.sb("neg_g", [P, NB * HKV * TT])
            xn_hi = s.sb("xn_hi", [P, NB, KC, T], F32R)
            xn_lo = s.sb("xn_lo", [P, NB, KC, T], F32R)
            acc = s.sb("acc", [P, NB, KC, T])

        constants(nc, c)
        g_rows = nc.dram_tensor("g_rows", (NB * HKV, T), F32).ap()
        gates0 = nc.dram_tensor("gates0", (E0 + SHARED0, NB * T), F32).ap()
        with ExitStack() as c2:
            logits = Space(nc, c2, "l0").sb("logits", [P, NT, LOG0])
            layernorm(nc, c, "ln0", a["rw0"], LOG0, logits, a["x"])
            decay_logs(nc, c, logits, g_rows)
            route0(nc, c, logits, a["br0"], gates0)
        attention(nc, c, a["w_att"], g_rows)
        mixer0 = nc.dram_tensor("mixer0", (NB, P, KC, T), F32).ap()
        experts(nc, c, "moe0", a["w_e0"], gates0, E0 // GROUP, SHARED0, False, mixer0)
        x1 = nc.dram_tensor("x1", (NB, P, KC, T), F32).ap()
        mixer1 = nc.dram_tensor("mixer1", (NB, P, KC, T), F32).ap()
        gates1 = nc.dram_tensor("gates1", (E1 + SHARED1, NB * T), F32).ap()

        class combine:
            mixer, bias, x_out = mixer0, a["bc0"], x1

        with ExitStack() as c2:
            logits = Space(nc, c2, "l1").sb("logits", [P, NT, E1])
            layernorm(nc, c, "ln1", a["rw1"], E1, logits, a["x"], combine)
            route1(nc, c, logits, gates1)
        mix(nc, c, a["w_mix"], a["cols"])
        experts(nc, c, "moe1", a["w_e1"], gates1, (E1 + SHARED1 - 1) // GROUP, GROUP, True, mixer1)
        finish(nc, c, x1, mixer1, out)


def by_chunk(w):
    import numpy as np
    return np.ascontiguousarray(w.reshape(KC, P, -1).transpose(1, 0, 2))


def lay_out(v):
    import numpy as np

    f = {n: np.asarray(x) for n, x in v.items()}
    a = {"x": np.ascontiguousarray(f["L0_attn_hidden_states"].reshape(NB, T, KC, P).transpose(0, 3, 2, 1))}
    a["rw0"] = by_chunk(np.concatenate([f["L0_ffn_Wr"].T, f["L0_attn_Wg"]], 1))
    a["br0"] = f["L0_ffn_br"][None]
    heads = [by_chunk(f[n]).reshape(P, KC, HKV, -1) for n in ("L0_attn_Wq", "L0_attn_Wk", "L0_attn_Wv")]
    w = np.zeros((HKV + 1, P, W_ATT), np.float32)
    w[:HKV, :, :KC * QKV] = np.concatenate(heads, 3).transpose(2, 0, 1, 3).reshape(HKV, P, KC * QKV)
    w[:HKV, :, KC * QKV:] = f["L0_attn_Wc"].reshape(HKV, REP, DH, D).transpose(0, 2, 1, 3).reshape(HKV, P, REP * D)
    a["w_att"] = w
    a["bc0"] = by_chunk(f["L0_attn_bc"][:, None])[:, :, 0].copy()

    def groups(parts, n):
        e = np.concatenate(parts, 2)
        g = np.zeros((n * GROUP, P, e.shape[2]), np.float32)
        g[:len(e)] = e
        return np.ascontiguousarray(g.reshape(n, GROUP, P, -1).transpose(0, 2, 1, 3).reshape(n, P, -1))

    def inward(w):
        return w.reshape(-1, P, KC, P).transpose(0, 3, 2, 1).reshape(-1, P, D)

    w1 = np.concatenate([f["L0_ffn_W1"], f["L0_ffn_Ws1"].reshape(SHARED0, P, D)])
    w2 = np.concatenate([f["L0_ffn_W2"].transpose(0, 2, 1), f["L0_ffn_Ws2"].T.reshape(SHARED0, P, D)])
    a["w_e0"] = groups([inward(w1), w2], (E0 + SHARED0 + GROUP - 1) // GROUP)
    a["rw1"] = by_chunk(f["L1_ffn_w_router"])
    ins = [np.concatenate([f[e].transpose(0, 2, 1), f[sh].T.reshape(SHARED1, P, D)])
           for e, sh in (("L1_ffn_we1", "L1_ffn_ws1"), ("L1_ffn_we3", "L1_ffn_ws3"))]
    w2 = np.concatenate([f["L1_ffn_we2"], f["L1_ffn_ws2"].reshape(SHARED1, P, D)])
    a["w_e1"] = groups([inward(ins[0]), inward(ins[1]), w2], (E1 + SHARED1) // GROUP)
    m = np.zeros((P, W_MIX), np.float32)
    m[:, MIX_AT["u"]:MIX_AT["v"]] = by_chunk(f["L1_attn_Wu"].T).reshape(P, -1)
    m[:, MIX_AT["v"]:MIX_AT["g1"]] = by_chunk(f["L1_attn_Wv"].T).reshape(P, -1)
    for k in range(KC):
        at = MIX_AT["g1"] + k * P
        m[:, at:at + DG] = f["L1_attn_Wg1"].T[k * P:(k + 1) * P]
    m[:DG, MIX_AT["g2"]:] = f["L1_attn_Wg2"].T
    a["w_mix"] = m
    cols = np.zeros((P, COLS), np.float32)
    for name, x in (("bu", "L1_attn_bu"), ("bv", "L1_attn_bv"), ("bg2", "L1_attn_bg2"), ("conv_b", "L1_attn_conv_b")):
        cols[:, COL_AT[name]:COL_AT[name] + KC] = f[x].reshape(KC, P).T
    cols[:DG, COL_AT["bg1"]] = f["L1_attn_bg1"]
    for tap in range(3):
        cols[:, COL_AT[f"conv{tap}"]:COL_AT[f"conv{tap}"] + KC] = f["L1_attn_conv_w"][:, 0, tap].reshape(KC, P).T
    a["cols"] = cols
    return a


def kernel(**inputs):
    import numpy as np
    from concourse import bacc
    from concourse.bass_utils import run_bass_kernel_spmd as run

    arrays = lay_out(inputs)
    nc = bacc.Bacc("TRN2", target_bir_lowering=False, num_devices=1)
    a = {n: nc.dram_tensor(f"in_{n}", x.shape, mybir.dt.from_np(x.dtype), kind="ExternalInput").ap() for n, x in arrays.items()}
    out = nc.dram_tensor("out", (NB, P, KC, T), F32, kind="ExternalOutput").ap()
    program(nc, a, out)
    r = run(nc, [{f"in_{n}": x for n, x in arrays.items()}], core_ids=[0])
    return np.ascontiguousarray(r.results[0]["out"].transpose(0, 3, 2, 1)).reshape(NB, T, D)
```

```python
from contextlib import ExitStack, contextmanager

import concourse.bass as bass
from concourse import mybir

F32 = mybir.dt.float32
F32R = mybir.dt.float32r
ALU = mybir.AluOpType
ACT = mybir.ActivationFunctionType
AX_X = mybir.AxisListType.X

P = 128
NB, T, D = 8, 512, 256
KC = D // P
TT = T // P
NT = NB * TT
HKV, REP, DH = 8, 2, 128
E0, TOP0, G0, TOPG0 = 32, 6, 8, 4
SHARED0 = 2
SCALE0 = 2.5
E1, TOP1 = 16, 4
SHARED1 = 4
LOG0 = E0 + HKV
EPS_LN = 1e-5
EPS_NORM = 1e-6
GATE_OFFSET = 6.906768
QKV = (REP + 2) * DH
W_USED = KC * QKV + REP * D
W_SLICE = 2 * -(-W_USED // (2 * (NB - 2)))
W_ATT = W_SLICE * (NB - 2)
W_E0 = KC * P + D
W_E1 = 2 * KC * P + D
DG = D // 4
MIX_AT = {"u": 0, "v": KC * D, "g1": 2 * KC * D, "g2": 2 * KC * D + KC * P}
W_MIX = 2 * KC * D + KC * P + D
COL_AT = {"bu": 0, "bv": 2, "bg1": 4, "bg2": 5, "conv0": 7, "conv1": 9, "conv2": 11, "conv_b": 13}
COLS = 15
GROUP = 4
CHUNKS = [(0, 0, 512), (1, 512, 384), (3, 896, 128), (2, 1024, 256)]
BANKS = [(0, 512), (512, 1024), (1024, 1280)]
CAUSAL = 1280


def w_slice(w_expert):
    return 2 * -(-GROUP * w_expert // (2 * (NB - 2)))


class Steps:

    def __init__(self, sem, per):
        self.sem, self.per = sem, per

    def prime(self, engine, left=0):
        engine.sem_inc(self.sem, 2 * self.per - left)

    def __call__(self, i, k=None):
        return self.sem, i * self.per + (2 * self.per + (self.per if k is None else k))


class Space:

    def __init__(self, nc, ctx, tag):
        self.nc, self.ctx, self.tag, self.sems = nc, ctx, tag, []

    def sb(self, name, shape, dt=F32):
        return self.ctx.enter_context(self.nc.sbuf_tensor(f"{self.tag}_{name}", shape, dt))

    def ps(self, name, shape):
        return self.ctx.enter_context(self.nc.psum_tensor(f"{self.tag}_{name}", shape, F32))

    def sem(self, name):
        self.sems.append(self.ctx.enter_context(self.nc.semaphore(f"{self.tag}_{name}")))
        return self.sems[-1]

    @contextmanager
    def block(self):
        with self.nc.Block() as block:
            yield block
        for sem in self.sems:
            self.nc.gpsimd.sem_clear(sem)

    def steps(self, name, per):
        return Steps(self.sem(name), per)


def product3(pe, out, w_hi, w_lo, x_hi, x_lo, first, last):
    pe.matmul(out, w_hi, x_hi, start=first, stop=False)
    pe.matmul(out, w_lo, x_hi, start=False, stop=False)
    return pe.matmul(out, w_hi, x_lo, start=False, stop=last)


def constants(nc, c):
    with ExitStack() as ctx:
        s = Space(nc, ctx, "cst")
        filled, shaped = s.sem("filled"), s.sem("shaped")
        block = ctx.enter_context(s.block())

        @block.gpsimd
        def _(pool):
            pool.memset(c.mean[:, :], 1.0 / D)
            pool.memset(c.ones[:, :], 1.0)
            pool.memset(c.ones_r[:, :].bitcast(F32), 1.0)
            pool.memset(c.eps_ln[:, :], EPS_LN)
            pool.memset(c.eps_norm[:, :], EPS_NORM)
            pool.memset(c.ident[:, :], 0.0).then_inc(filled, 1)
            pool.memset(c.upto[:, :], 1.0).then_inc(filled, 1)
            pool.wait_ge(filled, 2)
            pool.affine_select(out=c.ident[:, :], in_=c.ident[:, :], compare_op=ALU.not_equal, fill=1.0,
                               base=0, pattern=[[-1, P]], channel_multiplier=1).then_inc(shaped, 1)
            pool.affine_select(out=c.upto[:, :], in_=c.upto[:, :], compare_op=ALU.is_ge, fill=0.0,
                               base=0, pattern=[[1, P]], channel_multiplier=-1).then_inc(shaped, 1)
            pool.wait_ge(shaped, 2)


def layernorm(nc, c, tag, rw_dram, n_log, logits, x_dram, combine=None):
    with ExitStack() as ctx:
        s = Space(nc, ctx, tag)
        x = s.sb("x", [P, 2, KC, T])
        xc = s.sb("xc", [P, 2, KC, T])
        sq = s.sb("sq", [P, 2, KC, T])
        xn = s.sb("xn", [P, 2, KC, T])
        rstd = s.sb("rstd", [P, 2, T])
        newt = s.sb("newt", [P, T])
        lgt = s.sb("lgt", [P, 2, T])
        rw = s.sb("rw", [P, KC, P])
        rw_hi = s.sb("rw_hi", [P, KC, P], F32R)
        rw_lo = s.sb("rw_lo", [P, KC, P], F32R)
        mean_ps = s.ps("mean", [P, 2, T])
        var_ps = s.ps("var", [P, 2, T])
        log_ps = s.ps("log", [P, 2, T])
        tok_ps = s.ps("tok", [P, 2, T])
        rw_cleared, rw_loaded, rw_split = s.sem("rw_cleared"), s.sem("rw_loaded"), s.sem("rw_split")
        x_loaded = [s.steps(f"x_loaded{q}", 16) for q in range(2)]
        mean_ready = s.steps("mean_ready", 1)
        centred = s.steps("centred", KC)
        squared = s.steps("squared", KC)
        var_ready = s.steps("var_ready", 1)
        ln_var = s.steps("ln_var", 1)
        rstd_raw = s.steps("rstd_raw", 1)
        newton = s.steps("newton", 4)
        normed = s.steps("normed", KC)
        hi_ready = s.steps("hi_ready", KC)
        lo_ready = s.steps("lo_ready", KC)
        log_ready = s.steps("log_ready", 1)
        log_out = s.steps("log_out", 1)
        tok_ready = s.steps("tok_ready", 1)
        tok_out = s.steps("tok_out", 1)
        if combine:
            mixer = s.sb("mixer", [P, 2, KC, T])
            bias = s.sb("bias", [P, KC])
            bias_loaded = s.sem("bias_loaded")
            mixer_loaded = [s.steps(f"mixer_loaded{q}", 16) for q in range(2)]
            silu_ready = s.steps("silu_ready", 1)
            gated = s.steps("gated", KC)
            x_ready = s.steps("x_ready", KC)
            x_stored = [s.steps(f"x_stored{q}", 16) for q in range(2)]
        block = ctx.enter_context(s.block())

        def x_there(i, pair, par):
            return x_ready(i) if combine else x_loaded[par](pair)

        def walk(engine, first, second=None, third=None, peel_last=False):
            def step(row):
                first(*row(0))
                if second:
                    second(*row(1))
                if third:
                    third(*row(2))

            first(0, 0, 0)
            first(1, 0, 1)
            if second:
                second(0, 0, 0)
            with engine.Fori(1, NB // 2 - (1 if peel_last else 0)) as pair:
                for par in range(2):
                    step(lambda d: (pair * 2 + (par - d), pair - (1 if d > par else 0), (par + d) % 2))
            if peel_last:
                for i in (NB - 2, NB - 1):
                    step(lambda d: (i - d, (i - d) // 2, (i - d) % 2))
            if second:
                second(NB - 1, NB // 2 - 1, 1)
            if third:
                third(NB - 2, NB // 2 - 1, 0)
                third(NB - 1, NB // 2 - 1, 1)

        @block.sync
        def _(sp):
            [q.prime(sp) for q in x_loaded]
            if combine:
                [q.prime(sp) for q in mixer_loaded]

            def load(i, pair, par):
                if combine:
                    sp.wait_ge(*gated(i - 2))
                    sp.wait_ge(*x_ready(i - 2))
                    sp.dma_start(mixer[:, par], combine.mixer[i]).then_inc(mixer_loaded[par].sem, 16)
                    sp.wait_ge(*x_stored[par](pair - 1))
                sp.wait_ge(*centred(i - 2))
                sp.dma_start(x[:, par], x_dram[i]).then_inc(x_loaded[par].sem, 16)

            if combine:
                sp.dma_start(bias[:, :], combine.bias).then_inc(bias_loaded, 16)
            sp.wait_ge(rw_cleared, 1)
            sp.dma_start(rw[:, :, 0:n_log], rw_dram).then_inc(rw_loaded, 16)
            walk(sp, load)
            if combine:
                for q in x_stored:
                    sp.wait_ge(*q(NB // 2 - 1))

        @block.tensor
        def _(pe):
            for counter in (mean_ready, var_ready, log_ready, tok_ready):
                counter.prime(pe)

            def mean(i, pair, par):
                pe.wait_ge(*x_there(i, pair, par))
                pe.wait_ge(*centred(i - 2))
                for k in range(KC):
                    mm = pe.matmul(mean_ps[:, par], c.mean[:, :], x[:, par, k], start=(k == 0), stop=(k == KC - 1))
                mm.then_inc(mean_ready.sem, 1)

            def variance(i, pair, par):
                pe.wait_ge(*squared(i))
                pe.wait_ge(*newton(i - 2))
                for k in range(KC):
                    mm = pe.matmul(var_ps[:, par], c.mean[:, :], sq[:, par, k], start=(k == 0), stop=(k == KC - 1))
                mm.then_inc(var_ready.sem, 1)

            def log_product(i, pair, par):
                pe.wait_ge(rw_split, 2)
                pe.wait_ge(*hi_ready(i))
                pe.wait_ge(*lo_ready(i))
                pe.wait_ge(*log_out(i - 2))
                for k in range(KC):
                    mm = product3(pe, log_ps[:, par], rw_hi[:, k], rw_lo[:, k], c.xn_hi[:, i, k], c.xn_lo[:, i, k],
                                  k == 0, k == KC - 1)
                mm.then_inc(log_ready.sem, 1)
                pe.wait_ge(*log_out(i))
                pe.wait_ge(*tok_out(i - 2))
                for j in range(TT):
                    mm = pe.transpose(tok_ps[:, par, j * P:(j + 1) * P], lgt[:, par, j * P:(j + 1) * P], c.ident[:, :])
                mm.then_inc(tok_ready.sem, 1)

            walk(pe, mean, variance, log_product)

        @block.vector
        def _(dve):
            for counter in (centred, newton, normed, tok_out):
                counter.prime(dve)
            dve.wait_ge(rw_split, 1)
            dve.tensor_tensor(rw_lo[:, :, :], rw[:, :, :], rw_hi[:, :, :].bitcast(F32), ALU.subtract).then_inc(rw_split, 1)
            if combine:
                gated.prime(dve)
                dve.wait_ge(bias_loaded, 16)

            def gate(i, pair, par):
                dve.wait_ge(*mixer_loaded[par](pair))
                dve.wait_ge(*silu_ready(i))
                for k in range(KC):
                    dve.scalar_tensor_tensor(out=mixer[:, par, k], in0=mixer[:, par, k], scalar=bias[:, k:k + 1],
                                             in1=c.acc[:, i, k], op0=ALU.add, op1=ALU.mult).then_inc(gated.sem, 1)

            def centre(i, pair, par):
                dve.wait_ge(*x_there(i, pair, par))
                dve.wait_ge(*mean_ready(i))
                dve.wait_ge(*squared(i - 2))
                dve.wait_ge(*normed(i - 2))
                for k in range(KC):
                    dve.tensor_tensor(xc[:, par, k], x[:, par, k], mean_ps[:, par], ALU.subtract).then_inc(centred.sem, 1)

            def norm(i, pair, par):
                dve.wait_ge(*rstd_raw(i))
                dve.wait_ge(*newton(i - 1))
                dve.tensor_tensor(newt[:, :], rstd[:, par], rstd[:, par], ALU.mult).then_inc(newton.sem, 1)
                dve.wait_ge(*newton(i, 1))
                dve.scalar_tensor_tensor(out=newt[:, :], in0=var_ps[:, par], scalar=EPS_LN, in1=newt[:, :],
                                         op0=ALU.add, op1=ALU.mult).then_inc(newton.sem, 1)
                dve.wait_ge(*newton(i, 2))
                dve.tensor_scalar(newt[:, :], newt[:, :], -0.5, 1.5, ALU.mult, ALU.add).then_inc(newton.sem, 1)
                dve.wait_ge(*newton(i, 3))
                dve.tensor_tensor(rstd[:, par], rstd[:, par], newt[:, :], ALU.mult).then_inc(newton.sem, 1)
                dve.wait_ge(*newton(i))
                dve.wait_ge(*hi_ready(i - 2))
                dve.wait_ge(*lo_ready(i - 2))
                for k in range(KC):
                    dve.tensor_tensor(xn[:, par, k], xc[:, par, k], rstd[:, par], ALU.mult).then_inc(normed.sem, 1)

            def take_logits(i, pair, par):
                dve.wait_ge(*tok_ready(i))
                dve.tensor_copy(logits[:, bass.ds(i * TT, TT), :],
                                tok_ps[:, par].rearrange("p (j n) -> p j n", j=TT)[:, :, 0:n_log])\
                   .then_inc(tok_out.sem, 1)

            if not combine:
                walk(dve, centre, norm, take_logits)
            else:
                gate(0, 0, 0)

                def centre_and_gate(i, pair, par):
                    last = isinstance(i, int) and i == NB - 1
                    if not last:
                        gate(i + 1, pair + par, 1 - par)
                    centre(i, pair, par)

                walk(dve, centre_and_gate, norm, take_logits, peel_last=True)

        @block.scalar
        def _(act):
            for counter in (squared, ln_var, rstd_raw, hi_ready, log_out):
                counter.prime(act)
            if combine:
                silu_ready.prime(act)
                [q.prime(act) for q in x_stored]
                act.preload_act_table_set("silu_and_others")
            act.wait_ge(rw_loaded, 16)
            act.activation(rw_hi[:, :, :], rw[:, :, :], ACT.Copy).then_inc(rw_split, 1)
            if combine:
                with act.Fori(0, NB) as i:
                    act.activation(c.acc[:, i], c.acc[:, i], ACT.Silu).then_inc(silu_ready.sem, 1)
            act.preload_act_table_set("natural_log_exp_and_others")

            def square(i, pair, par):
                if combine:
                    act.wait_ge(*x_ready(i))
                    act.dma_start(combine.x_out[i], x[:, par]).then_inc(x_stored[par].sem, 16)
                act.wait_ge(*var_ready(i - 2))
                for k in range(KC):
                    act.wait_ge(*centred(i, k + 1))
                    act.activation(sq[:, par, k], xc[:, par, k], ACT.Square).then_inc(squared.sem, 1)

            def high(i, pair, par):
                act.wait_ge(*var_ready(i))
                act.wait_ge(*normed(i - 2))
                act.activation(rstd[:, par], var_ps[:, par], ACT.Ln, bias=c.eps_ln[:, :]).then_inc(ln_var.sem, 1)
                act.wait_ge(*ln_var(i))
                act.activation(rstd[:, par], rstd[:, par], ACT.Exp, scale=-0.5).then_inc(rstd_raw.sem, 1)
                for k in range(KC):
                    act.wait_ge(*normed(i, k + 1))
                    act.activation(c.xn_hi[:, i, k], xn[:, par, k], ACT.Copy).then_inc(hi_ready.sem, 1)

            def copy_logits(i, pair, par):
                act.wait_ge(*log_ready(i))
                act.wait_ge(*tok_ready(i - 2))
                act.activation(lgt[:, par], log_ps[:, par], ACT.Copy).then_inc(log_out.sem, 1)

            walk(act, square, high, copy_logits)

        @block.gpsimd
        def _(pool):
            lo_ready.prime(pool)
            pool.memset(rw[:, :, :], 0.0).then_inc(rw_cleared, 1)
            if combine:
                x_ready.prime(pool)

            def add_x(i, pair, par):
                if combine:
                    pool.wait_ge(*x_loaded[par](pair))
                    for k in range(KC):
                        pool.wait_ge(*gated(i, k + 1))
                        pool.tensor_tensor(x[:, par, k], x[:, par, k], mixer[:, par, k], ALU.add).then_inc(x_ready.sem, 1)

            def low(i, pair, par):
                for k in range(KC):
                    pool.wait_ge(*hi_ready(i, k + 1))
                    pool.tensor_tensor(c.xn_lo[:, i, k], xn[:, par, k], c.xn_hi[:, i, k].bitcast(F32), ALU.subtract)\
                        .then_inc(lo_ready.sem, 1)

            walk(pool, add_x, low)


class Chain:

    def __init__(self, engine, sem):
        self.engine, self.sem, self.n = engine, sem, 0

    def __call__(self, instruction):
        self.n += 1
        instruction.then_inc(self.sem, 1)
        self.engine.wait_ge(self.sem, self.n)
        return self.n


def decay_logs(nc, c, logits, g_rows):
    with ExitStack() as ctx:
        s = Space(nc, ctx, "dec")
        N = NT * HKV
        z, absz, u, den, ratio, q, poly, logg = (s.sb(n, [P, N]) for n in ("z", "absz", "u", "den", "ratio", "q", "poly", "logg"))
        total = s.sb("total", [P, NB, TT, HKV])
        before = s.sb("before", [P, NB, TT, HKV])
        g = s.sb("g", [P, NB, HKV, TT])
        g_t = s.sb("g_t", [P, 2, P])
        cum_ps = s.ps("cum", [P, NB, TT, HKV])
        tot_ps = s.ps("tot", [P, NB, TT, HKV])
        turn_ps = s.ps("turn", [P, 2, P])
        absz_ready, u_ready, log_ready, sums_ready, g_ready, turned, stored = (
            s.sem(n) for n in ("absz_ready", "u_ready", "log_ready", "sums_ready", "g_ready", "turned", "stored"))
        steps = s.sem("dve_steps")
        block = ctx.enter_context(s.block())

        @block.vector
        def _(dve):
            link = Chain(dve, steps)
            link(dve.tensor_scalar(z[:, :].rearrange("p (n h) -> p n h", h=HKV), logits[:, :, E0:LOG0],
                                   GATE_OFFSET, None, ALU.add))
            dve.scalar_tensor_tensor(out=absz[:, :], in0=z[:, :], scalar=-1.0, in1=z[:, :],
                                     op0=ALU.mult, op1=ALU.max).then_inc(absz_ready, 1)
            dve.wait_ge(u_ready, 1)
            link(dve.tensor_scalar(den[:, :], u[:, :], 2.0, None, ALU.add))
            link(dve.reciprocal(den[:, :], den[:, :]))
            link(dve.tensor_tensor(ratio[:, :], u[:, :], den[:, :], ALU.mult))
            link(dve.tensor_tensor(q[:, :], ratio[:, :], ratio[:, :], ALU.mult))
            link(dve.tensor_scalar(poly[:, :], q[:, :], 1.0 / 17.0, None, ALU.mult))
            for odd in (15, 13, 11, 9, 7, 5, 3):
                link(dve.scalar_tensor_tensor(out=poly[:, :], in0=poly[:, :], scalar=1.0 / odd, in1=q[:, :],
                                              op0=ALU.add, op1=ALU.mult))
            link(dve.scalar_tensor_tensor(out=poly[:, :], in0=poly[:, :], scalar=1.0, in1=ratio[:, :],
                                          op0=ALU.add, op1=ALU.mult))
            link(dve.tensor_scalar(z[:, :], z[:, :], 0.0, None, ALU.min))
            dve.scalar_tensor_tensor(out=logg[:, :], in0=poly[:, :], scalar=-2.0, in1=z[:, :],
                                     op0=ALU.mult, op1=ALU.add).then_inc(log_ready, 1)
            dve.wait_ge(sums_ready, 2)
            link(dve.memset(before[:, :, :, :], 0.0))
            link(dve.tensor_copy(total[:, :, :, :], tot_ps[:, :, :, :]))
            for j in range(1, TT):
                link(dve.tensor_tensor(before[:, :, j], before[:, :, j - 1], total[:, :, j - 1], ALU.add))
            link(dve.tensor_tensor(g[:, :, :, :].rearrange("p b h j -> p b j h"), cum_ps[:, :, :, :], before[:, :, :, :],
                                   ALU.add))
            dve.tensor_scalar(c.neg_g[:, :], g[:, :, :, :].rearrange("p b h j -> p (b h j)"), -1.0, None,
                              ALU.mult).then_inc(g_ready, 1)
            dve.wait_ge(turned, 1)
            dve.tensor_copy(g_t[:, :, :], turn_ps[:, :, :]).then_inc(g_ready, 1)

        @block.scalar
        def _(act):
            act.preload_act_table_set("natural_log_exp_and_others")
            act.wait_ge(absz_ready, 1)
            act.activation(u[:, :], absz[:, :], ACT.Exp, scale=-1.0).then_inc(u_ready, 1)

        @block.tensor
        def _(pe):
            pe.wait_ge(log_ready, 1)
            pe.matmul(cum_ps[:, :, :, :].rearrange("p b j h -> p (b j h)"), c.upto[:, :], logg[:, :],
                      start=True, stop=True).then_inc(sums_ready, 1)
            pe.matmul(tot_ps[:, :, :, :].rearrange("p b j h -> p (b j h)"), c.ones[:, :], logg[:, :],
                      start=True, stop=True).then_inc(sums_ready, 1)
            pe.wait_ge(g_ready, 1)
            for half in range(2):
                mm = pe.transpose(turn_ps[:, half], g[:, :, :, :].rearrange("p b h j -> p (b h j)")[:, half * P:(half + 1) * P],
                                  c.ident[:, :])
            mm.then_inc(turned, 1)

        @block.sync
        def _(sp):
            sp.wait_ge(g_ready, 2)
            sp.dma_start(g_rows.rearrange("r (j t) -> (r j) t", t=P).rearrange("(a p) t -> p a t", p=P), g_t[:, :, :])\
              .then_inc(stored, 16)
            sp.wait_ge(stored, 16)


def pick_top(dve, link, values, pad_at, top8, picked, k, is_picked):
    for n in range(NT):
        dve.max(top8[:, n], values[:, n, 0:pad_at]).then_inc(link.sem, 1)
    link.n += NT
    dve.wait_ge(link.sem, link.n)
    link(dve.memset(top8[:, :, k:8], -1.0))
    for n in range(NT):
        dve.match_replace(picked[:, n], top8[:, n], values[:, n], -2.0).then_inc(link.sem, 1)
    link.n += NT
    dve.wait_ge(link.sem, link.n)
    link(dve.tensor_scalar(is_picked, picked[:, :, 0:pad_at], -2.0, None, ALU.is_equal))


def store_gates(sp, gates, g_t, n_e, tiles, stored):
    to = gates[0:n_e, :].rearrange("e (g l t) -> l e g t", l=tiles, t=P)
    for tile in range(tiles):
        sp.dma_start(to[tile], g_t[tile * n_e:(tile + 1) * n_e]).then_inc(stored, 16)


def route0(nc, c, logits, bias_row, gates):
    with ExitStack() as ctx:
        s = Space(nc, ctx, "rt0")
        GS = E0 // G0
        bias = s.sb("bias", [P, E0])
        score = s.sb("score", [P, NT, E0])
        pair = s.sb("pair", [P, NT * G0, 6])
        group = s.sb("group", [P, NT, G0 + 8])
        top8 = s.sb("top8", [P, NT, 8])
        gpick = s.sb("gpick", [P, NT, G0 + 8])
        gmask = s.sb("gmask", [P, NT, G0])
        masked = s.sb("masked", [P, NT, E0 + 8])
        epick = s.sb("epick", [P, NT, E0 + 8])
        weight = s.sb("weight", [P, NT, E0])
        norm = s.sb("norm", [P, NT])
        g_t = s.sb("g_t", [P, NB, P])
        turn_ps = s.ps("turn", [P, NB, P])
        loaded, logit_ready, score_ready, gates_ready, turned, g_t_ready, stored = (
            s.sem(n) for n in ("loaded", "logit_ready", "score_ready", "gates_ready", "turned", "g_t_ready", "stored"))
        steps = s.sem("dve_steps")
        block = ctx.enter_context(s.block())

        @block.scalar
        def _(act):
            act.wait_ge(logit_ready, 1)
            act.activation(score[:, :, :], weight[:, :, :], ACT.Sigmoid).then_inc(score_ready, 1)

        @block.vector
        def _(dve):
            link = Chain(dve, steps)
            link(dve.memset(group[:, :, :], -1.0))
            link(dve.memset(masked[:, :, :], -1.0))
            dve.wait_ge(loaded, 16)
            dve.tensor_tensor(weight[:, :, :], logits[:, :, 0:E0], bias[:, :].unsqueeze(1).to_broadcast([P, NT, E0]),
                              ALU.add).then_inc(logit_ready, 1)
            dve.wait_ge(score_ready, 1)
            four = score[:, :, :].rearrange("p n (g e) -> p (n g) e", e=GS)
            link(dve.tensor_tensor(pair[:, :, 0:2], four[:, :, 0:2], four[:, :, 2:4], ALU.add))
            link(dve.tensor_tensor(pair[:, :, 2:4], four[:, :, 0:4:2], four[:, :, 1:4:2], ALU.add))
            link(dve.tensor_tensor(pair[:, :, 4:5], four[:, :, 0:1], four[:, :, 3:4], ALU.add))
            link(dve.tensor_tensor(pair[:, :, 5:6], four[:, :, 1:2], four[:, :, 2:3], ALU.add))
            link(dve.tensor_reduce(group[:, :, 0:G0], pair[:, :, :].rearrange("p (n g) e -> p n g e", g=G0), AX_X, ALU.max))
            pick_top(dve, link, group, G0, top8, gpick, TOPG0, gmask[:, :, :])
            link(dve.tensor_tensor(masked[:, :, 0:E0].rearrange("p n (g e) -> p n g e", e=GS),
                                   score[:, :, :].rearrange("p n (g e) -> p n g e", e=GS),
                                   gmask[:, :, :].unsqueeze(3).to_broadcast([P, NT, G0, GS]), ALU.mult))
            pick_top(dve, link, masked, E0, top8, epick, TOP0, weight[:, :, :])
            link(dve.tensor_tensor(weight[:, :, :], weight[:, :, :], score[:, :, :], ALU.mult))
            link(dve.tensor_reduce(norm[:, :], weight[:, :, :], AX_X, ALU.add))
            link(dve.tensor_scalar(norm[:, :], norm[:, :], 1e-20, None, ALU.add))
            link(dve.reciprocal(norm[:, :], norm[:, :]))
            link(dve.tensor_tensor(weight[:, :, :], weight[:, :, :], norm[:, :].unsqueeze(2).to_broadcast([P, NT, E0]), ALU.mult))
            dve.tensor_scalar(weight[:, :, :], weight[:, :, :], SCALE0, None, ALU.mult).then_inc(gates_ready, 1)
            dve.wait_ge(turned, 1)
            dve.tensor_copy(g_t[:, :, :], turn_ps[:, :, :]).then_inc(g_t_ready, 1)

        @block.tensor
        def _(pe):
            pe.wait_ge(gates_ready, 1)
            for b in range(NB):
                mm = pe.transpose(turn_ps[:, b], weight[:, b * TT:(b + 1) * TT].rearrange("p n e -> p (n e)"), c.ident[:, :])
            mm.then_inc(turned, 1)

        @block.sync
        def _(sp):
            sp.dma_start(bias[:, :], bias_row.to_broadcast([P, E0])).then_inc(loaded, 16)
            sp.dma_start(gates[E0:E0 + SHARED0, :].rearrange("e (n t) -> (e n) t", t=P), c.ones[0:SHARED0 * NT, :])\
              .then_inc(stored, 16)
            sp.wait_ge(g_t_ready, 1)
            store_gates(sp, gates, g_t, E0, TT, stored)
            sp.wait_ge(stored, 16 * (1 + TT))


def attention(nc, c, weights, g_rows):
    TILES = len(BANKS)
    with ExitStack() as ctx:
        s = Space(nc, ctx, "att")
        w_hi = s.sb("w_hi", [P, 2, W_ATT], F32R)
        w_lo = s.sb("w_lo", [P, 2, W_ATT], F32R)
        w_raw = s.sb("w_raw", [P, W_SLICE])
        qk_hi = s.sb("qk_hi", [P, REP + 1, T], F32R)
        qk_lo = s.sb("qk_lo", [P, REP + 1, T], F32R)
        v_feat = s.sb("v_feat", [P, T])
        v_hi = s.sb("v_hi", [P, T], F32R)
        v_lo = s.sb("v_lo", [P, T], F32R)
        g_all = s.sb("g_all", [P, T])
        decay = s.sb("decay", [P, CAUSAL])
        a = s.sb("a", [P, REP, CAUSAL])
        a_hi = s.sb("a_hi", [P, REP, CAUSAL], F32R)
        a_lo = s.sb("a_lo", [P, REP, CAUSAL], F32R)
        inv = s.sb("inv", [P, T])
        fix = s.sb("fix", [P, T])
        y = s.sb("y", [P, T])
        y_hi = s.sb("y_hi", [P, REP, T], F32R)
        y_lo = s.sb("y_lo", [P, REP, T], F32R)
        work_ps = s.ps("work", [P, 3, T])
        score_ps = s.ps("score", [P, 2, T])
        y_ps = s.ps("y_ps", [P, REP, T])
        norm_ps = s.ps("norm", [P, T])

        cleared, cleared_ps, mask_begun = s.sem("cleared"), s.sem("cleared_ps"), s.sem("mask_begun")
        w0_loaded, w0_hi_ready = s.sem("w0_loaded"), s.sem("w0_hi_ready")
        w_loaded = s.steps("w_loaded", 16 * (NB - 2))
        w_hi_ready = s.steps("w_hi_ready", NB - 2)
        w_ready = s.steps("w_ready", NB - 2)
        g_loaded = s.steps("g_loaded", 16)
        decay_raw = s.steps("decay_raw", 1)
        decay_ready = s.steps("decay_ready", 1)
        qk_proj = s.steps("qk_proj", REP + 1)
        qk_hi_ready = s.steps("qk_hi_ready", REP + 1)
        qk_ready = s.steps("qk_ready", REP + 1)
        v_proj = s.steps("v_proj", 1)
        v_copied = s.steps("v_copied", 1)
        v_turned = s.steps("v_turned", 1)
        v_hi_ready = s.steps("v_hi_ready", 1)
        v_ready = s.steps("v_ready", 1)
        scored = s.steps("scored", REP * TILES)
        squared = s.steps("squared", REP * TILES)
        decayed = s.steps("decayed", REP * TILES)
        a_hi_ready = s.steps("a_hi_ready", REP * TILES)
        a_ready = s.steps("a_ready", REP * TILES)
        summed = s.steps("summed", REP)
        logged = s.steps("logged", REP)
        inv_raw = s.steps("inv_raw", REP)
        fixed = s.steps("fixed", 3 * REP)
        y_hi_ready = s.steps("y_hi_ready", REP)
        y_ready = s.steps("y_ready", REP)
        mixed = s.steps("mixed", KC)
        added = s.steps("added", KC)
        block = ctx.enter_context(s.block())

        def col(w, par, part, k=0):
            at = {"q0": 0, "q1": DH, "k": REP * DH, "v": (REP + 1) * DH}
            if part in at:
                return w[:, par, k * QKV + at[part]:k * QKV + at[part] + DH]
            q, chunk = part
            at = KC * QKV + q * D + chunk * P
            return w[:, par, at:at + P]

        def walk(engine, unit):
            with engine.Fori(0, HKV // 2) as pair:
                for par in range(2):
                    i0 = pair * (2 * NB) + par * NB
                    unit(i0, 0, par, pair, (i0 + 1, 1, par), (i0 - 1, NB - 1, 1 - par))
                    with engine.Fori(1, NB - 1) as b:
                        unit(i0 + b, b, par, pair, (i0 + b + 1, b + 1, par), (i0 + b - 1, b - 1, par))
                    unit(i0 + (NB - 1), NB - 1, par, pair, (i0 + NB, 0, 1 - par), (i0 + (NB - 2), NB - 2, par))

        LAST = HKV * NB - 1

        def next_head(pair, par, nxt):
            return pair * 2 + (par + 1 if first_row(nxt[1]) else par)

        def first_row(b):
            return isinstance(b, int) and b == 0

        def middle(b):
            return not isinstance(b, int)

        @block.sync
        def _(sp):
            w_loaded.prime(sp, left=-16 * (NB - 2))
            g_loaded.prime(sp)

            def load_w(h, b):
                sp.wait_ge(*w_ready(h, b - 1))
                sp.dma_start(w_raw[:, :], weights[h, :, bass.ds((b - 1) * W_SLICE, W_SLICE)]).then_inc(w_loaded.sem, 16)

            def load_g(i, b, h):
                sp.wait_ge(*decay_raw(i - 1))
                sp.dma_start(g_all[:, :], g_rows[bass.ds(b * HKV + h, 1), :].to_broadcast([P, T])).then_inc(g_loaded.sem, 16)

            sp.dma_start(a[:, :, :].rearrange("p q n -> p (q n)")[:, 0:W_USED], weights[0, :, 0:W_USED]).then_inc(w0_loaded, 16)
            load_g(0, 0, 0)

            def unit(i, b, par, pair, nxt, prev):
                if middle(b):
                    load_w(pair * 2 + (par + 1), b)
                load_g(nxt[0], nxt[1], next_head(pair, par, nxt))

            walk(sp, unit)

        @block.tensor
        def _(pe):
            for counter in (qk_proj, v_proj, v_turned, scored, summed):
                counter.prime(pe)
            mixed.prime(pe, left=KC)

            def project(i, b, par, part, n, chunks=range(KC)):
                bank = {"q0": 2, "q1": 0, "k": 1, "v": 2}[part]
                for k in chunks:
                    mm = product3(pe, work_ps[:, bank], col(w_hi, par, part, k), col(w_lo, par, part, k),
                                  c.xn_hi[:, b, k], c.xn_lo[:, b, k], k == 0, k == KC - 1)
                if k == KC - 1:
                    mm.then_inc(n.sem, 1)

            def project_q0(i, b, par, chunks=range(KC)):
                pe.wait_ge(*v_copied(i - 1))
                project(i, b, par, "q0", qk_proj, chunks)

            def project_v_q1_k(i, b, par, last_out):
                pe.wait_ge(*qk_ready(i, 1))
                project(i, b, par, "v", v_proj)
                pe.wait_ge(*v_ready(i - 1))
                pe.wait_ge(*added(last_out, 1))
                project(i, b, par, "q1", qk_proj)
                pe.wait_ge(*added(last_out))
                project(i, b, par, "k", qk_proj)

            def turn_v(i):
                pe.wait_ge(*qk_ready(i, 2))
                pe.wait_ge(*v_copied(i))
                for j in range(TT):
                    mm = pe.transpose(work_ps[:, 0, j * P:(j + 1) * P], v_feat[:, j * P:(j + 1) * P], c.ident[:, :])
                mm.then_inc(v_turned.sem, 1)

            def output(i, par, last_proj):
                pe.wait_ge(*v_ready(last_proj))
                pe.wait_ge(*qk_ready(last_proj))
                for q in range(REP):
                    pe.wait_ge(*y_ready(i, q + 1))
                    for chunk in range(KC):
                        mm = product3(pe, work_ps[:, chunk], col(w_hi, par, (q, chunk)), col(w_lo, par, (q, chunk)),
                                      y_hi[:, q], y_lo[:, q], q == 0, q == REP - 1)
                        if q == REP - 1:
                            mm.then_inc(mixed.sem, 1)

            def scores(i, q, tiles=range(TILES)):
                pe.wait_ge(*qk_ready(i))
                for tile in tiles:
                    lo, hi = BANKS[tile]
                    n = q * TILES + tile
                    pe.wait_ge(*(squared(i, n - 1) if n >= 2 else squared(i - 1, REP * TILES + n - 1)))
                    for j, at, width in CHUNKS:
                        if lo <= at < hi:
                            keys, t0 = slice(j * P, (j + 1) * P), T - width
                            mm = product3(pe, score_ps[:, n % 2, at - lo:at - lo + width],
                                          qk_hi[:, REP, keys], qk_lo[:, REP, keys],
                                          qk_hi[:, q, t0:T], qk_lo[:, q, t0:T], True, True)
                    mm.then_inc(scored.sem, 1)

            def weigh(i, q):
                pe.wait_ge(*v_ready(i))
                pe.wait_ge(*fixed(i - 1, 3 * q + 3))
                pe.wait_ge(*(fixed(i, 1) if q else fixed(i - 1, 4)))
                for tile, (lo, hi) in enumerate(BANKS):
                    pe.wait_ge(*a_ready(i, q * TILES + tile + 1))
                    for j, at, width in CHUNKS:
                        if lo <= at < hi:
                            keys, t0 = slice(j * P, (j + 1) * P), T - width
                            first, last = j == 0, j == 2
                            product3(pe, y_ps[:, q, t0:T], v_hi[:, keys], v_lo[:, keys],
                                     a_hi[:, q, at:at + width], a_lo[:, q, at:at + width], first, last)
                            pe.matmul(norm_ps[:, t0:T], c.ones_r[:, :], a_hi[:, q, at:at + width], start=first, stop=False)
                            mm = pe.matmul(norm_ps[:, t0:T], c.ones_r[:, :], a_lo[:, q, at:at + width], start=False, stop=last)
                mm.then_inc(summed.sem, 1)

            pe.wait_ge(*w_ready(0))
            project_q0(0, 0, 0)
            pe.wait_ge(*v_ready(-1))
            project(0, 0, 0, "q1", qk_proj)
            project(0, 0, 0, "k", qk_proj)
            pe.wait_ge(*qk_ready(0, 1))
            project(0, 0, 0, "v", v_proj)
            turn_v(0)
            scores(0, 0)
            pe.wait_ge(cleared, 1)
            pe.wait_ge(cleared_ps, 1)

            def unit(i, b, par, pair, nxt, prev):
                if first_row(nxt[1]):
                    pe.wait_ge(*w_ready(next_head(pair, par, nxt)))
                project_q0(*nxt, (0,))
                scores(i, 1, (0, 1))
                project_q0(*nxt, (1,))
                scores(i, 1, (2,))
                weigh(i, 0)
                output(prev[0], prev[2], i)
                project_v_q1_k(*nxt, prev[0])
                weigh(i, 1)
                scores(nxt[0], 0, (0, 1))
                turn_v(nxt[0])
                scores(nxt[0], 0, (2,))

            walk(pe, unit)
            output(LAST, (HKV - 1) % 2, LAST + 1)

        @block.scalar
        def _(act):
            w_hi_ready.prime(act, left=2 - NB)
            for counter in (decay_raw, qk_hi_ready, v_copied, v_hi_ready, squared, logged, inv_raw):
                counter.prime(act)
            y_hi_ready.prime(act, left=1)
            act.preload_act_table_set("natural_log_exp_and_others")

            def split_w(h, par, b, last_out):
                act.wait_ge(*w_loaded(h, 16 * b))
                act.wait_ge(*mixed(last_out))
                act.activation(w_hi[:, par, bass.ds((b - 1) * W_SLICE, W_SLICE)], w_raw[:, :], ACT.Copy)\
                   .then_inc(w_hi_ready.sem, 1)

            def decays(i, b, h):
                act.wait_ge(*g_loaded(i))
                act.wait_ge(*decayed(i - 1))
                for j, at, width in CHUNKS:
                    ins = act.activation(decay[:, at:at + width], g_all[:, T - width:T], ACT.Exp,
                                         bias=c.neg_g[:, bass.ds(b * (HKV * TT) + h * TT + j, 1)])
                ins.then_inc(decay_raw.sem, 1)

            def qk_high(i, n):
                act.wait_ge(*qk_proj(i, n + 1))
                act.wait_ge(*scored(i - 1))
                act.activation(qk_hi[:, n], work_ps[:, {0: 2, 1: 0, 2: 1}[n]], ACT.Copy).then_inc(qk_hi_ready.sem, 1)

            def v_copy(i):
                act.wait_ge(*v_proj(i))
                act.wait_ge(*v_turned(i - 1))
                act.activation(v_feat[:, :], work_ps[:, 2], ACT.Copy).then_inc(v_copied.sem, 1)

            def v_high(i):
                act.wait_ge(*v_turned(i))
                act.wait_ge(*summed(i - 1))
                act.activation(v_hi[:, :], work_ps[:, 0], ACT.Copy).then_inc(v_hi_ready.sem, 1)

            def square(i, q, tile):
                lo, hi = BANKS[tile]
                n = q * TILES + tile
                act.wait_ge(*scored(i, n + 1))
                act.wait_ge(*a_ready(i - 1, n + 1))
                act.activation(a[:, q, lo:hi], score_ps[:, n % 2, 0:hi - lo], ACT.Square,
                               scale=DH ** -0.5).then_inc(squared.sem, 1)

            def log_norm(i, q):
                act.wait_ge(*summed(i, q + 1))
                act.wait_ge(*(fixed(i, 2) if q else fixed(i - 1, 5)))
                act.activation(inv[:, :], norm_ps[:, :], ACT.Ln, bias=c.eps_norm[:, :]).then_inc(logged.sem, 1)

            def invert(i, q):
                act.wait_ge(*logged(i, q + 1))
                act.activation(inv[:, :], inv[:, :], ACT.Exp, scale=-1.0).then_inc(inv_raw.sem, 1)

            def y_high(i, q):
                act.wait_ge(*fixed(i, 3 * q + 3))
                act.wait_ge(*mixed(i - 1))
                act.activation(y_hi[:, q], y[:, :], ACT.Copy).then_inc(y_hi_ready.sem, 1)

            act.wait_ge(w0_loaded, 16)
            act.activation(w_hi[:, 0, 0:W_USED], a[:, :, :].rearrange("p q n -> p (q n)")[:, 0:W_USED], ACT.Copy).then_inc(w0_hi_ready, 1)
            decays(0, 0, 0)
            for n in range(REP + 1):
                qk_high(0, n)
            v_copy(0)
            v_high(0)
            for tile in range(TILES):
                square(0, 0, tile)

            def unit(i, b, par, pair, nxt, prev):
                for tile in range(TILES):
                    square(i, 1, tile)
                y_high(prev[0], 1)
                qk_high(nxt[0], 0)
                log_norm(i, 0)
                invert(i, 0)
                decays(nxt[0], nxt[1], next_head(pair, par, nxt))
                v_copy(nxt[0])
                qk_high(nxt[0], 1)
                y_high(i, 0)
                qk_high(nxt[0], 2)
                if middle(b):
                    split_w(pair * 2 + (par + 1), 1 - par, b, i - 2)
                log_norm(i, 1)
                square(nxt[0], 0, 0)
                square(nxt[0], 0, 1)
                v_high(nxt[0])
                square(nxt[0], 0, 2)
                invert(i, 1)

            walk(act, unit)
            y_high(LAST, 1)

        @block.vector
        def _(dve):
            for counter in (qk_ready, v_ready, a_hi_ready, a_ready):
                counter.prime(dve)
            fixed.prime(dve, left=3)
            y_ready.prime(dve, left=1)
            added.prime(dve, left=KC)
            dve.memset(y_ps[:, 1], 0.0)
            dve.memset(norm_ps[:, :], 1.0).then_inc(cleared_ps, 1)
            dve.wait_ge(cleared_ps, 1)
            dve.wait_ge(cleared, 1)

            def qk_low(i, n):
                dve.wait_ge(*qk_hi_ready(i, n + 1))
                dve.tensor_tensor(qk_lo[:, n], work_ps[:, {0: 2, 1: 0, 2: 1}[n]], qk_hi[:, n].bitcast(F32),
                                  ALU.subtract).then_inc(qk_ready.sem, 1)

            def v_low(i):
                dve.wait_ge(*v_hi_ready(i))
                dve.tensor_tensor(v_lo[:, :], work_ps[:, 0], v_hi[:, :].bitcast(F32), ALU.subtract).then_inc(v_ready.sem, 1)

            def split_a(i, q, tile):
                lo, hi = BANKS[tile]
                n = q * TILES + tile
                dve.wait_ge(*decayed(i, n + 1))
                dve.wait_ge(*summed(i - 1, q + 1))
                dve.tensor_copy(a_hi[:, q, lo:hi], a[:, q, lo:hi]).then_inc(a_hi_ready.sem, 1)
                dve.wait_ge(*a_hi_ready(i, n + 1))
                dve.tensor_tensor(a_lo[:, q, lo:hi], a[:, q, lo:hi], a_hi[:, q, lo:hi].bitcast(F32),
                                  ALU.subtract).then_inc(a_ready.sem, 1)

            def fix_a(i, q):
                dve.wait_ge(*inv_raw(i, q + 1))
                dve.wait_ge(*(fixed(i, 3) if q else fixed(i - 1)))
                dve.scalar_tensor_tensor(out=fix[:, :], in0=norm_ps[:, :], scalar=EPS_NORM, in1=inv[:, :],
                                         op0=ALU.add, op1=ALU.mult).then_inc(fixed.sem, 1)

            def fix_b(i, q):
                dve.wait_ge(*fixed(i, 3 * q + 1))
                dve.scalar_tensor_tensor(out=fix[:, :], in0=fix[:, :], scalar=-2.0, in1=inv[:, :],
                                         op0=ALU.add, op1=ALU.mult).then_inc(fixed.sem, 1)

            def divide(i, q):
                dve.wait_ge(*fixed(i, 3 * q + 2))
                dve.wait_ge(*(y_ready(i, 1) if q else y_ready(i - 1)))
                dve.scalar_tensor_tensor(out=y[:, :], in0=y_ps[:, q], scalar=-1.0, in1=fix[:, :],
                                         op0=ALU.mult, op1=ALU.mult).then_inc(fixed.sem, 1)

            def y_low(i):
                dve.wait_ge(*y_hi_ready(i))
                dve.tensor_tensor(y_lo[:, 1], y[:, :], y_hi[:, 1].bitcast(F32), ALU.subtract).then_inc(y_ready.sem, 1)

            def add(i, b, chunk):
                dve.wait_ge(*mixed(i, chunk + 1))
                dve.tensor_tensor(c.acc[:, b, chunk], c.acc[:, b, chunk], work_ps[:, chunk], ALU.add).then_inc(added.sem, 1)

            for n in range(REP + 1):
                qk_low(0, n)
            v_low(0)

            def unit(i, b, par, pair, nxt, prev):
                fix_a(prev[0], 1)
                split_a(i, 0, 0)
                split_a(i, 0, 1)
                fix_b(prev[0], 1)
                divide(prev[0], 1)
                split_a(i, 0, 2)
                y_low(prev[0])
                qk_low(nxt[0], 0)
                split_a(i, 1, 0)
                split_a(i, 1, 1)
                add(prev[0], prev[1], 0)
                add(prev[0], prev[1], 1)
                split_a(i, 1, 2)
                fix_a(i, 0)
                fix_b(i, 0)
                divide(i, 0)
                qk_low(nxt[0], 1)
                qk_low(nxt[0], 2)
                v_low(nxt[0])

            walk(dve, unit)
            fix_a(LAST, 1)
            fix_b(LAST, 1)
            divide(LAST, 1)
            y_low(LAST)
            for chunk in range(KC):
                add(LAST, NB - 1, chunk)

        @block.gpsimd
        def _(pool):
            for counter in (w_ready, decay_ready, decayed):
                counter.prime(pool)
            for zero in (y_hi[:, 0].bitcast(F32), y_lo[:, 0].bitcast(F32), w_hi[:, 1].bitcast(F32), w_lo[:, 1].bitcast(F32)):
                pool.memset(zero, 0.0)
            pool.memset(inv[:, :], 1.0)
            pool.memset(c.acc[:, :, :, :], 0.0).then_inc(cleared, 1)

            def split_w(h, par, b):
                pool.wait_ge(*w_hi_ready(h, b))
                cols = bass.ds((b - 1) * W_SLICE, W_SLICE)
                pool.tensor_tensor(w_lo[:, par, cols], w_raw[:, :], w_hi[:, par, cols].bitcast(F32), ALU.subtract)\
                    .then_inc(w_ready.sem, 1)

            def y_low(i):
                pool.wait_ge(*y_hi_ready(i, 1))
                pool.tensor_tensor(y_lo[:, 0], y[:, :], y_hi[:, 0].bitcast(F32), ALU.subtract).then_inc(y_ready.sem, 1)

            def mask(i):
                pool.wait_ge(*decay_raw(i))
                pool.sem_inc(mask_begun, 1)
                for j, at, width in CHUNKS:
                    ins = pool.affine_select(out=decay[:, at:at + P], in_=decay[:, at:at + P], compare_op=ALU.is_ge,
                                             fill=0.0, base=0, pattern=[[1, P]], channel_multiplier=-1)
                ins.then_inc(decay_ready.sem, 1)

            def apply_decay(i, q):
                if q == 0:
                    pool.wait_ge(*decay_ready(i))
                for tile, (lo, hi) in enumerate(BANKS):
                    n = q * TILES + tile
                    pool.wait_ge(*squared(i, n + 1))
                    pool.tensor_tensor(a[:, q, lo:hi], a[:, q, lo:hi], decay[:, lo:hi], ALU.mult)\
                        .then_inc(decayed.sem, 1)

            pool.wait_ge(w0_hi_ready, 1)
            pool.tensor_tensor(w_lo[:, 0, 0:W_USED], a[:, :, :].rearrange("p q n -> p (q n)")[:, 0:W_USED], w_hi[:, 0, 0:W_USED].bitcast(F32),
                               ALU.subtract).then_inc(w_ready.sem, NB - 2)
            mask(0)
            apply_decay(0, 0)

            def unit(i, b, par, pair, nxt, prev):
                apply_decay(i, 1)
                mask(nxt[0])
                y_low(i)
                if middle(b):
                    split_w(pair * 2 + (par + 1), 1 - par, b)
                apply_decay(nxt[0], 0)

            walk(pool, unit)


def experts(nc, c, tag, weights, gates, n_full, last_size, swiglu, mixer_out):
    NZ = 2 if swiglu else 1
    W_E = W_E1 if swiglu else W_E0
    W_SL = w_slice(W_E)
    W_G = W_SL * (NB - 2)
    ZB = 4
    AHEAD = ZB // NZ
    with ExitStack() as ctx:
        s = Space(nc, ctx, tag)
        w_hi = s.sb("w_hi", [P, 2, W_G], F32R)
        w_lo = s.sb("w_lo", [P, 2, W_G], F32R)
        w_raw = s.sb("w_raw", [P, W_SL])
        w_first = s.sb("w_first", [P, GROUP, W_E])
        gate = s.sb("gate", [P, 2, GROUP, T])
        act_gate = s.sb("act_gate", [P, 2, T])
        h = s.sb("h", [P, 2, T])
        h_hi = s.sb("h_hi", [P, GROUP, T], F32R)
        h_lo = s.sb("h_lo", [P, GROUP, T], F32R)
        z_ps = s.ps("z", [P, ZB, T])
        out_ps = s.ps("out", [P, 2, KC, T])
        acc_parts = [(NB - 1, NB), (0, 1), (1, NB - 1)]
        mixer_stored = [s.sem(f"mixer_stored{n}") for n in range(len(acc_parts))]
        cleared, cleared_ps = s.sem("acc_cleared"), s.sem("cleared_ps")
        w0_loaded = [s.sem(f"w0_loaded{e}") for e in range(GROUP)]
        w0_hi_ready, w0_ready = s.sem("w0_hi_ready"), s.sem("w0_ready")
        w_loaded = s.steps("w_loaded", 16 * (NB - 2))
        w_hi_ready = s.steps("w_hi_ready", NB - 2)
        w_ready = s.steps("w_ready", NB - 2)
        g_loaded = [s.steps(f"g_loaded{q}", 16) for q in range(2)]
        projected = s.steps("projected", GROUP)
        silu_ready = s.steps("silu_ready", GROUP)
        act_ready = s.steps("act_ready", GROUP)
        h_ready = s.steps("h_ready", GROUP)
        h_hi_ready = s.steps("h_hi_ready", GROUP)
        h_split = s.steps("h_split", GROUP)
        used = s.steps("used", GROUP)
        added = s.steps("added", KC)
        block = ctx.enter_context(s.block())

        def walk(engine, unit, split=None):
            def group(g, par, size, last):
                i0 = g * NB
                unit(i0, g, 0, 0, 0, par, size, (i0 + 1, g, 1, par, size))
                with engine.Fori(0, NB // 2 - 1) as pair:
                    for sub in (1, 0):
                        b = pair * 2 + (2 - sub)
                        unit(i0 + b, g, b, pair + (1 - sub), sub, par, size, (i0 + b + 1, g, b + 1, par, size))
                        if split and not last:
                            split(g + 1, 1 - par, pair * 2 + (1 - sub), i0 - 1)
                unit(i0 + (NB - 1), g, NB - 1, NB // 2 - 1, 1, par, size, None if last else (i0 + NB, g + 1, 0, 1 - par, GROUP))

            with engine.Fori(0, n_full // 2) as two:
                for par in range(2):
                    group(two * 2 + par, par, GROUP, False)
            group(n_full, 0, last_size, True)

        LAST = n_full * NB + NB - 1

        @block.sync
        def _(sp):
            w_loaded.prime(sp, left=-16 * (NB - 2))
            for q in g_loaded:
                q.prime(sp)

            def load_w(g, par, part, last):
                sp.wait_ge(*w_ready(g, part))
                sp.dma_start(w_raw[:, :], weights[g, :, bass.ds(part * W_SL, W_SL)]).then_inc(w_loaded.sem, 16)

            def unit(i, g, b, pr, sub, par, size, nxt):
                sp.wait_ge(*act_ready(i - 2))
                src = gates[bass.ds(g * GROUP, size), bass.ds(b * T, T)]
                sp.dma_start(gate[:, sub, 0:size], src.unsqueeze(0).to_broadcast([P, size, T])).then_inc(g_loaded[sub].sem, 16)

            for e in range(GROUP):
                sp.dma_start(w_first[:, e], weights[0, :, e * W_E:(e + 1) * W_E]).then_inc(w0_loaded[e], 16)
            for (b0, b1), stored in zip(acc_parts, mixer_stored):
                sp.dma_start(mixer_out[b0:b1].rearrange("b p k t -> p b k t"), c.acc[:, b0:b1]).then_inc(stored, 16)
            walk(sp, unit, load_w)
            for stored in mixer_stored:
                sp.wait_ge(stored, 16)

        @block.tensor
        def _(pe):
            projected.prime(pe)
            used.prime(pe)

            def project(i, b, par, e, inc, inc_before):
                pe.wait_ge(*(h_ready(i, (e - AHEAD + 1) * inc) if e >= AHEAD
                             else h_ready(i - 1, (GROUP // inc_before + e - AHEAD + 1) * inc_before) if inc_before < GROUP // AHEAD
                             else h_ready(i - 1, (e + 1) * inc_before)))
                for n in range(NZ):
                    for k in range(KC):
                        at = e * W_E + (n * KC + k) * P
                        mm = product3(pe, z_ps[:, (e * NZ + n) % ZB], w_hi[:, par, at:at + P], w_lo[:, par, at:at + P],
                                      c.xn_hi[:, b, k], c.xn_lo[:, b, k], k == 0, k == KC - 1)
                mm.then_inc(projected.sem, inc)

            def unit(i, g, b, pr, sub, par, size, nxt):
                inc = GROUP // size
                if nxt and isinstance(nxt[2], int) and nxt[2] == 0:
                    pe.wait_ge(*w_ready(nxt[1]))
                pe.wait_ge(*added(i - 2))
                for e in range(GROUP):
                    if nxt and e < nxt[4]:
                        project(nxt[0], nxt[2], nxt[3], e, GROUP // nxt[4], inc)
                    if e < size:
                        pe.wait_ge(*h_split(i, (e + 1) * inc))
                        for chunk in range(KC):
                            at = e * W_E + NZ * KC * P + chunk * P
                            mm = product3(pe, out_ps[:, sub, chunk], w_hi[:, par, at:at + P], w_lo[:, par, at:at + P],
                                          h_hi[:, e], h_lo[:, e], e == 0, e == size - 1)
                        mm.then_inc(used.sem, inc)

            for e in range(GROUP):
                pe.wait_ge(w0_ready, e + 1)
                project(0, 0, 0, e, 1, 1)
            walk(pe, unit)

        @block.scalar
        def _(act):
            w_hi_ready.prime(act, left=2 - NB)
            silu_ready.prime(act)
            h_hi_ready.prime(act)
            if swiglu:
                act.preload_act_table_set("silu_and_others")

            def split_w(g, par, part, last):
                act.wait_ge(*w_loaded(g, 16 * (part + 1)))
                act.wait_ge(*used(last))
                act.activation(w_hi[:, par, bass.ds(part * W_SL, W_SL)], w_raw[:, :], ACT.Copy).then_inc(w_hi_ready.sem, 1)

            def silu(i, e, inc):
                act.wait_ge(*projected(i, (e + 1) * inc))
                act.wait_ge(*(h_ready(i, (e - 1) * inc) if e >= 2 else h_ready(i - 1)))
                act.activation(act_gate[:, e % 2], z_ps[:, e * NZ % ZB], ACT.Silu).then_inc(silu_ready.sem, inc)

            def unit(i, g, b, pr, sub, par, size, nxt):
                inc = GROUP // size
                for e in range(size + 1):
                    if swiglu and e < size:
                        silu(i, e, inc)
                    if e >= 1:
                        act.wait_ge(*h_ready(i, e * inc))
                        act.wait_ge(*used(i - 1, e * inc))
                        act.activation(h_hi[:, e - 1], h[:, (e - 1) % 2], ACT.Copy).then_inc(h_hi_ready.sem, inc)

            for e in range(GROUP):
                act.wait_ge(w0_loaded[e], 16)
                act.activation(w_hi[:, 0, e * W_E:(e + 1) * W_E], w_first[:, e], ACT.Copy).then_inc(w0_hi_ready, 1)
            walk(act, unit, split_w)

        @block.vector
        def _(dve):
            for counter in (h_ready, h_split) + (() if swiglu else (act_ready,)):
                counter.prime(dve)
            added.prime(dve, left=KC)
            for e in range(GROUP):
                dve.wait_ge(w0_hi_ready, e + 1)
                dve.tensor_tensor(w_lo[:, 0, e * W_E:(e + 1) * W_E], w_first[:, e],
                                  w_hi[:, 0, e * W_E:(e + 1) * W_E].bitcast(F32), ALU.subtract).then_inc(w0_ready, 1)
            dve.memset(out_ps[:, 1], 0.0).then_inc(cleared_ps, 1)
            dve.wait_ge(cleared_ps, 1)

            def low(i, e, inc):
                dve.wait_ge(*h_hi_ready(i, (e + 1) * inc))
                dve.tensor_tensor(h_lo[:, e], h[:, e % 2], h_hi[:, e].bitcast(F32), ALU.subtract).then_inc(h_split.sem, inc)

            def add(i, b, sub):
                dve.wait_ge(*used(i))
                for chunk in range(KC):
                    dve.tensor_tensor(c.acc[:, b, chunk], c.acc[:, b, chunk], out_ps[:, sub, chunk], ALU.add).then_inc(added.sem, 1)

            def unit(i, g, b, pr, sub, par, size, nxt):
                inc = GROUP // size
                if not swiglu:
                    dve.wait_ge(*g_loaded[sub](g * (NB // 2) + pr))
                for e in range(size):
                    n = (e + 1) * inc
                    z = z_ps[:, (e * NZ + NZ - 1) % ZB]
                    if swiglu:
                        dve.wait_ge(*act_ready(i, n))
                    else:
                        dve.wait_ge(*projected(i, n))
                        dve.wait_ge(*(h_ready(i, n - 2 * inc) if e >= 2 else h_ready(i - 1)))
                        dve.scalar_tensor_tensor(out=act_gate[:, e % 2], in0=z, scalar=0.0, in1=gate[:, sub, e],
                                                 op0=ALU.max, op1=ALU.mult).then_inc(act_ready.sem, inc)
                        dve.wait_ge(*act_ready(i, n))
                    dve.wait_ge(*(h_split(i, n - 2 * inc) if e >= 2 else h_split(i - 1)))
                    dve.tensor_tensor(h[:, e % 2], act_gate[:, e % 2], z, ALU.mult).then_inc(h_ready.sem, inc)
                    if e >= 1:
                        low(i, e - 1, inc)
                low(i, size - 1, inc)
                dve.wait_ge(cleared, 1 if isinstance(b, int) and b == 0 else len(acc_parts))
                if isinstance(b, int):
                    add(i - 1, (b - 1) % NB, 1 - sub)
                else:
                    add(i - 1, b - 1, 1 - sub)

            walk(dve, unit)
            add(LAST, NB - 1, 1)

        @block.gpsimd
        def _(pool):
            w_ready.prime(pool, left=2 - NB)
            if swiglu:
                act_ready.prime(pool)

            def split_w(g, par, part, last):
                pool.wait_ge(*w_hi_ready(g, part + 1))
                cols = bass.ds(part * W_SL, W_SL)
                pool.tensor_tensor(w_lo[:, par, cols], w_raw[:, :], w_hi[:, par, cols].bitcast(F32), ALU.subtract)\
                    .then_inc(w_ready.sem, 1)

            def unit(i, g, b, pr, sub, par, size, nxt):
                if not swiglu:
                    return
                inc = GROUP // size
                pool.wait_ge(*g_loaded[sub](g * (NB // 2) + pr))
                for e in range(size):
                    pool.wait_ge(*silu_ready(i, (e + 1) * inc))
                    pool.tensor_tensor(act_gate[:, e % 2], act_gate[:, e % 2], gate[:, sub, e], ALU.mult)\
                        .then_inc(act_ready.sem, inc)

            for (b0, b1), stored in zip(acc_parts, mixer_stored):
                pool.wait_ge(stored, 16)
                pool.memset(c.acc[:, b0:b1], 0.0).then_inc(cleared, 1)
            walk(pool, unit, split_w)


def route1(nc, c, logits, gates):
    TILES = P // E1
    with ExitStack() as ctx:
        s = Space(nc, ctx, "rt1")
        shifted = s.sb("shifted", [P, NT, E1])
        prob = s.sb("prob", [P, NT, E1 + 8])
        top8 = s.sb("top8", [P, NT, 8])
        pick = s.sb("pick", [P, NT, E1 + 8])
        weight = s.sb("weight", [P, NT, E1])
        stat = s.sb("stat", [P, NT])
        shared = s.sb("shared", [P, P])
        g_t = s.sb("g_t", [P, NT // TILES, P])
        turn_ps = s.ps("turn", [P, NT // TILES, P])
        shifted_ready, exp_ready, shared_ready, gates_ready, turned, g_t_ready, stored = (
            s.sem(n) for n in ("shifted_ready", "exp_ready", "shared_ready", "gates_ready", "turned", "g_t_ready", "stored"))
        steps = s.sem("dve_steps")
        block = ctx.enter_context(s.block())

        @block.scalar
        def _(act):
            act.preload_act_table_set("natural_log_exp_and_others")
            act.wait_ge(shifted_ready, 1)
            act.activation(weight[:, :, :], shifted[:, :, :], ACT.Exp).then_inc(exp_ready, 1)

        @block.gpsimd
        def _(pool):
            pool.memset(shared[:, :], 1.0 / (TOP1 + 1)).then_inc(shared_ready, 1)

        @block.vector
        def _(dve):
            link = Chain(dve, steps)

            def by_tile():
                return stat[:, :].unsqueeze(2).to_broadcast([P, NT, E1])

            link(dve.memset(prob[:, :, :], -1.0))
            link(dve.tensor_reduce(stat[:, :], logits[:, :, :], AX_X, ALU.max))
            dve.tensor_tensor(shifted[:, :, :], logits[:, :, :], by_tile(), ALU.subtract).then_inc(shifted_ready, 1)
            dve.wait_ge(exp_ready, 1)
            link(dve.tensor_reduce(stat[:, :], weight[:, :, :], AX_X, ALU.add))
            link(dve.reciprocal(stat[:, :], stat[:, :]))
            link(dve.tensor_tensor(prob[:, :, 0:E1], weight[:, :, :], by_tile(), ALU.mult))
            pick_top(dve, link, prob, E1, top8, pick, TOP1, weight[:, :, :])
            link(dve.tensor_tensor(weight[:, :, :], weight[:, :, :], prob[:, :, 0:E1], ALU.mult))
            link(dve.tensor_reduce(stat[:, :], weight[:, :, :], AX_X, ALU.add))
            link(dve.reciprocal(stat[:, :], stat[:, :]))
            link(dve.tensor_tensor(weight[:, :, :], weight[:, :, :], by_tile(), ALU.mult))
            dve.tensor_scalar(weight[:, :, :], weight[:, :, :], TOP1 / (TOP1 + 1), None, ALU.mult).then_inc(gates_ready, 1)
            dve.wait_ge(turned, 1)
            dve.tensor_copy(g_t[:, :, :], turn_ps[:, :, :]).then_inc(g_t_ready, 1)

        @block.tensor
        def _(pe):
            pe.wait_ge(gates_ready, 1)
            for n in range(NT // TILES):
                mm = pe.transpose(turn_ps[:, n], weight[:, n * TILES:(n + 1) * TILES].rearrange("p n e -> p (n e)"), c.ident[:, :])
            mm.then_inc(turned, 1)

        @block.sync
        def _(sp):
            sp.wait_ge(shared_ready, 1)
            sp.dma_start(gates[E1:E1 + SHARED1, :].rearrange("e (n t) -> (e n) t", t=P), shared[0:SHARED1 * NT, :])\
              .then_inc(stored, 16)
            sp.wait_ge(g_t_ready, 1)
            store_gates(sp, gates, g_t, E1, TILES, stored)
            sp.wait_ge(stored, 16 * (1 + TILES))


def mix(nc, c, w_mix, cols):
    U, V, G1, G2 = 0, 1, 2, 3
    with ExitStack() as ctx:
        s = Space(nc, ctx, "mix")
        w_raw = s.sb("w_raw", [P, W_MIX])
        w_hi = s.sb("w_hi", [P, W_MIX], F32R)
        w_lo = s.sb("w_lo", [P, W_MIX], F32R)
        col = s.sb("col", [P, COLS])
        ones = s.sb("ones", [P, T])
        hid = s.sb("hid", [P, T])
        hid_hi = s.sb("hid_hi", [P, T], F32R)
        hid_lo = s.sb("hid_lo", [P, T], F32R)
        gate = s.sb("gate", [P, KC, T])
        u = s.sb("u", [P, KC, T])
        v = s.sb("v", [P, KC, T])
        total = s.sb("total", [P, KC, T])
        prod = s.sb("prod", [P, KC, T])
        prod_hi = s.sb("prod_hi", [P, KC, T], F32R)
        prod_lo = s.sb("prod_lo", [P, KC, T], F32R)
        xn = s.sb("xn", [P, KC, T])
        conv = s.sb("conv", [P, 2, KC, T])
        u_ps = s.ps("u_ps", [P, KC, T])
        v_ps = s.ps("v_ps", [P, KC, T])
        g_ps = s.ps("g_ps", [P, 2, T])
        out_ps = s.ps("out", [P, KC, T])
        w_loaded, w_hi_ready, w_ready, col_loaded, ones_ready = (
            s.sem(n) for n in ("w_loaded", "w_hi_ready", "w_ready", "col_loaded", "ones_ready"))
        hid_proj = s.steps("hid_proj", 1)
        uv_proj = s.steps("uv_proj", 2)
        relu_ready = s.steps("relu_ready", 1)
        hid_hi_ready = s.steps("hid_hi_ready", 1)
        hid_split = s.steps("hid_split", 1)
        gate_proj = s.steps("gate_proj", KC)
        gate_ready = s.steps("gate_ready", KC)
        u_ready = s.steps("u_ready", KC)
        v_ready = s.steps("v_ready", KC)
        summed = s.steps("summed", KC)
        prod_ready = s.steps("prod_ready", KC)
        prod_hi_ready = s.steps("prod_hi_ready", KC)
        prod_split = s.steps("prod_split", KC)
        out_ready = s.steps("out_ready", KC)
        xn_ready = s.steps("xn_ready", KC)
        centre_ready = s.steps("centre_ready", KC)
        conv_ready = s.steps("conv_ready", 2 * KC)
        stored = s.steps("stored", KC)
        block = ctx.enter_context(s.block())

        def walk(engine, unit, end):
            unit(0, 0, None)
            with engine.Fori(0, NB // 2 - 1) as pair:
                for par in (1, 0):
                    i = pair * 2 + (2 - par)
                    unit(i, par, i - 1)
            unit(NB - 1, 1, NB - 2)
            end(NB - 1, 1)

        def w(which, k, chunk):
            return MIX_AT[which] + (k * KC + chunk) * P

        def cc(name, k):
            at = COL_AT[name] + k
            return col[:, at:at + 1]

        @block.sync
        def _(sp):
            sp.dma_start(w_raw[:, :], w_mix).then_inc(w_loaded, 16)
            sp.dma_start(col[:, :], cols).then_inc(col_loaded, 16)

        @block.tensor
        def _(pe):
            for counter in (hid_proj, uv_proj, gate_proj, out_ready):
                counter.prime(pe)
            pe.wait_ge(w_ready, 1)

            def project(out, i, at, step):
                for k in range(KC):
                    mm = product3(pe, out, w_hi[:, at + k * step:at + k * step + P], w_lo[:, at + k * step:at + k * step + P],
                                  c.xn_hi[:, i, k], c.xn_lo[:, i, k], k == 0, k == KC - 1)
                return mm

            def output(i):
                pe.wait_ge(*prod_split(i))
                pe.wait_ge(*stored(i - 1))
                for chunk in range(KC):
                    for k in range(KC):
                        at = w("u", k, chunk)
                        mm = product3(pe, out_ps[:, chunk], w_hi[:, at:at + P], w_lo[:, at:at + P],
                                      prod_hi[:, k], prod_lo[:, k], k == 0, k == KC - 1)
                    mm.then_inc(out_ready.sem, 1)

            def unit(i, par, prev):
                pe.wait_ge(*gate_ready(i - 1))
                project(g_ps[:, 0], i, MIX_AT["g1"], P).then_inc(hid_proj.sem, 1)
                pe.wait_ge(*u_ready(i - 1))
                pe.wait_ge(*v_ready(i - 1))
                for n, (name, out) in enumerate((("u", u_ps), ("v", v_ps))):
                    for chunk in range(KC):
                        mm = project(out[:, chunk], i, w(name, 0, chunk), KC * P)
                    mm.then_inc(uv_proj.sem, 1)
                    if n == 0:
                        pe.wait_ge(*hid_split(i))
                        for chunk in (1, 0):
                            at = MIX_AT["g2"] + chunk * P
                            product3(pe, g_ps[:, chunk], w_hi[:, at:at + P], w_lo[:, at:at + P], hid_hi[:, :], hid_lo[:, :],
                                     True, True).then_inc(gate_proj.sem, 1)
                if prev is not None:
                    output(prev)

            walk(pe, unit, lambda i, par: output(i))

        @block.scalar
        def _(act):
            for counter in (relu_ready, hid_hi_ready, gate_ready, prod_hi_ready, centre_ready):
                counter.prime(act)
            act.preload_act_table_set("sigmoid_and_others")
            act.wait_ge(w_loaded, 16)
            act.activation(w_hi[:, :], w_raw[:, :], ACT.Copy).then_inc(w_hi_ready, 1)
            act.wait_ge(col_loaded, 16)

            def prod_high(i):
                for k in range(KC):
                    act.wait_ge(*prod_ready(i, k + 1))
                    act.wait_ge(*out_ready(i - 1))
                    act.activation(prod_hi[:, k], prod[:, k], ACT.Copy).then_inc(prod_hi_ready.sem, 1)

            def unit(i, par, prev):
                act.wait_ge(*hid_proj(i))
                act.wait_ge(*hid_split(i - 1))
                act.activation(hid[:, :], g_ps[:, 0], ACT.Relu, bias=cc("bg1", 0)).then_inc(relu_ready.sem, 1)
                act.wait_ge(*relu_ready(i))
                act.wait_ge(*gate_proj(i - 1))
                act.activation(hid_hi[:, :], hid[:, :], ACT.Copy).then_inc(hid_hi_ready.sem, 1)
                if prev is not None:
                    prod_high(prev)
                for k in range(KC):
                    act.wait_ge(*xn_ready(i, k + 1))
                    act.wait_ge(*stored(i - 2))
                    act.activation(conv[:, par, k], xn[:, k], ACT.Identity, bias=cc("conv_b", k), scale=cc("conv1", k))\
                       .then_inc(centre_ready.sem, 1)
                for n, chunk in enumerate((1, 0)):
                    act.wait_ge(*gate_proj(i, n + 1))
                    act.wait_ge(*u_ready(i - 1))
                    act.wait_ge(*v_ready(i - 1))
                    act.activation(gate[:, chunk], g_ps[:, chunk], ACT.Sigmoid, bias=cc("bg2", chunk)).then_inc(gate_ready.sem, 1)

            walk(act, unit, lambda i, par: prod_high(i))

        @block.vector
        def _(dve):
            for counter in (u_ready, v_ready, summed, conv_ready, stored):
                counter.prime(dve)
            dve.memset(ones[:, :], 1.0).then_inc(ones_ready, 1)
            dve.wait_ge(ones_ready, 1)
            dve.wait_ge(col_loaded, 16)

            def store(i, par):
                for k in range(KC):
                    dve.wait_ge(*out_ready(i, k + 1))
                    dve.tensor_tensor(c.acc[:, i, k], conv[:, par, k], out_ps[:, k], ALU.add).then_inc(stored.sem, 1)

            def unit(i, par, prev):
                for k in range(KC):
                    dve.wait_ge(*centre_ready(i, k + 1))
                    dve.scalar_tensor_tensor(out=conv[:, par, k, 1:T], in0=xn[:, k, 0:T - 1], scalar=cc("conv0", k),
                                             in1=conv[:, par, k, 1:T], op0=ALU.mult, op1=ALU.add).then_inc(conv_ready.sem, 1)
                for k in range(KC):
                    dve.wait_ge(*conv_ready(i, k + 1))
                    dve.scalar_tensor_tensor(out=conv[:, par, k, 0:T - 1], in0=xn[:, k, 1:T], scalar=cc("conv2", k),
                                             in1=conv[:, par, k, 0:T - 1], op0=ALU.mult, op1=ALU.add).then_inc(conv_ready.sem, 1)
                dve.wait_ge(*conv_ready(i))
                dve.wait_ge(*gate_ready(i))
                dve.wait_ge(*uv_proj(i, 1))
                for k in range(KC):
                    dve.scalar_tensor_tensor(out=u[:, k], in0=u_ps[:, k], scalar=cc("bu", k), in1=gate[:, k],
                                             op0=ALU.add, op1=ALU.mult).then_inc(u_ready.sem, 1)
                dve.wait_ge(*uv_proj(i))
                dve.wait_ge(*prod_ready(i - 1))
                for k in range(KC):
                    dve.scalar_tensor_tensor(out=v[:, k], in0=v_ps[:, k], scalar=cc("bv", k), in1=gate[:, k],
                                             op0=ALU.add, op1=ALU.mult).then_inc(v_ready.sem, 1)
                for k in range(KC):
                    dve.wait_ge(*u_ready(i, k + 1))
                    dve.tensor_tensor_scan(total[:, k], ones[:, :], u[:, k], 0.0, ALU.mult, ALU.add).then_inc(summed.sem, 1)
                if prev is not None:
                    store(prev, 1 - par)

            walk(dve, unit, store)

        @block.gpsimd
        def _(pool):
            for counter in (hid_split, xn_ready, prod_ready, prod_split):
                counter.prime(pool)
            pool.wait_ge(w_hi_ready, 1)
            pool.tensor_tensor(w_lo[:, :], w_raw[:, :], w_hi[:, :].bitcast(F32), ALU.subtract).then_inc(w_ready, 1)

            def prod_low(i):
                for k in range(KC):
                    pool.wait_ge(*prod_hi_ready(i, k + 1))
                    pool.tensor_tensor(prod_lo[:, k], prod[:, k], prod_hi[:, k].bitcast(F32), ALU.subtract)\
                        .then_inc(prod_split.sem, 1)

            def unit(i, par, prev):
                pool.wait_ge(*hid_hi_ready(i))
                pool.tensor_tensor(hid_lo[:, :], hid[:, :], hid_hi[:, :].bitcast(F32), ALU.subtract).then_inc(hid_split.sem, 1)
                if prev is not None:
                    prod_low(prev)
                for k in range(KC):
                    pool.wait_ge(*conv_ready(i - 1))
                    pool.tensor_tensor(xn[:, k], c.xn_hi[:, i, k].bitcast(F32), c.xn_lo[:, i, k].bitcast(F32), ALU.add)\
                        .then_inc(xn_ready.sem, 1)
                for k in range(KC):
                    pool.wait_ge(*summed(i, k + 1))
                    pool.wait_ge(*v_ready(i, k + 1))
                    pool.wait_ge(*prod_split(i - 1))
                    pool.tensor_tensor(prod[:, k], total[:, k], v[:, k], ALU.mult).then_inc(prod_ready.sem, 1)

            walk(pool, unit, lambda i, par: prod_low(i))


def finish(nc, c, x1, mixer, out):
    with ExitStack() as ctx:
        s = Space(nc, ctx, "fin")
        x = s.sb("x", [P, 2, KC, T])
        m = s.sb("m", [P, 2, KC, T])
        act_ffn = s.sb("act_ffn", [P, 2, KC, T])
        x_loaded = [s.steps(f"x_loaded{q}", 16) for q in range(2)]
        m_loaded = [s.steps(f"m_loaded{q}", 16) for q in range(2)]
        stored = [s.steps(f"stored{q}", 16) for q in range(2)]
        silu_ready = s.steps("silu_ready", 1)
        gated = s.steps("gated", 1)
        summed = s.steps("summed", 1)
        block = ctx.enter_context(s.block())

        def rows(engine):
            with engine.Fori(0, NB // 2) as pair:
                for par in range(2):
                    yield pair, par, pair * 2 + par

        @block.sync
        def _(sp):
            for q in x_loaded + m_loaded:
                q.prime(sp)
            for pair, par, i in rows(sp):
                sp.wait_ge(*stored[par](pair - 1))
                sp.dma_start(x[:, par], x1[i]).then_inc(x_loaded[par].sem, 16)
                sp.dma_start(m[:, par], mixer[i]).then_inc(m_loaded[par].sem, 16)

        @block.scalar
        def _(act):
            silu_ready.prime(act)
            for q in stored:
                q.prime(act)
            act.preload_act_table_set("silu_and_others")
            for pair, par, i in rows(act):
                act.wait_ge(*gated(i - 2))
                act.activation(act_ffn[:, par], c.acc[:, i], ACT.Silu).then_inc(silu_ready.sem, 1)
                act.wait_ge(*summed(i))
                act.dma_start(out[i], x[:, par]).then_inc(stored[par].sem, 16)
            for q in stored:
                act.wait_ge(*q(NB // 2 - 1))

        @block.vector
        def _(dve):
            gated.prime(dve)
            summed.prime(dve)
            for pair, par, i in rows(dve):
                dve.wait_ge(*silu_ready(i))
                dve.wait_ge(*m_loaded[par](pair))
                dve.tensor_tensor(act_ffn[:, par], act_ffn[:, par], m[:, par], ALU.mult).then_inc(gated.sem, 1)
                dve.wait_ge(*gated(i))
                dve.wait_ge(*x_loaded[par](pair))
                dve.tensor_tensor(x[:, par], x[:, par], act_ffn[:, par], ALU.add).then_inc(summed.sem, 1)


def program(nc, a, out):
    with ExitStack() as ctx:
        s = Space(nc, ctx, "all")

        class c:
            mean = s.sb("mean", [P, P])
            ones = s.sb("ones", [P, P])
            ones_r = s.sb("ones_r", [P, P], F32R)
            ident = s.sb("ident", [P, P])
            upto = s.sb("upto", [P, P])
            eps_ln = s.sb("eps_ln", [P, 1])
            eps_norm = s.sb("eps_norm", [P, 1])
            neg_g = s.sb("neg_g", [P, NB * HKV * TT])
            xn_hi = s.sb("xn_hi", [P, NB, KC, T], F32R)
            xn_lo = s.sb("xn_lo", [P, NB, KC, T], F32R)
            acc = s.sb("acc", [P, NB, KC, T])

        constants(nc, c)
        g_rows = nc.dram_tensor("g_rows", (NB * HKV, T), F32).ap()
        gates0 = nc.dram_tensor("gates0", (E0 + SHARED0, NB * T), F32).ap()
        with ExitStack() as c2:
            logits = Space(nc, c2, "l0").sb("logits", [P, NT, LOG0])
            layernorm(nc, c, "ln0", a["rw0"], LOG0, logits, a["x"])
            decay_logs(nc, c, logits, g_rows)
            route0(nc, c, logits, a["br0"], gates0)
        attention(nc, c, a["w_att"], g_rows)
        mixer0 = nc.dram_tensor("mixer0", (NB, P, KC, T), F32).ap()
        experts(nc, c, "moe0", a["w_e0"], gates0, E0 // GROUP, SHARED0, False, mixer0)
        x1 = nc.dram_tensor("x1", (NB, P, KC, T), F32).ap()
        mixer1 = nc.dram_tensor("mixer1", (NB, P, KC, T), F32).ap()
        gates1 = nc.dram_tensor("gates1", (E1 + SHARED1, NB * T), F32).ap()

        class combine:
            mixer, bias, x_out = mixer0, a["bc0"], x1

        with ExitStack() as c2:
            logits = Space(nc, c2, "l1").sb("logits", [P, NT, E1])
            layernorm(nc, c, "ln1", a["rw1"], E1, logits, a["x"], combine)
            route1(nc, c, logits, gates1)
        mix(nc, c, a["w_mix"], a["cols"])
        experts(nc, c, "moe1", a["w_e1"], gates1, (E1 + SHARED1 - 1) // GROUP, GROUP, True, mixer1)
        finish(nc, c, x1, mixer1, out)


def by_chunk(w):
    import numpy as np
    return np.ascontiguousarray(w.reshape(KC, P, -1).transpose(1, 0, 2))


def lay_out(v):
    import numpy as np

    f = {n: np.asarray(x) for n, x in v.items()}
    a = {"x": np.ascontiguousarray(f["L0_attn_hidden_states"].reshape(NB, T, KC, P).transpose(0, 3, 2, 1))}
    a["rw0"] = by_chunk(np.concatenate([f["L0_ffn_Wr"].T, f["L0_attn_Wg"]], 1))
    a["br0"] = f["L0_ffn_br"][None]
    heads = [by_chunk(f[n]).reshape(P, KC, HKV, -1) for n in ("L0_attn_Wq", "L0_attn_Wk", "L0_attn_Wv")]
    w = np.zeros((HKV + 1, P, W_ATT), np.float32)
    w[:HKV, :, :KC * QKV] = np.concatenate(heads, 3).transpose(2, 0, 1, 3).reshape(HKV, P, KC * QKV)
    w[:HKV, :, KC * QKV:KC * QKV + REP * D] = f["L0_attn_Wc"].reshape(HKV, REP, DH, D).transpose(0, 2, 1, 3).reshape(HKV, P, REP * D)
    a["w_att"] = w
    a["bc0"] = by_chunk(f["L0_attn_bc"][:, None])[:, :, 0].copy()

    def groups(parts, n):
        e = np.concatenate(parts, 2)
        g = np.zeros((n * GROUP, P, e.shape[2]), np.float32)
        g[:len(e)] = e
        out = np.zeros((n, P, (NB - 2) * w_slice(e.shape[2])), np.float32)
        out[:, :, :GROUP * e.shape[2]] = g.reshape(n, GROUP, P, -1).transpose(0, 2, 1, 3).reshape(n, P, -1)
        return out

    def inward(w):
        return w.reshape(-1, P, KC, P).transpose(0, 3, 2, 1).reshape(-1, P, D)

    w1 = np.concatenate([f["L0_ffn_W1"], f["L0_ffn_Ws1"].reshape(SHARED0, P, D)])
    w2 = np.concatenate([f["L0_ffn_W2"].transpose(0, 2, 1), f["L0_ffn_Ws2"].T.reshape(SHARED0, P, D)])
    a["w_e0"] = groups([inward(w1), w2], (E0 + SHARED0 + GROUP - 1) // GROUP)
    a["rw1"] = by_chunk(f["L1_ffn_w_router"])
    ins = [np.concatenate([f[e].transpose(0, 2, 1), f[sh].T.reshape(SHARED1, P, D)])
           for e, sh in (("L1_ffn_we1", "L1_ffn_ws1"), ("L1_ffn_we3", "L1_ffn_ws3"))]
    w2 = np.concatenate([f["L1_ffn_we2"], f["L1_ffn_ws2"].reshape(SHARED1, P, D)])
    a["w_e1"] = groups([inward(ins[0]), inward(ins[1]), w2], (E1 + SHARED1) // GROUP)
    m = np.zeros((P, W_MIX), np.float32)
    m[:, MIX_AT["u"]:MIX_AT["v"]] = by_chunk(f["L1_attn_Wu"].T).reshape(P, -1)
    m[:, MIX_AT["v"]:MIX_AT["g1"]] = by_chunk(f["L1_attn_Wv"].T).reshape(P, -1)
    for k in range(KC):
        at = MIX_AT["g1"] + k * P
        m[:, at:at + DG] = f["L1_attn_Wg1"].T[k * P:(k + 1) * P]
    m[:DG, MIX_AT["g2"]:] = f["L1_attn_Wg2"].T
    a["w_mix"] = m
    cols = np.zeros((P, COLS), np.float32)
    for name, x in (("bu", "L1_attn_bu"), ("bv", "L1_attn_bv"), ("bg2", "L1_attn_bg2"), ("conv_b", "L1_attn_conv_b")):
        cols[:, COL_AT[name]:COL_AT[name] + KC] = f[x].reshape(KC, P).T
    cols[:DG, COL_AT["bg1"]] = f["L1_attn_bg1"]
    for tap in range(3):
        cols[:, COL_AT[f"conv{tap}"]:COL_AT[f"conv{tap}"] + KC] = f["L1_attn_conv_w"][:, 0, tap].reshape(KC, P).T
    a["cols"] = cols
    return a


def kernel(**inputs):
    import numpy as np
    from concourse import bacc
    from concourse.bass_utils import run_bass_kernel_spmd as run

    arrays = lay_out(inputs)
    nc = bacc.Bacc("TRN2", target_bir_lowering=False, num_devices=1)
    a = {n: nc.dram_tensor(f"in_{n}", x.shape, mybir.dt.from_np(x.dtype), kind="ExternalInput").ap() for n, x in arrays.items()}
    out = nc.dram_tensor("out", (NB, P, KC, T), F32, kind="ExternalOutput").ap()
    program(nc, a, out)
    r = run(nc, [{f"in_{n}": x for n, x in arrays.items()}], core_ids=[0])
    return np.ascontiguousarray(r.results[0]["out"].transpose(0, 3, 2, 1)).reshape(NB, T, D)
```

```python
from contextlib import ExitStack, contextmanager

import concourse.bass as bass
from concourse import mybir

F32 = mybir.dt.float32
F32R = mybir.dt.float32r
ALU = mybir.AluOpType
ACT = mybir.ActivationFunctionType
AX_X = mybir.AxisListType.X

P = 128
NB, T, D = 8, 512, 256
KC = D // P
TT = T // P
NT = NB * TT
HKV, REP, DH = 8, 2, 128
E0, TOP0, G0, TOPG0 = 32, 6, 8, 4
SHARED0 = 2
SCALE0 = 2.5
E1, TOP1 = 16, 4
SHARED1 = 4
LOG0 = E0 + HKV
EPS_LN = 1e-5
EPS_NORM = 1e-6
GATE_OFFSET = 6.906768
QKV = (REP + 2) * DH
W_USED = KC * QKV + REP * D
W_SLICE = 2 * -(-W_USED // (2 * (NB - 2)))
W_ATT = W_SLICE * (NB - 2)
W_E0 = KC * P + D
W_E1 = 2 * KC * P + D
DG = D // 4
MIX_AT = {"u": 0, "v": KC * D, "g1": 2 * KC * D, "g2": 2 * KC * D + KC * P}
W_MIX = 2 * KC * D + KC * P + D
COL_AT = {"bu": 0, "bv": 2, "bg1": 4, "bg2": 5, "conv0": 7, "conv1": 9, "conv2": 11, "conv_b": 13}
COLS = 15
GROUP = 4
CHUNKS = [(0, 0, 512), (1, 512, 384), (3, 896, 128), (2, 1024, 256)]
BANKS = [(0, 512), (512, 1024), (1024, 1280)]
CAUSAL = 1280


def w_slice(w_expert):
    return 2 * -(-GROUP * w_expert // (2 * (NB - 2)))


class Steps:

    def __init__(self, sem, per):
        self.sem, self.per = sem, per

    def prime(self, engine, left=0):
        engine.sem_inc(self.sem, 2 * self.per - left)

    def __call__(self, i, k=None):
        return self.sem, i * self.per + (2 * self.per + (self.per if k is None else k))


class Space:

    def __init__(self, nc, ctx, tag):
        self.nc, self.ctx, self.tag, self.sems = nc, ctx, tag, []

    def sb(self, name, shape, dt=F32):
        return self.ctx.enter_context(self.nc.sbuf_tensor(f"{self.tag}_{name}", shape, dt))

    def ps(self, name, shape):
        return self.ctx.enter_context(self.nc.psum_tensor(f"{self.tag}_{name}", shape, F32))

    def sem(self, name):
        self.sems.append(self.ctx.enter_context(self.nc.semaphore(f"{self.tag}_{name}")))
        return self.sems[-1]

    @contextmanager
    def block(self):
        with self.nc.Block() as block:
            yield block
        for sem in self.sems:
            self.nc.gpsimd.sem_clear(sem)

    def steps(self, name, per):
        return Steps(self.sem(name), per)


def product3(pe, out, w_hi, w_lo, x_hi, x_lo, first, last):
    pe.matmul(out, w_hi, x_hi, start=first, stop=False)
    pe.matmul(out, w_lo, x_hi, start=False, stop=False)
    return pe.matmul(out, w_hi, x_lo, start=False, stop=last)


def constants(nc, c):
    with ExitStack() as ctx:
        s = Space(nc, ctx, "cst")
        filled, shaped = s.sem("filled"), s.sem("shaped")
        block = ctx.enter_context(s.block())

        @block.gpsimd
        def _(pool):
            pool.memset(c.mean[:, :], 1.0 / D)
            pool.memset(c.ones[:, :], 1.0)
            pool.memset(c.ones_r[:, :].bitcast(F32), 1.0)
            pool.memset(c.eps_ln[:, :], EPS_LN)
            pool.memset(c.eps_norm[:, :], EPS_NORM)
            pool.memset(c.ident[:, :], 0.0).then_inc(filled, 1)
            pool.memset(c.upto[:, :], 1.0).then_inc(filled, 1)
            pool.wait_ge(filled, 2)
            pool.affine_select(out=c.ident[:, :], in_=c.ident[:, :], compare_op=ALU.not_equal, fill=1.0,
                               base=0, pattern=[[-1, P]], channel_multiplier=1).then_inc(shaped, 1)
            pool.affine_select(out=c.upto[:, :], in_=c.upto[:, :], compare_op=ALU.is_ge, fill=0.0,
                               base=0, pattern=[[1, P]], channel_multiplier=-1).then_inc(shaped, 1)
            pool.wait_ge(shaped, 2)


def layernorm(nc, c, tag, rw_dram, n_log, logits, x_dram=None):
    with ExitStack() as ctx:
        s = Space(nc, ctx, tag)
        x_buf = s.sb("x", [P, 2, KC, T]) if x_dram is not None else None
        xc = s.sb("xc", [P, 2, KC, T])
        sq = s.sb("sq", [P, 2, KC, T])
        xn = s.sb("xn", [P, 2, KC, T])
        rstd = s.sb("rstd", [P, 2, T])
        newt = s.sb("newt", [P, T])
        lgt = s.sb("lgt", [P, 2, T])
        rw = s.sb("rw", [P, KC, P])
        rw_hi = s.sb("rw_hi", [P, KC, P], F32R)
        rw_lo = s.sb("rw_lo", [P, KC, P], F32R)
        mean_ps = s.ps("mean", [P, 2, T])
        var_ps = s.ps("var", [P, 2, T])
        log_ps = s.ps("log", [P, 2, T])
        tok_ps = s.ps("tok", [P, 2, T])
        rw_cleared, rw_loaded, rw_split = s.sem("rw_cleared"), s.sem("rw_loaded"), s.sem("rw_split")
        x_loaded = [s.steps(f"x_loaded{q}", 16) for q in range(2)]
        mean_ready = s.steps("mean_ready", 1)
        centred = s.steps("centred", KC)
        squared = s.steps("squared", KC)
        var_ready = s.steps("var_ready", 1)
        ln_var = s.steps("ln_var", 1)
        rstd_raw = s.steps("rstd_raw", 1)
        newton = s.steps("newton", 4)
        normed = s.steps("normed", KC)
        hi_ready = s.steps("hi_ready", KC)
        lo_ready = s.steps("lo_ready", KC)
        log_ready = s.steps("log_ready", 1)
        log_out = s.steps("log_out", 1)
        tok_ready = s.steps("tok_ready", 1)
        tok_out = s.steps("tok_out", 1)
        block = ctx.enter_context(s.block())

        def x_row(i, par, k):
            return c.acc[:, i, k] if x_dram is None else x_buf[:, par, k]

        def walk(engine, *parts):
            head = max(lag for lag, _ in parts)
            head += head % 2

            def step(row):
                for lag, part in parts:
                    if row(lag):
                        part(*row(lag))

            def fixed(i):
                step(lambda lag: (i - lag, (i - lag) // 2, (i - lag) % 2) if 0 <= i - lag < NB else None)

            for i in range(head):
                fixed(i)
            with engine.Fori(head // 2, NB // 2) as pair:
                for par in range(2):
                    step(lambda lag: (pair * 2 + (par - lag), pair + (par - lag) // 2, (par - lag) % 2))
            for i in range(NB, NB + head):
                fixed(i)

        @block.sync
        def _(sp):
            [q.prime(sp) for q in x_loaded]

            def load(i, pair, par):
                sp.wait_ge(*centred(i - 2))
                sp.dma_start(x_buf[:, par], x_dram[i]).then_inc(x_loaded[par].sem, 16)

            if x_dram is not None:
                load(0, 0, 0)
                load(1, 0, 1)
            sp.wait_ge(rw_cleared, 1)
            sp.dma_start(rw[:, :, 0:n_log], rw_dram).then_inc(rw_loaded, 16)
            if x_dram is not None:
                with sp.Fori(1, NB // 2) as pair:
                    for par in range(2):
                        load(pair * 2 + par, pair, par)

        @block.tensor
        def _(pe):
            for counter in (mean_ready, var_ready, log_ready, tok_ready):
                counter.prime(pe)

            def mean(i, pair, par):
                if x_dram is not None:
                    pe.wait_ge(*x_loaded[par](pair))
                pe.wait_ge(*centred(i - 2))
                for k in range(KC):
                    mm = pe.matmul(mean_ps[:, par], c.mean[:, :], x_row(i, par, k), start=(k == 0), stop=(k == KC - 1))
                mm.then_inc(mean_ready.sem, 1)

            def variance(i, pair, par):
                pe.wait_ge(*squared(i))
                pe.wait_ge(*newton(i - 2))
                for k in range(KC):
                    mm = pe.matmul(var_ps[:, par], c.mean[:, :], sq[:, par, k], start=(k == 0), stop=(k == KC - 1))
                mm.then_inc(var_ready.sem, 1)

            def log_product(i, pair, par):
                pe.wait_ge(rw_split, 2)
                pe.wait_ge(*hi_ready(i))
                pe.wait_ge(*lo_ready(i))
                pe.wait_ge(*log_out(i - 2))
                for k in range(KC):
                    mm = product3(pe, log_ps[:, par], rw_hi[:, k], rw_lo[:, k], c.xn_hi[:, i, k], c.xn_lo[:, i, k],
                                  k == 0, k == KC - 1)
                mm.then_inc(log_ready.sem, 1)

            def turn_logits(i, pair, par):
                pe.wait_ge(*log_out(i))
                pe.wait_ge(*tok_out(i - 2))
                for j in range(TT):
                    mm = pe.transpose(tok_ps[:, par, j * P:(j + 1) * P], lgt[:, par, j * P:(j + 1) * P], c.ident[:, :])
                mm.then_inc(tok_ready.sem, 1)

            walk(pe, (0, mean), (4, turn_logits), (1, variance), (3, log_product))

        @block.vector
        def _(dve):
            for counter in (centred, newton, normed, tok_out):
                counter.prime(dve)
            dve.wait_ge(rw_split, 1)
            dve.tensor_tensor(rw_lo[:, :, :], rw[:, :, :], rw_hi[:, :, :].bitcast(F32), ALU.subtract).then_inc(rw_split, 1)
            def centre(i, pair, par):
                if x_dram is not None:
                    dve.wait_ge(*x_loaded[par](pair))
                dve.wait_ge(*mean_ready(i))
                dve.wait_ge(*squared(i - 2))
                dve.wait_ge(*normed(i - 2))
                for k in range(KC):
                    dve.tensor_tensor(xc[:, par, k], x_row(i, par, k), mean_ps[:, par], ALU.subtract).then_inc(centred.sem, 1)

            def norm(i, pair, par):
                dve.wait_ge(*rstd_raw(i))
                dve.wait_ge(*newton(i - 1))
                dve.tensor_tensor(newt[:, :], rstd[:, par], rstd[:, par], ALU.mult).then_inc(newton.sem, 1)
                dve.wait_ge(*newton(i, 1))
                dve.scalar_tensor_tensor(out=newt[:, :], in0=var_ps[:, par], scalar=EPS_LN, in1=newt[:, :],
                                         op0=ALU.add, op1=ALU.mult).then_inc(newton.sem, 1)
                dve.wait_ge(*newton(i, 2))
                dve.tensor_scalar(newt[:, :], newt[:, :], -0.5, 1.5, ALU.mult, ALU.add).then_inc(newton.sem, 1)
                dve.wait_ge(*newton(i, 3))
                dve.tensor_tensor(rstd[:, par], rstd[:, par], newt[:, :], ALU.mult).then_inc(newton.sem, 1)
                dve.wait_ge(*newton(i))
                dve.wait_ge(*hi_ready(i - 2))
                dve.wait_ge(*lo_ready(i - 2))
                for k in range(KC):
                    dve.tensor_tensor(xn[:, par, k], xc[:, par, k], rstd[:, par], ALU.mult).then_inc(normed.sem, 1)

            def take_logits(i, pair, par):
                dve.wait_ge(*tok_ready(i))
                dve.tensor_copy(logits[:, bass.ds(i * TT, TT), :],
                                tok_ps[:, par].rearrange("p (j n) -> p j n", j=TT)[:, :, 0:n_log])\
                   .then_inc(tok_out.sem, 1)

            walk(dve, (2, norm), (0, centre), (4, take_logits))

        @block.scalar
        def _(act):
            for counter in (squared, ln_var, rstd_raw, hi_ready, log_out):
                counter.prime(act)
            act.preload_act_table_set("natural_log_exp_and_others")
            act.wait_ge(rw_loaded, 16)
            act.activation(rw_hi[:, :, :], rw[:, :, :], ACT.Copy).then_inc(rw_split, 1)

            def square(i, pair, par):
                act.wait_ge(*var_ready(i - 2))
                for k in range(KC):
                    act.wait_ge(*centred(i, k + 1))
                    act.activation(sq[:, par, k], xc[:, par, k], ACT.Square).then_inc(squared.sem, 1)

            def invert(i, pair, par):
                act.wait_ge(*var_ready(i))
                act.wait_ge(*normed(i - 2))
                act.activation(rstd[:, par], var_ps[:, par], ACT.Ln, bias=c.eps_ln[:, :]).then_inc(ln_var.sem, 1)
                act.wait_ge(*ln_var(i))
                act.activation(rstd[:, par], rstd[:, par], ACT.Exp, scale=-0.5).then_inc(rstd_raw.sem, 1)

            def high(i, pair, par):
                for k in range(KC):
                    act.wait_ge(*normed(i, k + 1))
                    act.activation(c.xn_hi[:, i, k], xn[:, par, k], ACT.Copy).then_inc(hi_ready.sem, 1)

            def copy_logits(i, pair, par):
                act.wait_ge(*log_ready(i))
                act.wait_ge(*tok_ready(i - 2))
                act.activation(lgt[:, par], log_ps[:, par], ACT.Copy).then_inc(log_out.sem, 1)

            walk(act, (4, copy_logits), (3, high), (0, square), (1, invert))

        @block.gpsimd
        def _(pool):
            lo_ready.prime(pool)
            pool.memset(rw[:, :, :], 0.0).then_inc(rw_cleared, 1)

            def low(i, pair, par):
                for k in range(KC):
                    pool.wait_ge(*hi_ready(i, k + 1))
                    pool.tensor_tensor(c.xn_lo[:, i, k], xn[:, par, k], c.xn_hi[:, i, k].bitcast(F32), ALU.subtract)\
                        .then_inc(lo_ready.sem, 1)

            walk(pool, (3, low))


class Chain:

    def __init__(self, engine, sem):
        self.engine, self.sem, self.n = engine, sem, 0

    def __call__(self, instruction):
        self.n += 1
        instruction.then_inc(self.sem, 1)
        self.engine.wait_ge(self.sem, self.n)
        return self.n


def decay_logs(nc, c, logits, g_rows):
    with ExitStack() as ctx:
        s = Space(nc, ctx, "dec")
        N = NT * HKV
        z, absz, u, den, ratio, q, poly, logg = (s.sb(n, [P, N]) for n in ("z", "absz", "u", "den", "ratio", "q", "poly", "logg"))
        total = s.sb("total", [P, NB, TT, HKV])
        before = s.sb("before", [P, NB, TT, HKV])
        g = s.sb("g", [P, NB, HKV, TT])
        g_t = s.sb("g_t", [P, 2, P])
        cum_ps = s.ps("cum", [P, NB, TT, HKV])
        tot_ps = s.ps("tot", [P, NB, TT, HKV])
        turn_ps = s.ps("turn", [P, 2, P])
        absz_ready, u_ready, log_ready, sums_ready, g_ready, turned, stored = (
            s.sem(n) for n in ("absz_ready", "u_ready", "log_ready", "sums_ready", "g_ready", "turned", "stored"))
        steps = s.sem("dve_steps")
        block = ctx.enter_context(s.block())

        @block.vector
        def _(dve):
            link = Chain(dve, steps)
            link(dve.tensor_scalar(z[:, :].rearrange("p (n h) -> p n h", h=HKV), logits[:, :, E0:LOG0],
                                   GATE_OFFSET, None, ALU.add))
            dve.scalar_tensor_tensor(out=absz[:, :], in0=z[:, :], scalar=-1.0, in1=z[:, :],
                                     op0=ALU.mult, op1=ALU.max).then_inc(absz_ready, 1)
            dve.wait_ge(u_ready, 1)
            link(dve.tensor_scalar(den[:, :], u[:, :], 2.0, None, ALU.add))
            link(dve.reciprocal(den[:, :], den[:, :]))
            link(dve.tensor_tensor(ratio[:, :], u[:, :], den[:, :], ALU.mult))
            link(dve.tensor_tensor(q[:, :], ratio[:, :], ratio[:, :], ALU.mult))
            link(dve.tensor_scalar(poly[:, :], q[:, :], 1.0 / 17.0, None, ALU.mult))
            for odd in (15, 13, 11, 9, 7, 5, 3):
                link(dve.scalar_tensor_tensor(out=poly[:, :], in0=poly[:, :], scalar=1.0 / odd, in1=q[:, :],
                                              op0=ALU.add, op1=ALU.mult))
            link(dve.scalar_tensor_tensor(out=poly[:, :], in0=poly[:, :], scalar=1.0, in1=ratio[:, :],
                                          op0=ALU.add, op1=ALU.mult))
            link(dve.tensor_scalar(z[:, :], z[:, :], 0.0, None, ALU.min))
            dve.scalar_tensor_tensor(out=logg[:, :], in0=poly[:, :], scalar=-2.0, in1=z[:, :],
                                     op0=ALU.mult, op1=ALU.add).then_inc(log_ready, 1)
            dve.wait_ge(sums_ready, 2)
            link(dve.memset(before[:, :, :, :], 0.0))
            link(dve.tensor_copy(total[:, :, :, :], tot_ps[:, :, :, :]))
            for j in range(1, TT):
                link(dve.tensor_tensor(before[:, :, j], before[:, :, j - 1], total[:, :, j - 1], ALU.add))
            link(dve.tensor_tensor(g[:, :, :, :].rearrange("p b h j -> p b j h"), cum_ps[:, :, :, :], before[:, :, :, :],
                                   ALU.add))
            dve.tensor_scalar(c.neg_g[:, :], g[:, :, :, :].rearrange("p b h j -> p (b h j)"), -1.0, None,
                              ALU.mult).then_inc(g_ready, 1)
            dve.wait_ge(turned, 1)
            dve.tensor_copy(g_t[:, :, :], turn_ps[:, :, :]).then_inc(g_ready, 1)

        @block.scalar
        def _(act):
            act.preload_act_table_set("natural_log_exp_and_others")
            act.wait_ge(absz_ready, 1)
            act.activation(u[:, :], absz[:, :], ACT.Exp, scale=-1.0).then_inc(u_ready, 1)

        @block.tensor
        def _(pe):
            pe.wait_ge(log_ready, 1)
            pe.matmul(cum_ps[:, :, :, :].rearrange("p b j h -> p (b j h)"), c.upto[:, :], logg[:, :],
                      start=True, stop=True).then_inc(sums_ready, 1)
            pe.matmul(tot_ps[:, :, :, :].rearrange("p b j h -> p (b j h)"), c.ones[:, :], logg[:, :],
                      start=True, stop=True).then_inc(sums_ready, 1)
            pe.wait_ge(g_ready, 1)
            for half in range(2):
                mm = pe.transpose(turn_ps[:, half], g[:, :, :, :].rearrange("p b h j -> p (b h j)")[:, half * P:(half + 1) * P],
                                  c.ident[:, :])
            mm.then_inc(turned, 1)

        @block.sync
        def _(sp):
            sp.wait_ge(g_ready, 2)
            sp.dma_start(g_rows.rearrange("r (j t) -> (r j) t", t=P).rearrange("(a p) t -> p a t", p=P), g_t[:, :, :])\
              .then_inc(stored, 16)
            sp.wait_ge(stored, 16)


def pick_top(dve, link, values, pad_at, top8, picked, k, is_picked):
    for n in range(NT):
        dve.max(top8[:, n], values[:, n, 0:pad_at]).then_inc(link.sem, 1)
    link.n += NT
    dve.wait_ge(link.sem, link.n)
    link(dve.memset(top8[:, :, k:8], -1.0))
    for n in range(NT):
        dve.match_replace(picked[:, n], top8[:, n], values[:, n], -2.0).then_inc(link.sem, 1)
    link.n += NT
    dve.wait_ge(link.sem, link.n)
    link(dve.tensor_scalar(is_picked, picked[:, :, 0:pad_at], -2.0, None, ALU.is_equal))


def store_gates(sp, gates, g_t, n_e, tiles, stored):
    to = gates[0:n_e, :].rearrange("e (g l t) -> l e g t", l=tiles, t=P)
    for tile in range(tiles):
        sp.dma_start(to[tile], g_t[tile * n_e:(tile + 1) * n_e]).then_inc(stored, 16)


def route0(nc, c, logits, bias_row, gates):
    with ExitStack() as ctx:
        s = Space(nc, ctx, "rt0")
        GS = E0 // G0
        bias = s.sb("bias", [P, E0])
        score = s.sb("score", [P, NT, E0])
        pair = s.sb("pair", [P, NT * G0, 6])
        group = s.sb("group", [P, NT, G0 + 8])
        top8 = s.sb("top8", [P, NT, 8])
        gpick = s.sb("gpick", [P, NT, G0 + 8])
        gmask = s.sb("gmask", [P, NT, G0])
        masked = s.sb("masked", [P, NT, E0 + 8])
        epick = s.sb("epick", [P, NT, E0 + 8])
        weight = s.sb("weight", [P, NT, E0])
        norm = s.sb("norm", [P, NT])
        g_t = s.sb("g_t", [P, NB, P])
        turn_ps = s.ps("turn", [P, NB, P])
        loaded, logit_ready, score_ready, gates_ready, turned, g_t_ready, stored = (
            s.sem(n) for n in ("loaded", "logit_ready", "score_ready", "gates_ready", "turned", "g_t_ready", "stored"))
        steps = s.sem("dve_steps")
        block = ctx.enter_context(s.block())

        @block.scalar
        def _(act):
            act.wait_ge(logit_ready, 1)
            act.activation(score[:, :, :], weight[:, :, :], ACT.Sigmoid).then_inc(score_ready, 1)

        @block.vector
        def _(dve):
            link = Chain(dve, steps)
            link(dve.memset(group[:, :, :], -1.0))
            link(dve.memset(masked[:, :, :], -1.0))
            dve.wait_ge(loaded, 16)
            dve.tensor_tensor(weight[:, :, :], logits[:, :, 0:E0], bias[:, :].unsqueeze(1).to_broadcast([P, NT, E0]),
                              ALU.add).then_inc(logit_ready, 1)
            dve.wait_ge(score_ready, 1)
            four = score[:, :, :].rearrange("p n (g e) -> p (n g) e", e=GS)
            link(dve.tensor_tensor(pair[:, :, 0:2], four[:, :, 0:2], four[:, :, 2:4], ALU.add))
            link(dve.tensor_tensor(pair[:, :, 2:4], four[:, :, 0:4:2], four[:, :, 1:4:2], ALU.add))
            link(dve.tensor_tensor(pair[:, :, 4:5], four[:, :, 0:1], four[:, :, 3:4], ALU.add))
            link(dve.tensor_tensor(pair[:, :, 5:6], four[:, :, 1:2], four[:, :, 2:3], ALU.add))
            link(dve.tensor_reduce(group[:, :, 0:G0], pair[:, :, :].rearrange("p (n g) e -> p n g e", g=G0), AX_X, ALU.max))
            pick_top(dve, link, group, G0, top8, gpick, TOPG0, gmask[:, :, :])
            link(dve.tensor_tensor(masked[:, :, 0:E0].rearrange("p n (g e) -> p n g e", e=GS),
                                   score[:, :, :].rearrange("p n (g e) -> p n g e", e=GS),
                                   gmask[:, :, :].unsqueeze(3).to_broadcast([P, NT, G0, GS]), ALU.mult))
            pick_top(dve, link, masked, E0, top8, epick, TOP0, weight[:, :, :])
            link(dve.tensor_tensor(weight[:, :, :], weight[:, :, :], score[:, :, :], ALU.mult))
            link(dve.tensor_reduce(norm[:, :], weight[:, :, :], AX_X, ALU.add))
            link(dve.tensor_scalar(norm[:, :], norm[:, :], 1e-20, None, ALU.add))
            link(dve.reciprocal(norm[:, :], norm[:, :]))
            link(dve.tensor_tensor(weight[:, :, :], weight[:, :, :], norm[:, :].unsqueeze(2).to_broadcast([P, NT, E0]), ALU.mult))
            dve.tensor_scalar(weight[:, :, :], weight[:, :, :], SCALE0, None, ALU.mult).then_inc(gates_ready, 1)
            dve.wait_ge(turned, 1)
            dve.tensor_copy(g_t[:, :, :], turn_ps[:, :, :]).then_inc(g_t_ready, 1)

        @block.tensor
        def _(pe):
            pe.wait_ge(gates_ready, 1)
            for b in range(NB):
                mm = pe.transpose(turn_ps[:, b], weight[:, b * TT:(b + 1) * TT].rearrange("p n e -> p (n e)"), c.ident[:, :])
            mm.then_inc(turned, 1)

        @block.sync
        def _(sp):
            sp.dma_start(bias[:, :], bias_row.to_broadcast([P, E0])).then_inc(loaded, 16)
            sp.dma_start(gates[E0:E0 + SHARED0, :].rearrange("e (n t) -> (e n) t", t=P), c.ones[0:SHARED0 * NT, :])\
              .then_inc(stored, 16)
            sp.wait_ge(g_t_ready, 1)
            store_gates(sp, gates, g_t, E0, TT, stored)
            sp.wait_ge(stored, 16 * (1 + TT))


def attention(nc, c, weights, g_rows):
    TILES = len(BANKS)
    with ExitStack() as ctx:
        s = Space(nc, ctx, "att")
        w_hi = s.sb("w_hi", [P, 2, W_ATT], F32R)
        w_lo = s.sb("w_lo", [P, 2, W_ATT], F32R)
        w_raw = s.sb("w_raw", [P, W_SLICE])
        qk_hi = s.sb("qk_hi", [P, REP + 1, T], F32R)
        qk_lo = s.sb("qk_lo", [P, REP + 1, T], F32R)
        v_feat = s.sb("v_feat", [P, T])
        v_hi = s.sb("v_hi", [P, T], F32R)
        v_lo = s.sb("v_lo", [P, T], F32R)
        g_all = s.sb("g_all", [P, T])
        decay = s.sb("decay", [P, CAUSAL])
        a = s.sb("a", [P, REP, CAUSAL])
        a_hi = s.sb("a_hi", [P, REP, CAUSAL], F32R)
        a_lo = s.sb("a_lo", [P, REP, CAUSAL], F32R)
        a_sum = s.sb("a_sum", [P, T - P])
        sum_hi = s.sb("sum_hi", [P, T - P], F32R)
        sum_lo = s.sb("sum_lo", [P, T - P], F32R)
        inv = s.sb("inv", [P, T])
        fix = s.sb("fix", [P, T])
        y = s.sb("y", [P, T])
        y_hi = s.sb("y_hi", [P, REP, T], F32R)
        y_lo = s.sb("y_lo", [P, REP, T], F32R)
        work_ps = s.ps("work", [P, 3, T])
        score_ps = s.ps("score", [P, 2, T])
        y_ps = s.ps("y_ps", [P, REP, T])
        norm_ps = s.ps("norm", [P, T])

        cleared, cleared_ps, acc_cleared, mask_begun = (s.sem(n) for n in ("cleared", "cleared_ps", "acc_cleared", "mask_begun"))
        w0_loaded, w0_hi_ready = s.sem("w0_loaded"), s.sem("w0_hi_ready")
        w_loaded = s.steps("w_loaded", 16 * (NB - 2))
        w_hi_ready = s.steps("w_hi_ready", NB - 2)
        w_ready = s.steps("w_ready", NB - 2)
        g_loaded = s.steps("g_loaded", 16)
        decay_raw = s.steps("decay_raw", 1)
        decay_ready = s.steps("decay_ready", 1)
        qk_proj = s.steps("qk_proj", REP + 1)
        qk_hi_ready = s.steps("qk_hi_ready", REP + 1)
        qk_ready = s.steps("qk_ready", REP + 1)
        v_proj = s.steps("v_proj", 1)
        v_copied = s.steps("v_copied", 1)
        v_turned = s.steps("v_turned", 1)
        v_hi_ready = s.steps("v_hi_ready", 1)
        v_ready = s.steps("v_ready", 1)
        scored = s.steps("scored", REP * TILES)
        squared = s.steps("squared", REP * TILES)
        decayed = s.steps("decayed", REP * TILES)
        a_hi_ready = s.steps("a_hi_ready", REP * TILES)
        a_ready = s.steps("a_ready", REP * TILES)
        chunks_added = s.steps("chunks_added", REP * (TT - 1))
        sum_hi_ready = s.steps("sum_hi_ready", REP)
        sum_ready = s.steps("sum_ready", REP)
        summed = s.steps("summed", REP)
        logged = s.steps("logged", REP)
        inv_raw = s.steps("inv_raw", REP)
        fixed = s.steps("fixed", 3 * REP)
        y_hi_ready = s.steps("y_hi_ready", REP)
        y_ready = s.steps("y_ready", REP)
        mixed = s.steps("mixed", KC)
        added = s.steps("added", KC)
        block = ctx.enter_context(s.block())

        def col(w, par, part, k=0):
            at = {"q0": 0, "q1": DH, "k": REP * DH, "v": (REP + 1) * DH}
            if part in at:
                return w[:, par, k * QKV + at[part]:k * QKV + at[part] + DH]
            q, chunk = part
            at = KC * QKV + q * D + chunk * P
            return w[:, par, at:at + P]

        def walk(engine, unit):
            with engine.Fori(0, HKV // 2) as pair:
                for par in range(2):
                    i0 = pair * (2 * NB) + par * NB
                    unit(i0, 0, par, pair, (i0 + 1, 1, par), (i0 - 1, NB - 1, 1 - par))
                    with engine.Fori(1, NB - 1) as b:
                        unit(i0 + b, b, par, pair, (i0 + b + 1, b + 1, par), (i0 + b - 1, b - 1, par))
                    unit(i0 + (NB - 1), NB - 1, par, pair, (i0 + NB, 0, 1 - par), (i0 + (NB - 2), NB - 2, par))

        LAST = HKV * NB - 1

        def next_head(pair, par, nxt):
            return pair * 2 + (par + 1 if first_row(nxt[1]) else par)

        def first_row(b):
            return isinstance(b, int) and b == 0

        def middle(b):
            return not isinstance(b, int)

        @block.sync
        def _(sp):
            w_loaded.prime(sp, left=-16 * (NB - 2))
            g_loaded.prime(sp)

            def load_w(h, b):
                sp.wait_ge(*w_ready(h, b - 1))
                sp.dma_start(w_raw[:, :], weights[h, :, bass.ds((b - 1) * W_SLICE, W_SLICE)]).then_inc(w_loaded.sem, 16)

            def load_g(i, b, h):
                sp.wait_ge(*decay_raw(i - 1))
                sp.dma_start(g_all[:, :], g_rows[bass.ds(b * HKV + h, 1), :].to_broadcast([P, T])).then_inc(g_loaded.sem, 16)

            sp.dma_start(a[:, :, :].rearrange("p q n -> p (q n)")[:, 0:W_USED], weights[0, :, 0:W_USED]).then_inc(w0_loaded, 16)
            load_g(0, 0, 0)

            def unit(i, b, par, pair, nxt, prev):
                if middle(b):
                    load_w(pair * 2 + (par + 1), b)
                load_g(nxt[0], nxt[1], next_head(pair, par, nxt))

            walk(sp, unit)

        @block.tensor
        def _(pe):
            for counter in (qk_proj, v_proj, v_turned, scored, summed):
                counter.prime(pe)
            mixed.prime(pe, left=KC)

            def project(i, b, par, part, n, chunks=range(KC)):
                bank = {"q0": 2, "q1": 0, "k": 1, "v": 2}[part]
                for k in chunks:
                    mm = product3(pe, work_ps[:, bank], col(w_hi, par, part, k), col(w_lo, par, part, k),
                                  c.xn_hi[:, b, k], c.xn_lo[:, b, k], k == 0, k == KC - 1)
                if k == KC - 1:
                    mm.then_inc(n.sem, 1)

            def project_q0(i, b, par, chunks=range(KC)):
                pe.wait_ge(*v_copied(i - 1))
                project(i, b, par, "q0", qk_proj, chunks)

            def project_v_q1_k(i, b, par, last_out):
                pe.wait_ge(*qk_ready(i, 1))
                project(i, b, par, "v", v_proj)
                pe.wait_ge(*v_ready(i - 1))
                pe.wait_ge(*added(last_out, 1))
                project(i, b, par, "q1", qk_proj)
                pe.wait_ge(*added(last_out))
                project(i, b, par, "k", qk_proj)

            def turn_v(i):
                pe.wait_ge(*qk_ready(i, 2))
                pe.wait_ge(*v_copied(i))
                for j in range(TT):
                    mm = pe.transpose(work_ps[:, 0, j * P:(j + 1) * P], v_feat[:, j * P:(j + 1) * P], c.ident[:, :])
                mm.then_inc(v_turned.sem, 1)

            def output(i, par, last_proj):
                pe.wait_ge(*v_ready(last_proj))
                pe.wait_ge(*qk_ready(last_proj))
                for q in range(REP):
                    pe.wait_ge(*y_ready(i, q + 1))
                    for chunk in range(KC):
                        mm = product3(pe, work_ps[:, chunk], col(w_hi, par, (q, chunk)), col(w_lo, par, (q, chunk)),
                                      y_hi[:, q], y_lo[:, q], q == 0, q == REP - 1)
                        if q == REP - 1:
                            mm.then_inc(mixed.sem, 1)

            def scores(i, q, tiles=range(TILES)):
                pe.wait_ge(*qk_ready(i))
                for tile in tiles:
                    lo, hi = BANKS[tile]
                    n = q * TILES + tile
                    pe.wait_ge(*(squared(i, n - 1) if n >= 2 else squared(i - 1, REP * TILES + n - 1)))
                    for j, at, width in CHUNKS:
                        if lo <= at < hi:
                            keys, t0 = slice(j * P, (j + 1) * P), T - width
                            mm = product3(pe, score_ps[:, n % 2, at - lo:at - lo + width],
                                          qk_hi[:, REP, keys], qk_lo[:, REP, keys],
                                          qk_hi[:, q, t0:T], qk_lo[:, q, t0:T], True, True)
                    mm.then_inc(scored.sem, 1)

            def weigh(i, q):
                pe.wait_ge(*v_ready(i))
                pe.wait_ge(*fixed(i - 1, 3 * q + 3))
                pe.wait_ge(*(fixed(i, 1) if q else fixed(i - 1, 4)))
                for tile, (lo, hi) in enumerate(BANKS):
                    pe.wait_ge(*a_ready(i, q * TILES + tile + 1))
                    for j, at, width in CHUNKS:
                        if lo <= at < hi:
                            keys, t0 = slice(j * P, (j + 1) * P), T - width
                            first, last = j == 0, j == 2
                            product3(pe, y_ps[:, q, t0:T], v_hi[:, keys], v_lo[:, keys],
                                     a_hi[:, q, at:at + width], a_lo[:, q, at:at + width], first, last)
                pe.matmul(norm_ps[:, 0:P], c.ones_r[:, :], a_hi[:, q, 0:P], start=True, stop=False)
                pe.matmul(norm_ps[:, 0:P], c.ones_r[:, :], a_lo[:, q, 0:P], start=False, stop=True)
                pe.wait_ge(*sum_ready(i, q + 1))
                pe.matmul(norm_ps[:, P:T], c.ones_r[:, :], sum_hi[:, :], start=True, stop=False)
                pe.matmul(norm_ps[:, P:T], c.ones_r[:, :], sum_lo[:, :], start=False, stop=True).then_inc(summed.sem, 1)

            pe.wait_ge(*w_ready(0))
            project_q0(0, 0, 0)
            pe.wait_ge(*v_ready(-1))
            project(0, 0, 0, "q1", qk_proj)
            project(0, 0, 0, "k", qk_proj)
            pe.wait_ge(*qk_ready(0, 1))
            project(0, 0, 0, "v", v_proj)
            turn_v(0)
            scores(0, 0)
            pe.wait_ge(cleared, 1)
            pe.wait_ge(cleared_ps, 1)

            def unit(i, b, par, pair, nxt, prev):
                if first_row(nxt[1]):
                    pe.wait_ge(*w_ready(next_head(pair, par, nxt)))
                project_q0(*nxt, (0,))
                scores(i, 1, (0, 1))
                project_q0(*nxt, (1,))
                scores(i, 1, (2,))
                weigh(i, 0)
                output(prev[0], prev[2], i)
                project_v_q1_k(*nxt, prev[0])
                weigh(i, 1)
                scores(nxt[0], 0, (0, 1))
                turn_v(nxt[0])
                scores(nxt[0], 0, (2,))

            walk(pe, unit)
            output(LAST, (HKV - 1) % 2, LAST + 1)

        @block.scalar
        def _(act):
            w_hi_ready.prime(act, left=2 - NB)
            for counter in (sum_hi_ready, decay_raw, qk_hi_ready, v_copied, v_hi_ready, squared, logged, inv_raw):
                counter.prime(act)
            y_hi_ready.prime(act, left=1)
            act.preload_act_table_set("natural_log_exp_and_others")

            def split_w(h, par, b, last_out):
                act.wait_ge(*w_loaded(h, 16 * b))
                act.wait_ge(*mixed(last_out))
                act.activation(w_hi[:, par, bass.ds((b - 1) * W_SLICE, W_SLICE)], w_raw[:, :], ACT.Copy)\
                   .then_inc(w_hi_ready.sem, 1)

            def decays(i, b, h):
                act.wait_ge(*g_loaded(i))
                act.wait_ge(*decayed(i - 1))
                for j, at, width in CHUNKS:
                    ins = act.activation(decay[:, at:at + width], g_all[:, T - width:T], ACT.Exp,
                                         bias=c.neg_g[:, bass.ds(b * (HKV * TT) + h * TT + j, 1)])
                ins.then_inc(decay_raw.sem, 1)

            def qk_high(i, n):
                act.wait_ge(*qk_proj(i, n + 1))
                act.wait_ge(*scored(i - 1))
                act.activation(qk_hi[:, n], work_ps[:, {0: 2, 1: 0, 2: 1}[n]], ACT.Copy).then_inc(qk_hi_ready.sem, 1)

            def v_copy(i):
                act.wait_ge(*v_proj(i))
                act.wait_ge(*v_turned(i - 1))
                act.activation(v_feat[:, :], work_ps[:, 2], ACT.Copy).then_inc(v_copied.sem, 1)

            def v_high(i):
                act.wait_ge(*v_turned(i))
                act.wait_ge(*summed(i - 1))
                act.activation(v_hi[:, :], work_ps[:, 0], ACT.Copy).then_inc(v_hi_ready.sem, 1)

            def square(i, q, tile):
                lo, hi = BANKS[tile]
                n = q * TILES + tile
                act.wait_ge(*scored(i, n + 1))
                act.wait_ge(*a_ready(i - 1, n + 1))
                act.wait_ge(*chunks_added(i - 1, (q + 1) * (TT - 1)))
                act.activation(a[:, q, lo:hi], score_ps[:, n % 2, 0:hi - lo], ACT.Square,
                               scale=DH ** -0.5).then_inc(squared.sem, 1)

            def sum_high(i, q):
                act.wait_ge(*chunks_added(i, (q + 1) * (TT - 1)))
                act.wait_ge(*(summed(i, 1) if q else summed(i - 1)))
                act.activation(sum_hi[:, :], a_sum[:, :], ACT.Copy).then_inc(sum_hi_ready.sem, 1)

            def log_norm(i, q):
                act.wait_ge(*summed(i, q + 1))
                act.wait_ge(*(fixed(i, 2) if q else fixed(i - 1, 5)))
                act.activation(inv[:, :], norm_ps[:, :], ACT.Ln, bias=c.eps_norm[:, :]).then_inc(logged.sem, 1)

            def invert(i, q):
                act.wait_ge(*logged(i, q + 1))
                act.activation(inv[:, :], inv[:, :], ACT.Exp, scale=-1.0).then_inc(inv_raw.sem, 1)

            def y_high(i, q):
                act.wait_ge(*fixed(i, 3 * q + 3))
                act.wait_ge(*mixed(i - 1))
                act.activation(y_hi[:, q], y[:, :], ACT.Copy).then_inc(y_hi_ready.sem, 1)

            act.wait_ge(w0_loaded, 16)
            act.activation(w_hi[:, 0, 0:W_USED], a[:, :, :].rearrange("p q n -> p (q n)")[:, 0:W_USED], ACT.Copy).then_inc(w0_hi_ready, 1)
            decays(0, 0, 0)
            for n in range(REP + 1):
                qk_high(0, n)
            v_copy(0)
            v_high(0)
            for tile in range(TILES):
                square(0, 0, tile)

            def unit(i, b, par, pair, nxt, prev):
                for tile in range(TILES):
                    square(i, 1, tile)
                sum_high(i, 0)
                y_high(prev[0], 1)
                qk_high(nxt[0], 0)
                log_norm(i, 0)
                invert(i, 0)
                decays(nxt[0], nxt[1], next_head(pair, par, nxt))
                sum_high(i, 1)
                v_copy(nxt[0])
                qk_high(nxt[0], 1)
                y_high(i, 0)
                qk_high(nxt[0], 2)
                if middle(b):
                    split_w(pair * 2 + (par + 1), 1 - par, b, i - 2)
                log_norm(i, 1)
                square(nxt[0], 0, 0)
                square(nxt[0], 0, 1)
                v_high(nxt[0])
                invert(i, 1)
                square(nxt[0], 0, 2)

            walk(act, unit)
            y_high(LAST, 1)

        @block.vector
        def _(dve):
            for counter in (qk_ready, v_ready, a_hi_ready, a_ready, sum_ready):
                counter.prime(dve)
            fixed.prime(dve, left=3)
            y_ready.prime(dve, left=1)
            added.prime(dve, left=KC)
            dve.memset(y_ps[:, 1], 0.0)
            dve.memset(norm_ps[:, :], 1.0).then_inc(cleared_ps, 1)
            dve.memset(c.acc[:, :, :, :], 0.0).then_inc(acc_cleared, 1)
            dve.wait_ge(cleared_ps, 1)
            dve.wait_ge(acc_cleared, 1)
            dve.wait_ge(cleared, 1)

            def qk_low(i, n):
                dve.wait_ge(*qk_hi_ready(i, n + 1))
                dve.tensor_tensor(qk_lo[:, n], work_ps[:, {0: 2, 1: 0, 2: 1}[n]], qk_hi[:, n].bitcast(F32),
                                  ALU.subtract).then_inc(qk_ready.sem, 1)

            def v_low(i):
                dve.wait_ge(*v_hi_ready(i))
                dve.tensor_tensor(v_lo[:, :], work_ps[:, 0], v_hi[:, :].bitcast(F32), ALU.subtract).then_inc(v_ready.sem, 1)

            def split_a(i, q, tile):
                lo, hi = BANKS[tile]
                n = q * TILES + tile
                dve.wait_ge(*decayed(i, n + 1))
                dve.wait_ge(*summed(i - 1, q + 1))
                dve.tensor_copy(a_hi[:, q, lo:hi], a[:, q, lo:hi]).then_inc(a_hi_ready.sem, 1)
                dve.wait_ge(*a_hi_ready(i, n + 1))
                dve.tensor_tensor(a_lo[:, q, lo:hi], a[:, q, lo:hi], a_hi[:, q, lo:hi].bitcast(F32),
                                  ALU.subtract).then_inc(a_ready.sem, 1)

            def sum_low(i, q):
                dve.wait_ge(*sum_hi_ready(i, q + 1))
                dve.tensor_tensor(sum_lo[:, :], a_sum[:, :], sum_hi[:, :].bitcast(F32), ALU.subtract).then_inc(sum_ready.sem, 1)

            def fix_a(i, q):
                dve.wait_ge(*inv_raw(i, q + 1))
                dve.wait_ge(*(fixed(i, 3) if q else fixed(i - 1)))
                dve.scalar_tensor_tensor(out=fix[:, :], in0=norm_ps[:, :], scalar=EPS_NORM, in1=inv[:, :],
                                         op0=ALU.add, op1=ALU.mult).then_inc(fixed.sem, 1)

            def fix_b(i, q):
                dve.wait_ge(*fixed(i, 3 * q + 1))
                dve.scalar_tensor_tensor(out=fix[:, :], in0=fix[:, :], scalar=-2.0, in1=inv[:, :],
                                         op0=ALU.add, op1=ALU.mult).then_inc(fixed.sem, 1)

            def divide(i, q):
                dve.wait_ge(*fixed(i, 3 * q + 2))
                dve.wait_ge(*(y_ready(i, 1) if q else y_ready(i - 1)))
                dve.scalar_tensor_tensor(out=y[:, :], in0=y_ps[:, q], scalar=-1.0, in1=fix[:, :],
                                         op0=ALU.mult, op1=ALU.mult).then_inc(fixed.sem, 1)

            def y_low(i):
                dve.wait_ge(*y_hi_ready(i))
                dve.tensor_tensor(y_lo[:, 1], y[:, :], y_hi[:, 1].bitcast(F32), ALU.subtract).then_inc(y_ready.sem, 1)

            def add(i, b, chunk):
                dve.wait_ge(*mixed(i, chunk + 1))
                dve.tensor_tensor(c.acc[:, b, chunk], c.acc[:, b, chunk], work_ps[:, chunk], ALU.add).then_inc(added.sem, 1)

            for n in range(REP + 1):
                qk_low(0, n)
            v_low(0)

            def unit(i, b, par, pair, nxt, prev):
                fix_a(prev[0], 1)
                split_a(i, 0, 0)
                split_a(i, 0, 1)
                fix_b(prev[0], 1)
                divide(prev[0], 1)
                split_a(i, 0, 2)
                sum_low(i, 0)
                y_low(prev[0])
                qk_low(nxt[0], 0)
                split_a(i, 1, 0)
                split_a(i, 1, 1)
                add(prev[0], prev[1], 0)
                add(prev[0], prev[1], 1)
                split_a(i, 1, 2)
                fix_a(i, 0)
                fix_b(i, 0)
                divide(i, 0)
                sum_low(i, 1)
                qk_low(nxt[0], 1)
                qk_low(nxt[0], 2)
                v_low(nxt[0])

            walk(dve, unit)
            fix_a(LAST, 1)
            fix_b(LAST, 1)
            divide(LAST, 1)
            y_low(LAST)
            for chunk in range(KC):
                add(LAST, NB - 1, chunk)

        @block.gpsimd
        def _(pool):
            for counter in (w_ready, decay_ready, decayed, chunks_added):
                counter.prime(pool)
            for zero in (y_hi[:, 0].bitcast(F32), y_lo[:, 0].bitcast(F32), w_hi[:, 1].bitcast(F32), w_lo[:, 1].bitcast(F32)):
                pool.memset(zero, 0.0)
            pool.memset(inv[:, :], 1.0).then_inc(cleared, 1)

            def split_w(h, par, b):
                pool.wait_ge(*w_hi_ready(h, b))
                cols = bass.ds((b - 1) * W_SLICE, W_SLICE)
                pool.tensor_tensor(w_lo[:, par, cols], w_raw[:, :], w_hi[:, par, cols].bitcast(F32), ALU.subtract)\
                    .then_inc(w_ready.sem, 1)

            def y_low(i):
                pool.wait_ge(*y_hi_ready(i, 1))
                pool.tensor_tensor(y_lo[:, 0], y[:, :], y_hi[:, 0].bitcast(F32), ALU.subtract).then_inc(y_ready.sem, 1)

            def mask(i):
                pool.wait_ge(*decay_raw(i))
                pool.sem_inc(mask_begun, 1)
                for j, at, width in CHUNKS:
                    ins = pool.affine_select(out=decay[:, at:at + P], in_=decay[:, at:at + P], compare_op=ALU.is_ge,
                                             fill=0.0, base=0, pattern=[[1, P]], channel_multiplier=-1)
                ins.then_inc(decay_ready.sem, 1)

            def apply_decay(i, q):
                if q == 0:
                    pool.wait_ge(*decay_ready(i))
                for tile, (lo, hi) in enumerate(BANKS):
                    n = q * TILES + tile
                    pool.wait_ge(*squared(i, n + 1))
                    pool.tensor_tensor(a[:, q, lo:hi], a[:, q, lo:hi], decay[:, lo:hi], ALU.mult)\
                        .then_inc(decayed.sem, 1)

            def add_chunks(i, q):
                pool.wait_ge(*decayed(i, (q + 1) * TILES))
                pool.wait_ge(*(sum_ready(i, 1) if q else sum_ready(i - 1)))
                for n, (j, at, width) in enumerate(CHUNKS[1:]):
                    there = slice(T - P - width, T - P)
                    before = a_sum[:, there]
                    if n == 0:
                        before = a[:, q, P:T]
                    else:
                        pool.wait_ge(*chunks_added(i, q * (TT - 1) + n))
                    pool.tensor_tensor(a_sum[:, there], before, a[:, q, at:at + width], ALU.add).then_inc(chunks_added.sem, 1)

            pool.wait_ge(w0_hi_ready, 1)
            pool.tensor_tensor(w_lo[:, 0, 0:W_USED], a[:, :, :].rearrange("p q n -> p (q n)")[:, 0:W_USED], w_hi[:, 0, 0:W_USED].bitcast(F32),
                               ALU.subtract).then_inc(w_ready.sem, NB - 2)
            mask(0)
            apply_decay(0, 0)

            def unit(i, b, par, pair, nxt, prev):
                add_chunks(i, 0)
                apply_decay(i, 1)
                add_chunks(i, 1)
                mask(nxt[0])
                y_low(i)
                if middle(b):
                    split_w(pair * 2 + (par + 1), 1 - par, b)
                apply_decay(nxt[0], 0)

            walk(pool, unit)


def experts(nc, c, tag, weights, gates, n_full, last_size, swiglu, mixer, x_in, x_out, bias_in=None):
    NZ = 2 if swiglu else 1
    W_E = W_E1 if swiglu else W_E0
    W_SL = w_slice(W_E)
    W_G = W_SL * (NB - 2)
    ZB = 4
    AHEAD = ZB // NZ
    with ExitStack() as ctx:
        s = Space(nc, ctx, tag)
        w_hi = s.sb("w_hi", [P, 2, W_G], F32R)
        w_lo = s.sb("w_lo", [P, 2, W_G], F32R)
        w_raw = s.sb("w_raw", [P, W_SL])
        shared_buf = s.sb("shared_buf", [P, 2, 2, KC * T])
        w_first = shared_buf[:, :, :, :].rearrange("p q r n -> p (q r n)")[:, 0:GROUP * W_E].rearrange("p (e n) -> p e n", e=GROUP)
        m_buf = [shared_buf[:, 0, q].rearrange("p (k t) -> p k t", k=KC) for q in range(2)]
        x_buf = [shared_buf[:, 1, q].rearrange("p (k t) -> p k t", k=KC) for q in range(2)]
        bias = s.sb("bias", [P, KC])
        gate = s.sb("gate", [P, 2, GROUP, T])
        act_gate = s.sb("act_gate", [P, 2, T])
        h = s.sb("h", [P, 2, T])
        h_hi = s.sb("h_hi", [P, GROUP, T], F32R)
        h_lo = s.sb("h_lo", [P, GROUP, T], F32R)
        z_ps = s.ps("z", [P, ZB, T])
        out_ps = s.ps("out", [P, 2, KC, T])
        acc_parts = [(NB - 1, NB), (0, 1), (1, NB - 1)]
        mixer_stored = [s.sem(f"mixer_stored{n}") for n in range(len(acc_parts))]
        cleared, cleared_ps = s.sem("acc_cleared"), s.sem("cleared_ps")
        w0_loaded = [s.sem(f"w0_loaded{e}") for e in range(GROUP)]
        w0_hi_ready, w0_ready = s.sem("w0_hi_ready"), s.sem("w0_ready")
        w_loaded = s.steps("w_loaded", 16 * (NB - 2))
        w_hi_ready = s.steps("w_hi_ready", NB - 2)
        w_ready = s.steps("w_ready", NB - 2)
        g_loaded = [s.steps(f"g_loaded{q}", 16) for q in range(2)]
        projected = s.steps("projected", GROUP)
        silu_ready = s.steps("silu_ready", GROUP)
        act_ready = s.steps("act_ready", GROUP)
        h_ready = s.steps("h_ready", GROUP)
        h_hi_ready = s.steps("h_hi_ready", GROUP)
        h_split = s.steps("h_split", GROUP)
        used = s.steps("used", GROUP)
        added = s.steps("added", KC)
        bias_loaded = s.sem("bias_loaded")
        m_loaded = [s.steps(f"m_loaded{q}", 16) for q in range(2)]
        x_loaded = [s.steps(f"x_loaded{q}", 16) for q in range(2)]
        acc_silu = s.steps("acc_silu", 1)
        biased = s.steps("biased", KC)
        gated = s.steps("gated", 1)
        x_ready = s.steps("x_ready", 1)
        x_stored = [s.steps(f"x_stored{q}", 16) for q in range(2)]
        block = ctx.enter_context(s.block())

        def walk(engine, unit, split=None):
            def group(g, par, size, last):
                i0 = g * NB
                if last:
                    def row(b, pr, sub, nxt=True):
                        unit(i0 + b, g, b, pr, sub, par, size, (i0 + b + 1, g, b + 1, par, size) if nxt else None)

                    row(0, 0, 0)
                    row(1, 0, 1)
                    with engine.Fori(1, NB // 2 - 1) as pair:
                        row(pair * 2, pair, 0)
                        row(pair * 2 + 1, pair, 1)
                    row(NB - 2, NB // 2 - 1, 0)
                    row(NB - 1, NB // 2 - 1, 1, False)
                    return
                unit(i0, g, 0, 0, 0, par, size, (i0 + 1, g, 1, par, size))
                with engine.Fori(0, NB // 2 - 1) as pair:
                    for sub in (1, 0):
                        b = pair * 2 + (2 - sub)
                        unit(i0 + b, g, b, pair + (1 - sub), sub, par, size, (i0 + b + 1, g, b + 1, par, size))
                        if split:
                            split(g + 1, 1 - par, pair * 2 + (1 - sub), i0 - 1)
                unit(i0 + (NB - 1), g, NB - 1, NB // 2 - 1, 1, par, size, (i0 + NB, g + 1, 0, 1 - par, GROUP))

            with engine.Fori(0, n_full // 2) as two:
                for par in range(2):
                    group(two * 2 + par, par, GROUP, False)
            group(n_full, 0, last_size, True)

        LAST = n_full * NB + NB - 1

        def finished(g, b, pr, sub):
            if isinstance(g, int) and g == n_full and not (isinstance(b, int) and b < 2):
                return b - 2, pr - 1, sub
            return None

        @block.sync
        def _(sp):
            w_loaded.prime(sp, left=-16 * (NB - 2))
            for q in g_loaded:
                q.prime(sp)

            def load_w(g, par, part, last):
                sp.wait_ge(*w_ready(g, part))
                sp.dma_start(w_raw[:, :], weights[g, :, bass.ds(part * W_SL, W_SL)]).then_inc(w_loaded.sem, 16)

            def load_gates(i, g, b, sub, size):
                sp.wait_ge(*act_ready(i - 2))
                src = gates[bass.ds(g * GROUP, size), bass.ds(b * T, T)]
                sp.dma_start(gate[:, sub, 0:size], src.unsqueeze(0).to_broadcast([P, size, T])).then_inc(g_loaded[sub].sem, 16)

            def unit(i, g, b, pr, sub, par, size, nxt):
                last = isinstance(g, int) and g == n_full
                first = isinstance(b, int) and b == 0
                if not last or first:
                    load_gates(i, g, b, sub, size)
                if last:
                    if nxt:
                        load_gates(nxt[0], g, nxt[2], 1 - sub, size)
                    sp.wait_ge(*x_ready(b - 2))
                    if finished(g, b, pr, sub):
                        store(*finished(g, b, pr, sub))
                    sp.dma_start(m_buf[sub], mixer[b]).then_inc(m_loaded[sub].sem, 16)
                    sp.dma_start(x_buf[sub], x_in[b]).then_inc(x_loaded[sub].sem, 16)

            def store(r, pair, par):
                sp.wait_ge(*x_ready(r))
                sp.wait_ge(*x_stored[par](pair - 1))
                sp.dma_start(x_out[r], c.acc[:, r]).then_inc(x_stored[par].sem, 16)

            for e in range(GROUP):
                sp.dma_start(w_first[:, e], weights[0, :, e * W_E:(e + 1) * W_E]).then_inc(w0_loaded[e], 16)
            if bias_in is not None:
                sp.dma_start(bias[:, :], bias_in).then_inc(bias_loaded, 16)
            for q in m_loaded + x_loaded + x_stored:
                q.prime(sp)
            for (b0, b1), stored in zip(acc_parts, mixer_stored):
                sp.dma_start(mixer[b0:b1].rearrange("b p k t -> p b k t"), c.acc[:, b0:b1]).then_inc(stored, 16)
            for stored in mixer_stored:
                sp.wait_ge(stored, 16)
            walk(sp, unit, load_w)
            store(NB - 2, NB // 2 - 1, 0)
            store(NB - 1, NB // 2 - 1, 1)
            for q in x_stored:
                sp.wait_ge(*q(NB // 2 - 1))

        @block.tensor
        def _(pe):
            projected.prime(pe)
            used.prime(pe)

            def project(i, b, par, e, inc, inc_before):
                if e >= AHEAD:
                    pe.wait_ge(*h_ready(i, (e - AHEAD + 1) * inc))
                else:
                    experts = GROUP // inc_before
                    had_it = e + max(experts - AHEAD, 0)
                    pe.wait_ge(*h_ready(i - 1, (had_it + 1) * inc_before))
                for n in range(NZ):
                    for k in range(KC):
                        at = e * W_E + (n * KC + k) * P
                        mm = product3(pe, z_ps[:, (e * NZ + n) % ZB], w_hi[:, par, at:at + P], w_lo[:, par, at:at + P],
                                      c.xn_hi[:, b, k], c.xn_lo[:, b, k], k == 0, k == KC - 1)
                mm.then_inc(projected.sem, inc)

            def unit(i, g, b, pr, sub, par, size, nxt):
                inc = GROUP // size
                if nxt and isinstance(nxt[2], int) and nxt[2] == 0:
                    pe.wait_ge(*w_ready(nxt[1]))
                pe.wait_ge(*added(i - 2))
                for e in range(GROUP):
                    if nxt and e < nxt[4]:
                        project(nxt[0], nxt[2], nxt[3], e, GROUP // nxt[4], inc)
                    if e < size:
                        pe.wait_ge(*h_split(i, (e + 1) * inc))
                        for chunk in range(KC):
                            at = e * W_E + NZ * KC * P + chunk * P
                            mm = product3(pe, out_ps[:, sub, chunk], w_hi[:, par, at:at + P], w_lo[:, par, at:at + P],
                                          h_hi[:, e], h_lo[:, e], e == 0, e == size - 1)
                        mm.then_inc(used.sem, inc)

            for e in range(GROUP):
                pe.wait_ge(w0_ready, e + 1)
                project(0, 0, 0, e, 1, 1)
            walk(pe, unit)

        @block.scalar
        def _(act):
            w_hi_ready.prime(act, left=2 - NB)
            silu_ready.prime(act)
            h_hi_ready.prime(act)
            acc_silu.prime(act)
            biased.prime(act)
            act.preload_act_table_set("silu_and_others")

            def split_w(g, par, part, last):
                act.wait_ge(*w_loaded(g, 16 * (part + 1)))
                act.wait_ge(*used(last))
                act.activation(w_hi[:, par, bass.ds(part * W_SL, W_SL)], w_raw[:, :], ACT.Copy).then_inc(w_hi_ready.sem, 1)

            def silu(i, e, inc):
                act.wait_ge(*projected(i, (e + 1) * inc))
                act.wait_ge(*(h_ready(i, (e - 1) * inc) if e >= 2 else h_ready(i - 1)))
                act.activation(act_gate[:, e % 2], z_ps[:, e * NZ % ZB], ACT.Silu).then_inc(silu_ready.sem, inc)

            def unit(i, g, b, pr, sub, par, size, nxt):
                inc = GROUP // size
                if finished(g, b, pr, sub):
                    finish_row(*finished(g, b, pr, sub))
                for e in range(size + 1):
                    if swiglu and e < size:
                        silu(i, e, inc)
                    if e >= 1:
                        act.wait_ge(*h_ready(i, e * inc))
                        act.wait_ge(*used(i - 1, e * inc))
                        act.activation(h_hi[:, e - 1], h[:, (e - 1) % 2], ACT.Copy).then_inc(h_hi_ready.sem, inc)

            def finish_row(r, pair, par):
                if bias_in is not None:
                    act.wait_ge(*m_loaded[par](pair))
                    for k in range(KC):
                        act.activation(m_buf[par][:, k], m_buf[par][:, k], ACT.Identity, bias=bias[:, k:k + 1])\
                           .then_inc(biased.sem, 1)
                act.wait_ge(*added(n_full * NB + r))
                act.activation(c.acc[:, r], c.acc[:, r], ACT.Silu).then_inc(acc_silu.sem, 1)

            if bias_in is not None:
                act.wait_ge(bias_loaded, 16)
            for e in range(GROUP):
                act.wait_ge(w0_loaded[e], 16)
                act.activation(w_hi[:, 0, e * W_E:(e + 1) * W_E], w_first[:, e], ACT.Copy).then_inc(w0_hi_ready, 1)
            walk(act, unit, split_w)
            finish_row(NB - 2, NB // 2 - 1, 0)
            finish_row(NB - 1, NB // 2 - 1, 1)

        @block.vector
        def _(dve):
            for counter in (h_ready, h_split) + (() if swiglu else (act_ready,)):
                counter.prime(dve)
            added.prime(dve, left=KC)
            gated.prime(dve)
            x_ready.prime(dve)
            for e in range(GROUP):
                dve.wait_ge(w0_hi_ready, e + 1)
                dve.tensor_tensor(w_lo[:, 0, e * W_E:(e + 1) * W_E], w_first[:, e],
                                  w_hi[:, 0, e * W_E:(e + 1) * W_E].bitcast(F32), ALU.subtract).then_inc(w0_ready, 1)
            dve.memset(out_ps[:, 1], 0.0).then_inc(cleared_ps, 1)
            dve.wait_ge(cleared_ps, 1)

            def low(i, e, inc):
                dve.wait_ge(*h_hi_ready(i, (e + 1) * inc))
                dve.tensor_tensor(h_lo[:, e], h[:, e % 2], h_hi[:, e].bitcast(F32), ALU.subtract).then_inc(h_split.sem, inc)

            def add(i, b, sub):
                dve.wait_ge(*used(i))
                for chunk in range(KC):
                    dve.tensor_tensor(c.acc[:, b, chunk], c.acc[:, b, chunk], out_ps[:, sub, chunk], ALU.add).then_inc(added.sem, 1)

            def unit(i, g, b, pr, sub, par, size, nxt):
                inc = GROUP // size
                if not swiglu:
                    dve.wait_ge(*g_loaded[sub](g * (NB // 2) + pr))
                for e in range(size):
                    n = (e + 1) * inc
                    z = z_ps[:, (e * NZ + NZ - 1) % ZB]
                    if swiglu:
                        dve.wait_ge(*act_ready(i, n))
                    else:
                        dve.wait_ge(*projected(i, n))
                        dve.wait_ge(*(h_ready(i, n - 2 * inc) if e >= 2 else h_ready(i - 1)))
                        dve.scalar_tensor_tensor(out=act_gate[:, e % 2], in0=z, scalar=0.0, in1=gate[:, sub, e],
                                                 op0=ALU.max, op1=ALU.mult).then_inc(act_ready.sem, inc)
                        dve.wait_ge(*act_ready(i, n))
                    dve.wait_ge(*(h_split(i, n - 2 * inc) if e >= 2 else h_split(i - 1)))
                    dve.tensor_tensor(h[:, e % 2], act_gate[:, e % 2], z, ALU.mult).then_inc(h_ready.sem, inc)
                    if e >= 1:
                        low(i, e - 1, inc)
                    if e == 1 and finished(g, b, pr, sub):
                        finish_row(*finished(g, b, pr, sub))
                low(i, size - 1, inc)
                dve.wait_ge(cleared, 1 if isinstance(b, int) and b == 0 else len(acc_parts))
                if isinstance(b, int):
                    add(i - 1, (b - 1) % NB, 1 - sub)
                else:
                    add(i - 1, b - 1, 1 - sub)

            def finish_row(r, pair, par):
                dve.wait_ge(*acc_silu(r))
                dve.wait_ge(*m_loaded[par](pair))
                if bias_in is not None:
                    dve.wait_ge(*biased(r))
                dve.tensor_tensor(m_buf[par], m_buf[par], c.acc[:, r], ALU.mult).then_inc(gated.sem, 1)
                dve.wait_ge(*gated(r))
                dve.wait_ge(*x_loaded[par](pair))
                dve.tensor_tensor(c.acc[:, r], x_buf[par], m_buf[par], ALU.add).then_inc(x_ready.sem, 1)

            walk(dve, unit)
            finish_row(NB - 2, NB // 2 - 1, 0)
            add(LAST, NB - 1, 1)
            finish_row(NB - 1, NB // 2 - 1, 1)

        @block.gpsimd
        def _(pool):
            w_ready.prime(pool, left=2 - NB)
            if swiglu:
                act_ready.prime(pool)

            def split_w(g, par, part, last):
                pool.wait_ge(*w_hi_ready(g, part + 1))
                cols = bass.ds(part * W_SL, W_SL)
                pool.tensor_tensor(w_lo[:, par, cols], w_raw[:, :], w_hi[:, par, cols].bitcast(F32), ALU.subtract)\
                    .then_inc(w_ready.sem, 1)

            def unit(i, g, b, pr, sub, par, size, nxt):
                if not swiglu:
                    return
                inc = GROUP // size
                pool.wait_ge(*g_loaded[sub](g * (NB // 2) + pr))
                for e in range(size):
                    pool.wait_ge(*silu_ready(i, (e + 1) * inc))
                    pool.tensor_tensor(act_gate[:, e % 2], act_gate[:, e % 2], gate[:, sub, e], ALU.mult)\
                        .then_inc(act_ready.sem, inc)

            for (b0, b1), stored in zip(acc_parts, mixer_stored):
                pool.wait_ge(stored, 16)
                pool.memset(c.acc[:, b0:b1], 0.0).then_inc(cleared, 1)
            walk(pool, unit, split_w)


def route1(nc, c, logits, gates):
    TILES = P // E1
    with ExitStack() as ctx:
        s = Space(nc, ctx, "rt1")
        shifted = s.sb("shifted", [P, NT, E1])
        prob = s.sb("prob", [P, NT, E1 + 8])
        top8 = s.sb("top8", [P, NT, 8])
        pick = s.sb("pick", [P, NT, E1 + 8])
        weight = s.sb("weight", [P, NT, E1])
        stat = s.sb("stat", [P, NT])
        shared = s.sb("shared", [P, P])
        g_t = s.sb("g_t", [P, NT // TILES, P])
        turn_ps = s.ps("turn", [P, NT // TILES, P])
        shifted_ready, exp_ready, shared_ready, gates_ready, turned, g_t_ready, stored = (
            s.sem(n) for n in ("shifted_ready", "exp_ready", "shared_ready", "gates_ready", "turned", "g_t_ready", "stored"))
        steps = s.sem("dve_steps")
        block = ctx.enter_context(s.block())

        @block.scalar
        def _(act):
            act.preload_act_table_set("natural_log_exp_and_others")
            act.wait_ge(shifted_ready, 1)
            act.activation(weight[:, :, :], shifted[:, :, :], ACT.Exp).then_inc(exp_ready, 1)

        @block.gpsimd
        def _(pool):
            pool.memset(shared[:, :], 1.0 / (TOP1 + 1)).then_inc(shared_ready, 1)

        @block.vector
        def _(dve):
            link = Chain(dve, steps)

            def by_tile():
                return stat[:, :].unsqueeze(2).to_broadcast([P, NT, E1])

            link(dve.memset(prob[:, :, :], -1.0))
            link(dve.tensor_reduce(stat[:, :], logits[:, :, :], AX_X, ALU.max))
            dve.tensor_tensor(shifted[:, :, :], logits[:, :, :], by_tile(), ALU.subtract).then_inc(shifted_ready, 1)
            dve.wait_ge(exp_ready, 1)
            link(dve.tensor_reduce(stat[:, :], weight[:, :, :], AX_X, ALU.add))
            link(dve.reciprocal(stat[:, :], stat[:, :]))
            link(dve.tensor_tensor(prob[:, :, 0:E1], weight[:, :, :], by_tile(), ALU.mult))
            pick_top(dve, link, prob, E1, top8, pick, TOP1, weight[:, :, :])
            link(dve.tensor_tensor(weight[:, :, :], weight[:, :, :], prob[:, :, 0:E1], ALU.mult))
            link(dve.tensor_reduce(stat[:, :], weight[:, :, :], AX_X, ALU.add))
            link(dve.reciprocal(stat[:, :], stat[:, :]))
            link(dve.tensor_tensor(weight[:, :, :], weight[:, :, :], by_tile(), ALU.mult))
            dve.tensor_scalar(weight[:, :, :], weight[:, :, :], TOP1 / (TOP1 + 1), None, ALU.mult).then_inc(gates_ready, 1)
            dve.wait_ge(turned, 1)
            dve.tensor_copy(g_t[:, :, :], turn_ps[:, :, :]).then_inc(g_t_ready, 1)

        @block.tensor
        def _(pe):
            pe.wait_ge(gates_ready, 1)
            for n in range(NT // TILES):
                mm = pe.transpose(turn_ps[:, n], weight[:, n * TILES:(n + 1) * TILES].rearrange("p n e -> p (n e)"), c.ident[:, :])
            mm.then_inc(turned, 1)

        @block.sync
        def _(sp):
            sp.wait_ge(shared_ready, 1)
            sp.dma_start(gates[E1:E1 + SHARED1, :].rearrange("e (n t) -> (e n) t", t=P), shared[0:SHARED1 * NT, :])\
              .then_inc(stored, 16)
            sp.wait_ge(g_t_ready, 1)
            store_gates(sp, gates, g_t, E1, TILES, stored)
            sp.wait_ge(stored, 16 * (1 + TILES))


def mix(nc, c, w_mix, cols):
    U, V, G1, G2 = 0, 1, 2, 3
    with ExitStack() as ctx:
        s = Space(nc, ctx, "mix")
        w_raw = s.sb("w_raw", [P, W_MIX])
        w_hi = s.sb("w_hi", [P, W_MIX], F32R)
        w_lo = s.sb("w_lo", [P, W_MIX], F32R)
        col = s.sb("col", [P, COLS])
        ones = s.sb("ones", [P, T])
        hid = s.sb("hid", [P, T])
        hid_hi = s.sb("hid_hi", [P, T], F32R)
        hid_lo = s.sb("hid_lo", [P, T], F32R)
        gate = s.sb("gate", [P, KC, T])
        u = s.sb("u", [P, KC, T])
        v = s.sb("v", [P, KC, T])
        total = s.sb("total", [P, KC, T])
        prod = s.sb("prod", [P, KC, T])
        prod_hi = s.sb("prod_hi", [P, KC, T], F32R)
        prod_lo = s.sb("prod_lo", [P, KC, T], F32R)
        xn = s.sb("xn", [P, KC, T])
        conv = s.sb("conv", [P, 2, KC, T])
        u_ps = s.ps("u_ps", [P, KC, T])
        v_ps = s.ps("v_ps", [P, KC, T])
        g_ps = s.ps("g_ps", [P, 2, T])
        out_ps = s.ps("out", [P, KC, T])
        w_loaded, w_hi_ready, w_ready, col_loaded, ones_ready = (
            s.sem(n) for n in ("w_loaded", "w_hi_ready", "w_ready", "col_loaded", "ones_ready"))
        hid_proj = s.steps("hid_proj", 1)
        uv_proj = s.steps("uv_proj", 2)
        relu_ready = s.steps("relu_ready", 1)
        hid_hi_ready = s.steps("hid_hi_ready", 1)
        hid_split = s.steps("hid_split", 1)
        gate_proj = s.steps("gate_proj", KC)
        gate_ready = s.steps("gate_ready", KC)
        u_ready = s.steps("u_ready", KC)
        v_ready = s.steps("v_ready", KC)
        summed = s.steps("summed", KC)
        prod_ready = s.steps("prod_ready", KC)
        prod_hi_ready = s.steps("prod_hi_ready", KC)
        prod_split = s.steps("prod_split", KC)
        out_ready = s.steps("out_ready", KC)
        xn_ready = s.steps("xn_ready", KC)
        centre_ready = s.steps("centre_ready", KC)
        conv_ready = s.steps("conv_ready", 2 * KC)
        stored = s.steps("stored", KC)
        block = ctx.enter_context(s.block())

        def walk(engine, unit, end):
            unit(0, 0, None)
            with engine.Fori(0, NB // 2 - 1) as pair:
                for par in (1, 0):
                    i = pair * 2 + (2 - par)
                    unit(i, par, i - 1)
            unit(NB - 1, 1, NB - 2)
            end(NB - 1, 1)

        def w(which, k, chunk):
            return MIX_AT[which] + (k * KC + chunk) * P

        def cc(name, k):
            at = COL_AT[name] + k
            return col[:, at:at + 1]

        @block.sync
        def _(sp):
            sp.dma_start(w_raw[:, :], w_mix).then_inc(w_loaded, 16)
            sp.dma_start(col[:, :], cols).then_inc(col_loaded, 16)

        @block.tensor
        def _(pe):
            for counter in (hid_proj, uv_proj, gate_proj, out_ready):
                counter.prime(pe)
            pe.wait_ge(w_ready, 1)

            def project(out, i, at, step):
                for k in range(KC):
                    mm = product3(pe, out, w_hi[:, at + k * step:at + k * step + P], w_lo[:, at + k * step:at + k * step + P],
                                  c.xn_hi[:, i, k], c.xn_lo[:, i, k], k == 0, k == KC - 1)
                return mm

            def output(i):
                pe.wait_ge(*prod_split(i))
                pe.wait_ge(*stored(i - 1))
                for chunk in range(KC):
                    for k in range(KC):
                        at = w("u", k, chunk)
                        mm = product3(pe, out_ps[:, chunk], w_hi[:, at:at + P], w_lo[:, at:at + P],
                                      prod_hi[:, k], prod_lo[:, k], k == 0, k == KC - 1)
                    mm.then_inc(out_ready.sem, 1)

            def unit(i, par, prev):
                pe.wait_ge(*gate_ready(i - 1))
                project(g_ps[:, 0], i, MIX_AT["g1"], P).then_inc(hid_proj.sem, 1)
                pe.wait_ge(*u_ready(i - 1))
                pe.wait_ge(*v_ready(i - 1))
                for n, (name, out) in enumerate((("u", u_ps), ("v", v_ps))):
                    for chunk in range(KC):
                        mm = project(out[:, chunk], i, w(name, 0, chunk), KC * P)
                    mm.then_inc(uv_proj.sem, 1)
                    if n == 0:
                        pe.wait_ge(*hid_split(i))
                        for chunk in (1, 0):
                            at = MIX_AT["g2"] + chunk * P
                            product3(pe, g_ps[:, chunk], w_hi[:, at:at + P], w_lo[:, at:at + P], hid_hi[:, :], hid_lo[:, :],
                                     True, True).then_inc(gate_proj.sem, 1)
                if prev is not None:
                    output(prev)

            walk(pe, unit, lambda i, par: output(i))

        @block.scalar
        def _(act):
            for counter in (relu_ready, hid_hi_ready, gate_ready, prod_hi_ready, centre_ready):
                counter.prime(act)
            act.preload_act_table_set("sigmoid_and_others")
            act.wait_ge(w_loaded, 16)
            act.activation(w_hi[:, :], w_raw[:, :], ACT.Copy).then_inc(w_hi_ready, 1)
            act.wait_ge(col_loaded, 16)

            def prod_high(i):
                for k in range(KC):
                    act.wait_ge(*prod_ready(i, k + 1))
                    act.wait_ge(*out_ready(i - 1))
                    act.activation(prod_hi[:, k], prod[:, k], ACT.Copy).then_inc(prod_hi_ready.sem, 1)

            def unit(i, par, prev):
                act.wait_ge(*hid_proj(i))
                act.wait_ge(*hid_split(i - 1))
                act.activation(hid[:, :], g_ps[:, 0], ACT.Relu, bias=cc("bg1", 0)).then_inc(relu_ready.sem, 1)
                act.wait_ge(*relu_ready(i))
                act.wait_ge(*gate_proj(i - 1))
                act.activation(hid_hi[:, :], hid[:, :], ACT.Copy).then_inc(hid_hi_ready.sem, 1)
                if prev is not None:
                    prod_high(prev)
                for n, chunk in enumerate((1, 0)):
                    act.wait_ge(*gate_proj(i, n + 1))
                    act.wait_ge(*u_ready(i - 1))
                    act.wait_ge(*v_ready(i - 1))
                    act.activation(gate[:, chunk], g_ps[:, chunk], ACT.Sigmoid, bias=cc("bg2", chunk)).then_inc(gate_ready.sem, 1)
                for k in range(KC):
                    act.wait_ge(*xn_ready(i, k + 1))
                    act.wait_ge(*stored(i - 2))
                    act.activation(conv[:, par, k], xn[:, k], ACT.Identity, bias=cc("conv_b", k), scale=cc("conv1", k))\
                       .then_inc(centre_ready.sem, 1)

            walk(act, unit, lambda i, par: prod_high(i))

        @block.vector
        def _(dve):
            for counter in (hid_split, u_ready, v_ready, summed, conv_ready, stored):
                counter.prime(dve)
            dve.memset(ones[:, :], 1.0).then_inc(ones_ready, 1)
            dve.wait_ge(ones_ready, 1)
            dve.wait_ge(col_loaded, 16)

            def store(i, par):
                for k in range(KC):
                    dve.wait_ge(*conv_ready(i))
                    dve.wait_ge(*out_ready(i, k + 1))
                    dve.tensor_tensor(c.acc[:, i, k], conv[:, par, k], out_ps[:, k], ALU.add).then_inc(stored.sem, 1)

            def unit(i, par, prev):
                dve.wait_ge(*hid_hi_ready(i))
                dve.tensor_tensor(hid_lo[:, :], hid[:, :], hid_hi[:, :].bitcast(F32), ALU.subtract).then_inc(hid_split.sem, 1)
                dve.wait_ge(*gate_ready(i))
                dve.wait_ge(*uv_proj(i, 1))
                for k in range(KC):
                    dve.scalar_tensor_tensor(out=u[:, k], in0=u_ps[:, k], scalar=cc("bu", k), in1=gate[:, k],
                                             op0=ALU.add, op1=ALU.mult).then_inc(u_ready.sem, 1)
                dve.wait_ge(*uv_proj(i))
                dve.wait_ge(*prod_ready(i - 1))
                for k in range(KC):
                    dve.scalar_tensor_tensor(out=v[:, k], in0=v_ps[:, k], scalar=cc("bv", k), in1=gate[:, k],
                                             op0=ALU.add, op1=ALU.mult).then_inc(v_ready.sem, 1)
                for k in range(KC):
                    dve.wait_ge(*u_ready(i, k + 1))
                    dve.tensor_tensor_scan(total[:, k], ones[:, :], u[:, k], 0.0, ALU.mult, ALU.add).then_inc(summed.sem, 1)
                if prev is not None:
                    store(prev, 1 - par)
                for k in range(KC):
                    dve.wait_ge(*centre_ready(i, k + 1))
                    dve.scalar_tensor_tensor(out=conv[:, par, k, 1:T], in0=xn[:, k, 0:T - 1], scalar=cc("conv0", k),
                                             in1=conv[:, par, k, 1:T], op0=ALU.mult, op1=ALU.add).then_inc(conv_ready.sem, 1)
                for k in range(KC):
                    dve.wait_ge(*conv_ready(i, k + 1))
                    dve.scalar_tensor_tensor(out=conv[:, par, k, 0:T - 1], in0=xn[:, k, 1:T], scalar=cc("conv2", k),
                                             in1=conv[:, par, k, 0:T - 1], op0=ALU.mult, op1=ALU.add).then_inc(conv_ready.sem, 1)

            walk(dve, unit, store)

        @block.gpsimd
        def _(pool):
            for counter in (xn_ready, prod_ready, prod_split):
                counter.prime(pool)
            pool.wait_ge(w_hi_ready, 1)
            pool.tensor_tensor(w_lo[:, :], w_raw[:, :], w_hi[:, :].bitcast(F32), ALU.subtract).then_inc(w_ready, 1)

            def prod_low(i):
                for k in range(KC):
                    pool.wait_ge(*prod_hi_ready(i, k + 1))
                    pool.tensor_tensor(prod_lo[:, k], prod[:, k], prod_hi[:, k].bitcast(F32), ALU.subtract)\
                        .then_inc(prod_split.sem, 1)

            def unit(i, par, prev):
                if prev is not None:
                    prod_low(prev)
                for k in range(KC):
                    pool.wait_ge(*conv_ready(i - 1))
                    pool.tensor_tensor(xn[:, k], c.xn_hi[:, i, k].bitcast(F32), c.xn_lo[:, i, k].bitcast(F32), ALU.add)\
                        .then_inc(xn_ready.sem, 1)
                for k in range(KC):
                    pool.wait_ge(*summed(i, k + 1))
                    pool.wait_ge(*v_ready(i, k + 1))
                    pool.wait_ge(*prod_split(i - 1))
                    pool.tensor_tensor(prod[:, k], total[:, k], v[:, k], ALU.mult).then_inc(prod_ready.sem, 1)

            walk(pool, unit, lambda i, par: prod_low(i))


def program(nc, a, out):
    with ExitStack() as ctx:
        s = Space(nc, ctx, "all")

        class c:
            mean = s.sb("mean", [P, P])
            ones = s.sb("ones", [P, P])
            ones_r = s.sb("ones_r", [P, P], F32R)
            ident = s.sb("ident", [P, P])
            upto = s.sb("upto", [P, P])
            eps_ln = s.sb("eps_ln", [P, 1])
            eps_norm = s.sb("eps_norm", [P, 1])
            neg_g = s.sb("neg_g", [P, NB * HKV * TT])
            xn_hi = s.sb("xn_hi", [P, NB, KC, T], F32R)
            xn_lo = s.sb("xn_lo", [P, NB, KC, T], F32R)
            acc = s.sb("acc", [P, NB, KC, T])

        constants(nc, c)
        g_rows = nc.dram_tensor("g_rows", (NB * HKV, T), F32).ap()
        gates0 = nc.dram_tensor("gates0", (E0 + SHARED0, NB * T), F32).ap()
        with ExitStack() as c2:
            logits = Space(nc, c2, "l0").sb("logits", [P, NT, LOG0])
            layernorm(nc, c, "ln0", a["rw0"], LOG0, logits, a["x"])
            decay_logs(nc, c, logits, g_rows)
            route0(nc, c, logits, a["br0"], gates0)
        attention(nc, c, a["w_att"], g_rows)
        mixer0 = nc.dram_tensor("mixer0", (NB, P, KC, T), F32).ap()
        x1 = nc.dram_tensor("x1", (NB, P, KC, T), F32).ap()
        experts(nc, c, "moe0", a["w_e0"], gates0, E0 // GROUP, SHARED0, False, mixer0, a["x"], x1, a["bc0"])
        mixer1 = nc.dram_tensor("mixer1", (NB, P, KC, T), F32).ap()
        gates1 = nc.dram_tensor("gates1", (E1 + SHARED1, NB * T), F32).ap()

        with ExitStack() as c2:
            logits = Space(nc, c2, "l1").sb("logits", [P, NT, E1])
            layernorm(nc, c, "ln1", a["rw1"], E1, logits)
            route1(nc, c, logits, gates1)
        mix(nc, c, a["w_mix"], a["cols"])
        experts(nc, c, "moe1", a["w_e1"], gates1, (E1 + SHARED1 - 1) // GROUP, GROUP, True, mixer1, x1, out)


def by_chunk(w):
    import numpy as np
    return np.ascontiguousarray(w.reshape(KC, P, -1).transpose(1, 0, 2))


def lay_out(v):
    import numpy as np

    f = {n: np.asarray(x) for n, x in v.items()}
    a = {"x": np.ascontiguousarray(f["L0_attn_hidden_states"].reshape(NB, T, KC, P).transpose(0, 3, 2, 1))}
    a["rw0"] = by_chunk(np.concatenate([f["L0_ffn_Wr"].T, f["L0_attn_Wg"]], 1))
    a["br0"] = f["L0_ffn_br"][None]
    heads = [by_chunk(f[n]).reshape(P, KC, HKV, -1) for n in ("L0_attn_Wq", "L0_attn_Wk", "L0_attn_Wv")]
    w = np.zeros((HKV + 1, P, W_ATT), np.float32)
    w[:HKV, :, :KC * QKV] = np.concatenate(heads, 3).transpose(2, 0, 1, 3).reshape(HKV, P, KC * QKV)
    w[:HKV, :, KC * QKV:KC * QKV + REP * D] = f["L0_attn_Wc"].reshape(HKV, REP, DH, D).transpose(0, 2, 1, 3).reshape(HKV, P, REP * D)
    a["w_att"] = w
    a["bc0"] = by_chunk(f["L0_attn_bc"][:, None])[:, :, 0].copy()

    def groups(parts, n):
        e = np.concatenate(parts, 2)
        g = np.zeros((n * GROUP, P, e.shape[2]), np.float32)
        g[:len(e)] = e
        out = np.zeros((n, P, (NB - 2) * w_slice(e.shape[2])), np.float32)
        out[:, :, :GROUP * e.shape[2]] = g.reshape(n, GROUP, P, -1).transpose(0, 2, 1, 3).reshape(n, P, -1)
        return out

    def inward(w):
        return w.reshape(-1, P, KC, P).transpose(0, 3, 2, 1).reshape(-1, P, D)

    w1 = np.concatenate([f["L0_ffn_W1"], f["L0_ffn_Ws1"].reshape(SHARED0, P, D)])
    w2 = np.concatenate([f["L0_ffn_W2"].transpose(0, 2, 1), f["L0_ffn_Ws2"].T.reshape(SHARED0, P, D)])
    a["w_e0"] = groups([inward(w1), w2], (E0 + SHARED0 + GROUP - 1) // GROUP)
    a["rw1"] = by_chunk(f["L1_ffn_w_router"])
    ins = [np.concatenate([f[e].transpose(0, 2, 1), f[sh].T.reshape(SHARED1, P, D)])
           for e, sh in (("L1_ffn_we1", "L1_ffn_ws1"), ("L1_ffn_we3", "L1_ffn_ws3"))]
    w2 = np.concatenate([f["L1_ffn_we2"], f["L1_ffn_ws2"].reshape(SHARED1, P, D)])
    a["w_e1"] = groups([inward(ins[0]), inward(ins[1]), w2], (E1 + SHARED1) // GROUP)
    m = np.zeros((P, W_MIX), np.float32)
    m[:, MIX_AT["u"]:MIX_AT["v"]] = by_chunk(f["L1_attn_Wu"].T).reshape(P, -1)
    m[:, MIX_AT["v"]:MIX_AT["g1"]] = by_chunk(f["L1_attn_Wv"].T).reshape(P, -1)
    for k in range(KC):
        at = MIX_AT["g1"] + k * P
        m[:, at:at + DG] = f["L1_attn_Wg1"].T[k * P:(k + 1) * P]
    m[:DG, MIX_AT["g2"]:] = f["L1_attn_Wg2"].T
    a["w_mix"] = m
    cols = np.zeros((P, COLS), np.float32)
    for name, x in (("bu", "L1_attn_bu"), ("bv", "L1_attn_bv"), ("bg2", "L1_attn_bg2"), ("conv_b", "L1_attn_conv_b")):
        cols[:, COL_AT[name]:COL_AT[name] + KC] = f[x].reshape(KC, P).T
    cols[:DG, COL_AT["bg1"]] = f["L1_attn_bg1"]
    for tap in range(3):
        cols[:, COL_AT[f"conv{tap}"]:COL_AT[f"conv{tap}"] + KC] = f["L1_attn_conv_w"][:, 0, tap].reshape(KC, P).T
    a["cols"] = cols
    return a


def kernel(**inputs):
    import numpy as np
    from concourse import bacc
    from concourse.bass_utils import run_bass_kernel_spmd as run

    arrays = lay_out(inputs)
    nc = bacc.Bacc("TRN2", target_bir_lowering=False, num_devices=1)
    a = {n: nc.dram_tensor(f"in_{n}", x.shape, mybir.dt.from_np(x.dtype), kind="ExternalInput").ap() for n, x in arrays.items()}
    out = nc.dram_tensor("out", (NB, P, KC, T), F32, kind="ExternalOutput").ap()
    program(nc, a, out)
    r = run(nc, [{f"in_{n}": x for n, x in arrays.items()}], core_ids=[0])
    return np.ascontiguousarray(r.results[0]["out"].transpose(0, 3, 2, 1)).reshape(NB, T, D)
```
